# Optimizing a Trainium2 kernel written in Bass

```python
import numpy as np
import jax
import jax.numpy as jnp

def _softmax(x, axis=-1):
    return jax.nn.softmax(x, axis=axis)

def _gelu(x):
    return jax.nn.gelu(x, approximate=True)

def _silu(x):
    return jax.nn.silu(x)

def _sigmoid(x):
    return jax.nn.sigmoid(x)

def _layernorm(x, axis=-1, eps=1e-05):
    m = jnp.mean(x, axis=axis, keepdims=True)
    v = jnp.var(x, axis=axis, keepdims=True)
    return (x - m) / jnp.sqrt(v + eps)

def _scatter_add(tgt, idx, src, axis=0):
    return tgt.at[idx].add(src)

def _segment_sum(src, seg, n):
    return jax.ops.segment_sum(src, seg, n)
kernel_name = 'mk_gnn_preln_d4_gnn_r8_eb8410'

def setup_inputs(seed: int=0):
    np.random.seed(seed)
    _w = jnp.asarray

    def _rec_inputs():
        import jax
        import jax.numpy as jnp
        _gk = jax.random.key(seed)
        x = -0.0003713 + 1 * jax.random.normal(jax.random.fold_in(_gk, 1), (6250, 256), jnp.float32)
        src = jax.random.randint(jax.random.fold_in(_gk, 2), (100000,), 0, 6250, jnp.int32)
        dst = jax.random.randint(jax.random.fold_in(_gk, 3), (100000,), 0, 6250, jnp.int32)
        _o = jnp.argsort(dst, stable=True)
        src = src[_o]
        dst = dst[_o]
        edge_attr_64 = 1.36993e-05 + 0.999972 * jax.random.normal(jax.random.fold_in(_gk, 11), (100000, 64), jnp.float32)
        edge_weight = jax.random.uniform(jax.random.fold_in(_gk, 13), (100000,), jnp.float32, 0.0, 0.999998)
        return (x, src, dst, edge_attr_64, edge_weight)
    x, src, dst, edge_attr_64, edge_weight = _rec_inputs()

    def _L0_gnn_setup():
        import jax, jax.numpy as jnp
        import numpy as np
        N, IN_CH, HEADS, OUT_CH, E = (6250, 256, 4, 64, 100000)
        key = jax.random.key(seed)
        k1, k2, k3, k4, k5 = jax.random.split(key, 5)
        x = jax.random.normal(k1, (N, IN_CH), dtype=jnp.float32)
        edge_index = jax.random.randint(k2, (2, E), 0, N, dtype=jnp.int64)
        bw = float(np.sqrt(6.0 / (IN_CH + HEADS * OUT_CH)))
        ba = float(np.sqrt(6.0 / (HEADS + OUT_CH)))
        weight = jax.random.uniform(k3, (IN_CH, HEADS * OUT_CH), jnp.float32, -bw, bw)
        attn_l = jax.random.uniform(k4, (HEADS, OUT_CH), jnp.float32, -ba, ba)
        attn_r = jax.random.uniform(k5, (HEADS, OUT_CH), jnp.float32, -ba, ba)
        return {'x': x, 'edge_index': edge_index, 'weight': weight, 'attn_l': attn_l, 'attn_r': attn_r}
    _L0_gnn_all = _L0_gnn_setup()
    _L0_gnn_in = {k: v for k, v in _L0_gnn_all.items() if k in ('weight', 'attn_l', 'attn_r')}
    del _L0_gnn_all

    def _L1_gnn_setup():
        import jax, jax.numpy as jnp
        import numpy as np
        N_NODES = 6250
        key = jax.random.key(seed)
        k1, k2, k3 = jax.random.split(key, 3)
        x = jax.random.normal(k1, (N_NODES, 256), dtype=jnp.float32)
        W = jax.random.normal(k2, (256, 256), dtype=jnp.float32) * (1.0 / np.sqrt(256))
        edge_index = jax.random.randint(k3, (2, 200000), 0, N_NODES, dtype=jnp.int64)
        return {'x': x, 'W': W, 'edge_index': edge_index}
    _L1_gnn_all = _L1_gnn_setup()
    _L1_gnn_in = {k: v for k, v in _L1_gnn_all.items() if k in ('W',)}
    del _L1_gnn_all

    def _L2_gnn_setup():
        import jax, jax.numpy as jnp
        import numpy as np
        N = 2500
        E = 40000
        D = 256
        H = 8
        DH = D // H
        ED = 64
        FF = 4 * D
        EPS = 1e-05

        def _layernorm(x, g, b):
            m = jnp.mean(x, axis=-1, keepdims=True)
            v = jnp.var(x, axis=-1, keepdims=True)
            return (x - m) * jax.lax.rsqrt(v + EPS) * g + b

        def _edge_attention(xn, edge_index, ef, ew, Wq, bq, Wk, bk, Wv, bv, We, be, Wo, bo):
            n = xn.shape[0]
            scale = DH ** (-0.5)
            q = (xn @ Wq + bq).reshape(n, H, DH)
            k = (xn @ Wk + bk).reshape(n, H, DH)
            v = (xn @ Wv + bv).reshape(n, H, DH)
            src, dst = (edge_index[0], edge_index[1])
            ep = ef @ We + be
            scores = jnp.einsum('ehd,ehd->eh', q[dst], k[src] + ep[:, None, :]) * scale
            scores = scores * ew[:, None]
            m = jax.ops.segment_max(scores, dst, num_segments=n)
            m = jnp.where(jnp.isfinite(m), m, 0.0)
            ex = jnp.exp(scores - m[dst])
            s = jax.ops.segment_sum(ex, dst, num_segments=n)
            attn = ex / s[dst]
            out = jax.ops.segment_sum(attn[:, :, None] * v[src], dst, num_segments=n)
            out = out.reshape(n, D) @ Wo + bo
            return out
        key = jax.random.key(seed)
        ks = jax.random.split(key, 32)

        def lin_w(k, i, o):
            return (jax.random.normal(k, (i, o), jnp.float32) / np.sqrt(i)).astype(jnp.float32)
        return {'x': jax.random.normal(ks[0], (N, D), jnp.float32), 'edge_features': jax.random.normal(ks[1], (E, ED), jnp.float32), 'edge_weights': jax.random.uniform(ks[2], (E,), jnp.float32), 'edge_index': jax.random.randint(ks[3], (2, E), 0, N, dtype=jnp.int32), 'Wq': lin_w(ks[4], D, D), 'bq': jnp.zeros((D,), jnp.float32), 'Wk': lin_w(ks[5], D, D), 'bk': jnp.zeros((D,), jnp.float32), 'Wv': lin_w(ks[6], D, D), 'bv': jnp.zeros((D,), jnp.float32), 'We': lin_w(ks[7], ED, DH), 'be': jnp.zeros((DH,), jnp.float32), 'Wo': lin_w(ks[8], D, D), 'bo': jnp.zeros((D,), jnp.float32), 'ln1_g': jnp.ones((D,), jnp.float32), 'ln1_b': jnp.zeros((D,), jnp.float32), 'ln2_g': jnp.ones((D,), jnp.float32), 'ln2_b': jnp.zeros((D,), jnp.float32), 'W1': lin_w(ks[9], D, FF), 'b1': jnp.zeros((FF,), jnp.float32), 'W2': lin_w(ks[10], FF, D), 'b2': jnp.zeros((D,), jnp.float32), 'alpha': jnp.ones((1,), jnp.float32), 'beta': jnp.ones((1,), jnp.float32)}
    _L2_gnn_all = _L2_gnn_setup()
    _L2_gnn_in = {k: v for k, v in _L2_gnn_all.items() if k in ('Wq', 'bq', 'Wk', 'bk', 'Wv', 'bv', 'We', 'be', 'Wo', 'bo', 'ln1_g', 'ln1_b', 'ln2_g', 'ln2_b', 'W1', 'b1', 'W2', 'b2', 'alpha', 'beta')}
    del _L2_gnn_all

    def _L3_gnn_setup():
        import jax, jax.numpy as jnp
        import numpy as np
        N, E = (6250, 100000)
        HID, EDIM, HEADS = (256, 64, 8)
        C = HID // HEADS
        NEG_SLOPE = 0.2
        LN_EPS = 1e-05

        def _gat_block(x, edge_index, edge_attr, W, W_e, att_src, att_dst, att_edge, bias, gamma, beta):
            n = x.shape[0]
            src, dst = (edge_index[0], edge_index[1])
            xp = (x @ W).reshape(n, HEADS, C)
            a_src = jnp.einsum('nhc,hc->nh', xp, att_src)
            a_dst = jnp.einsum('nhc,hc->nh', xp, att_dst)
            ep = (edge_attr @ W_e).reshape(-1, HEADS, C)
            a_edge = jnp.einsum('ehc,hc->eh', ep, att_edge)
            alpha = a_src[src] + a_dst[dst] + a_edge
            alpha = jax.nn.leaky_relu(alpha, NEG_SLOPE)
            m = jax.ops.segment_max(alpha, dst, num_segments=n)
            m = jnp.where(jnp.isfinite(m), m, 0.0)
            ea = jnp.exp(alpha - m[dst])
            den = jax.ops.segment_sum(ea, dst, num_segments=n)
            attn = ea / (den[dst] + 1e-16)
            msg = xp[src] * attn[:, :, None]
            out = jax.ops.segment_sum(msg, dst, num_segments=n)
            h = out.reshape(n, HEADS * C) + bias
            y = x + h
            mu = jnp.mean(y, axis=-1, keepdims=True)
            var = jnp.var(y, axis=-1, keepdims=True)
            return (y - mu) * jax.lax.rsqrt(var + LN_EPS) * gamma + beta
        key = jax.random.key(seed)
        ks = jax.random.split(key, 12)
        s = 1.0 / np.sqrt(HID)
        se = 1.0 / np.sqrt(EDIM)
        return {'x': jax.random.normal(ks[0], (N, HID), jnp.float32), 'edge_index': jax.random.randint(ks[1], (2, E), 0, N, jnp.int32), 'edge_attr': jax.random.normal(ks[2], (E, EDIM), jnp.float32), 'W': jax.random.uniform(ks[3], (HID, HEADS * C), jnp.float32, -s, s), 'W_e': jax.random.uniform(ks[4], (EDIM, HEADS * C), jnp.float32, -se, se), 'att_src': jax.random.normal(ks[5], (HEADS, C), jnp.float32) * 0.1, 'att_dst': jax.random.normal(ks[6], (HEADS, C), jnp.float32) * 0.1, 'att_edge': jax.random.normal(ks[7], (HEADS, C), jnp.float32) * 0.1, 'bias': jnp.zeros((HEADS * C,), jnp.float32), 'gamma': jnp.ones((HID,), jnp.float32), 'beta': jnp.zeros((HID,), jnp.float32)}
    _L3_gnn_all = _L3_gnn_setup()
    _L3_gnn_in = {k: v for k, v in _L3_gnn_all.items() if k in ('W', 'W_e', 'att_src', 'att_dst', 'att_edge', 'bias', 'gamma', 'beta')}
    del _L3_gnn_all
    return {'x': x, 'src': src, 'dst': dst, 'edge_attr_64': edge_attr_64, 'edge_weight': edge_weight, 'L0_gnn_weight': _L0_gnn_in['weight'], 'L0_gnn_attn_l': _L0_gnn_in['attn_l'], 'L0_gnn_attn_r': _L0_gnn_in['attn_r'], 'L1_gnn_W': _L1_gnn_in['W'], 'L2_gnn_Wq': _L2_gnn_in['Wq'], 'L2_gnn_bq': _L2_gnn_in['bq'], 'L2_gnn_Wk': _L2_gnn_in['Wk'], 'L2_gnn_bk': _L2_gnn_in['bk'], 'L2_gnn_Wv': _L2_gnn_in['Wv'], 'L2_gnn_bv': _L2_gnn_in['bv'], 'L2_gnn_We': _L2_gnn_in['We'], 'L2_gnn_be': _L2_gnn_in['be'], 'L2_gnn_Wo': _L2_gnn_in['Wo'], 'L2_gnn_bo': _L2_gnn_in['bo'], 'L2_gnn_ln1_g': _L2_gnn_in['ln1_g'], 'L2_gnn_ln1_b': _L2_gnn_in['ln1_b'], 'L2_gnn_ln2_g': _L2_gnn_in['ln2_g'], 'L2_gnn_ln2_b': _L2_gnn_in['ln2_b'], 'L2_gnn_W1': _L2_gnn_in['W1'], 'L2_gnn_b1': _L2_gnn_in['b1'], 'L2_gnn_W2': _L2_gnn_in['W2'], 'L2_gnn_b2': _L2_gnn_in['b2'], 'L2_gnn_alpha': _L2_gnn_in['alpha'], 'L2_gnn_beta': _L2_gnn_in['beta'], 'L3_gnn_W': _L3_gnn_in['W'], 'L3_gnn_W_e': _L3_gnn_in['W_e'], 'L3_gnn_att_src': _L3_gnn_in['att_src'], 'L3_gnn_att_dst': _L3_gnn_in['att_dst'], 'L3_gnn_att_edge': _L3_gnn_in['att_edge'], 'L3_gnn_bias': _L3_gnn_in['bias'], 'L3_gnn_gamma': _L3_gnn_in['gamma'], 'L3_gnn_beta': _L3_gnn_in['beta']}

def reference(x, src, dst, edge_attr_64, edge_weight, L0_gnn_weight, L0_gnn_attn_l, L0_gnn_attn_r, L1_gnn_W, L2_gnn_Wq, L2_gnn_bq, L2_gnn_Wk, L2_gnn_bk, L2_gnn_Wv, L2_gnn_bv, L2_gnn_We, L2_gnn_be, L2_gnn_Wo, L2_gnn_bo, L2_gnn_ln1_g, L2_gnn_ln1_b, L2_gnn_ln2_g, L2_gnn_ln2_b, L2_gnn_W1, L2_gnn_b1, L2_gnn_W2, L2_gnn_b2, L2_gnn_alpha, L2_gnn_beta, L3_gnn_W, L3_gnn_W_e, L3_gnn_att_src, L3_gnn_att_dst, L3_gnn_att_edge, L3_gnn_bias, L3_gnn_gamma, L3_gnn_beta):
    import jax
    import jax.numpy as jnp

    def _L0_gnn_ref(x, edge_index, weight, attn_l, attn_r):
        import jax, jax.numpy as jnp
        import numpy as np
        N, IN_CH, HEADS, OUT_CH, E = (6250, 256, 4, 64, 100000)
        heads, out_ch = attn_l.shape
        n = x.shape[0]
        xt = jnp.matmul(x, weight).reshape(-1, heads, out_ch)
        row, col = (edge_index[0], edge_index[1])
        alpha_l = jnp.einsum('ehd,hd->eh', xt[row], attn_l)
        alpha_r = jnp.einsum('ehd,hd->eh', xt[col], attn_r)
        alpha = jax.nn.softmax(jax.nn.leaky_relu(alpha_l + alpha_r, 0.01), axis=1)
        tmp = jnp.einsum('nh,nhd->nd', alpha[:n], xt[col[:n]])
        out = jnp.broadcast_to(tmp[:, None, :], (n, heads, out_ch))
        return out.reshape(n, heads * out_ch)

    def _L1_gnn_ref(x, W, edge_index):
        import jax, jax.numpy as jnp
        import numpy as np
        N_NODES = 6250
        N = x.shape[0]
        src, dst = (edge_index[0], edge_index[1])
        h = x @ W
        deg = jax.ops.segment_sum(jnp.ones_like(dst, dtype=h.dtype), dst, num_segments=N)
        deg_inv_sqrt = jnp.where(deg > 0, jax.lax.rsqrt(jnp.maximum(deg, 1)), 0.0)
        norm = deg_inv_sqrt[src] * deg_inv_sqrt[dst]
        msgs = h[src] * norm[:, None]
        out = jax.ops.segment_sum(msgs, dst, num_segments=N)
        return out

    def _L2_gnn_ref(x, edge_features, edge_weights, edge_index, Wq, bq, Wk, bk, Wv, bv, We, be, Wo, bo, ln1_g, ln1_b, ln2_g, ln2_b, W1, b1, W2, b2, alpha, beta):
        import jax, jax.numpy as jnp
        import numpy as np
        N = 2500
        E = 40000
        D = 256
        H = 8
        DH = D // H
        ED = 64
        FF = 4 * D
        EPS = 1e-05

        def _layernorm(x, g, b):
            m = jnp.mean(x, axis=-1, keepdims=True)
            v = jnp.var(x, axis=-1, keepdims=True)
            return (x - m) * jax.lax.rsqrt(v + EPS) * g + b

        def _edge_attention(xn, edge_index, ef, ew, Wq, bq, Wk, bk, Wv, bv, We, be, Wo, bo):
            n = xn.shape[0]
            scale = DH ** (-0.5)
            q = (xn @ Wq + bq).reshape(n, H, DH)
            k = (xn @ Wk + bk).reshape(n, H, DH)
            v = (xn @ Wv + bv).reshape(n, H, DH)
            src, dst = (edge_index[0], edge_index[1])
            ep = ef @ We + be
            scores = jnp.einsum('ehd,ehd->eh', q[dst], k[src] + ep[:, None, :]) * scale
            scores = scores * ew[:, None]
            m = jax.ops.segment_max(scores, dst, num_segments=n)
            m = jnp.where(jnp.isfinite(m), m, 0.0)
            ex = jnp.exp(scores - m[dst])
            s = jax.ops.segment_sum(ex, dst, num_segments=n)
            attn = ex / s[dst]
            out = jax.ops.segment_sum(attn[:, :, None] * v[src], dst, num_segments=n)
            out = out.reshape(n, D) @ Wo + bo
            return out
        xn = _layernorm(x, ln1_g, ln1_b)
        attn_out = _edge_attention(xn, edge_index, edge_features, edge_weights, Wq, bq, Wk, bk, Wv, bv, We, be, Wo, bo)
        x = x + alpha * attn_out
        xn = _layernorm(x, ln2_g, ln2_b)
        ff = jax.nn.gelu(xn @ W1 + b1, approximate=False) @ W2 + b2
        x = x + beta * ff
        return x

    def _L3_gnn_ref(x, edge_index, edge_attr, W, W_e, att_src, att_dst, att_edge, bias, gamma, beta):
        import jax, jax.numpy as jnp
        import numpy as np
        N, E = (6250, 100000)
        HID, EDIM, HEADS = (256, 64, 8)
        C = HID // HEADS
        NEG_SLOPE = 0.2
        LN_EPS = 1e-05

        def _gat_block(x, edge_index, edge_attr, W, W_e, att_src, att_dst, att_edge, bias, gamma, beta):
            n = x.shape[0]
            src, dst = (edge_index[0], edge_index[1])
            xp = (x @ W).reshape(n, HEADS, C)
            a_src = jnp.einsum('nhc,hc->nh', xp, att_src)
            a_dst = jnp.einsum('nhc,hc->nh', xp, att_dst)
            ep = (edge_attr @ W_e).reshape(-1, HEADS, C)
            a_edge = jnp.einsum('ehc,hc->eh', ep, att_edge)
            alpha = a_src[src] + a_dst[dst] + a_edge
            alpha = jax.nn.leaky_relu(alpha, NEG_SLOPE)
            m = jax.ops.segment_max(alpha, dst, num_segments=n)
            m = jnp.where(jnp.isfinite(m), m, 0.0)
            ea = jnp.exp(alpha - m[dst])
            den = jax.ops.segment_sum(ea, dst, num_segments=n)
            attn = ea / (den[dst] + 1e-16)
            msg = xp[src] * attn[:, :, None]
            out = jax.ops.segment_sum(msg, dst, num_segments=n)
            h = out.reshape(n, HEADS * C) + bias
            y = x + h
            mu = jnp.mean(y, axis=-1, keepdims=True)
            var = jnp.var(y, axis=-1, keepdims=True)
            return (y - mu) * jax.lax.rsqrt(var + LN_EPS) * gamma + beta
        return _gat_block(x, edge_index, edge_attr, W, W_e, att_src, att_dst, att_edge, bias, gamma, beta)
    edge_index = jnp.stack([src, dst])
    h = jnp.maximum(_layernorm(x, axis=-1), 0.0)
    x = x + _L0_gnn_ref(h, edge_index, L0_gnn_weight, L0_gnn_attn_l, L0_gnn_attn_r)
    h = jnp.maximum(_layernorm(x, axis=-1), 0.0)
    x = x + _L1_gnn_ref(h, L1_gnn_W, edge_index)
    h = jnp.maximum(_layernorm(x, axis=-1), 0.0)
    x = x + _L2_gnn_ref(h, edge_attr_64, edge_weight, edge_index, L2_gnn_Wq, L2_gnn_bq, L2_gnn_Wk, L2_gnn_bk, L2_gnn_Wv, L2_gnn_bv, L2_gnn_We, L2_gnn_be, L2_gnn_Wo, L2_gnn_bo, L2_gnn_ln1_g, L2_gnn_ln1_b, L2_gnn_ln2_g, L2_gnn_ln2_b, L2_gnn_W1, L2_gnn_b1, L2_gnn_W2, L2_gnn_b2, L2_gnn_alpha, L2_gnn_beta)
    h = jnp.maximum(_layernorm(x, axis=-1), 0.0)
    x = x + _L3_gnn_ref(h, edge_index, edge_attr_64, L3_gnn_W, L3_gnn_W_e, L3_gnn_att_src, L3_gnn_att_dst, L3_gnn_att_edge, L3_gnn_bias, L3_gnn_gamma, L3_gnn_beta)
    return x

_drawn_inputs = setup_inputs


def setup_inputs(seed=0):
    import zlib

    import numpy as np

    out = dict(_drawn_inputs(seed))
    spreads = {'L2_gnn_bq': (0.0, 0.391),
     'L2_gnn_bk': (0.0, 0.8),
     'L2_gnn_bv': (0.0, 0.1),
     'L2_gnn_be': (0.0, 0.8),
     'L2_gnn_bo': (0.0, 0.1),
     'L2_gnn_ln1_g': (1.0, 0.2),
     'L2_gnn_ln1_b': (0.0, 0.1),
     'L2_gnn_ln2_g': (1.0, 0.2),
     'L2_gnn_ln2_b': (0.0, 0.1),
     'L2_gnn_b1': (0.0, 0.1),
     'L2_gnn_b2': (0.0, 0.1),
     'L3_gnn_bias': (0.0, 0.1),
     'L3_gnn_gamma': (1.0, 0.2),
     'L3_gnn_beta': (0.0, 0.1)}
    factors = {'L3_gnn_W_e': 4.998,
     'L3_gnn_att_src': 6.183,
     'L3_gnn_att_dst': 64.0,
     'L3_gnn_att_edge': 4.794}
    for name, (base, spread) in spreads.items():
        noise = np.random.default_rng([zlib.crc32(name.encode()), seed]).standard_normal(out[name].shape)
        drawn = base * np.exp(spread * noise) if base else spread * noise
        out[name] = jnp.asarray(drawn.astype(out[name].dtype))
    for name, factor in factors.items():
        out[name] = (out[name] * factor).astype(out[name].dtype)
    return out
```

```python
from contextlib import ExitStack

import numpy as np

import concourse.bass as bass
from concourse import mybir

P = 128
N, E, D, ED = 6250, 100000, 256, 64
NT = -(-N // P)
NPAD = NT * P
LAST_ROWS = N - (NT - 1) * P
ET = -(-E // P)
TAIL = E - (ET - 1) * P
UNROLL = 16
NS = -(-(ET + NT - 1) // UNROLL) * UNROLL
SB = -(-NS // P)
H, C = 8, D // 8
H0, C0 = 4, D // 4
AW = D + H
CH = P // H
CB = NS // CH
SEQ = CB * P
KT = D // P
FF = 4 * D
FT = FF // P
EW = 32 + H
EPS = 1e-5
BIG = 1e30
NOWHERE = 1 << 20

F32 = mybir.dt.float32
I32 = mybir.dt.int32
ALU = mybir.AluOpType
ACT = mybir.ActivationFunctionType
AX = mybir.AxisListType
ds = bass.ds


class Kept:
    pass


def wait(eng, sem, value):
    if not isinstance(value, int) or value > 0:
        eng.wait_ge(sem, value)


def ticks(eng, total, unroll, lag, body):
    groups = total // unroll
    for u in range(unroll):
        body(0, u)
    with eng.Fori(1, groups) as it:
        for u in range(unroll):
            body(it, u)
    for u in range(total - groups * unroll + lag):
        body(groups, u)


def live(it, c, unroll, total):
    return not isinstance(it, int) or 0 <= it * unroll + c < total


def fills(it, c, unroll, ring):
    return it * (unroll // ring) + c // ring + 1


class Chain:

    def __init__(self, eng, sem):
        self.eng, self.sem, self.n = eng, sem, 0

    def __call__(self, ins):
        self.n += 1
        ins.then_inc(self.sem, 1)
        self.eng.wait_ge(self.sem, self.n)


def walk_tables(nc, k, src, dst, ew):
    with ExitStack() as c:
        sb = lambda name, shape, dt=F32: c.enter_context(nc.sbuf_tensor(name, shape, dt))
        sem = lambda name: c.enter_context(nc.semaphore(name))
        pad_row = sb("pad_row", [2, 3 * P], I32)
        same_i = sb("same_i", [P, NS], I32)
        pad_key = sb("pad_key", [1, P])
        last_dst = sb("last_dst", [1, ET], I32)
        last_shr = sb("last_shr", [1, ET], I32)
        last_f = sb("last_f", [1, 2, ET])
        tile_i = sb("tile_i", [1, ET], I32)
        step_i = sb("step_i", [P, SB], I32)
        step_col = sb("step_col", [P, SB])
        node_i = sb("node_i", [P, NT], I32)
        node_col = sb("node_col", [P, NT])
        less = sb("less", [P, ET])
        i_col = sb("i_col", [P, SB])
        j_col = sb("j_col", [P, SB])
        base_col = sb("base_col", [P, SB])
        jbase = sb("jbase", [P, SB])
        i_idx = sb("i_idx", [P, SB], I32)
        ij_row = sb("ij_row", [SB, 2, P], I32)
        before = sb("before", [P, NT])
        before_idx = sb("before_idx", [P, NT], I32)
        lo = sb("lo", [P, NT])
        lo_row = sb("lo_row", [NT, P])
        lo_next = sb("lo_next", [NT, P])
        deg_row = sb("deg_row", [NT, P])
        end_row = sb("end_row", [1, P])
        rows = sb("rows", [P, 2, 3 * P], I32)
        nrows = sb("nrows", [P, 4, 3 * P], I32)
        ncmp = sb("ncmp", [P, P])
        rowf = sb("rowf", [P, 2, 5, P])
        d1 = sb("d1", [P, P])
        ge0 = sb("ge0", [P, P])
        valid = sb("valid", [P, P])
        pv = c.enter_context(nc.psum_tensor("pv", [P, 2, 2, 512], F32))
        pt = [c.enter_context(nc.psum_tensor(f"ptab{n}", [P, 4, P], F32)) for n in range(2)]

        s_pad, s_tail, s_last, s_tab, s_io = sem("pad"), sem("tail"), sem("last"), sem("tab"), sem("io")
        s_key0 = sem("padkey")
        s_ij, s_ijrow, s_ijback = sem("ij"), sem("ijrow"), sem("ijback")
        s_v, s_bcast, s_vec = sem("v"), sem("bcast"), sem("vec")
        s_idx = sem("idx")
        s_rowf, s_rowt, s_rowc, s_key = sem("rowf"), sem("rowt"), sem("rowc"), [sem(f"key{n}") for n in range(2)]
        s_bidx, s_ncnt = sem("bidx"), sem("ncnt")
        s_lo, s_lot, s_lor, s_lod, s_lon, s_degr, s_degt, s_deg = (
            sem("lo_"), sem("lot"), sem("lor"), sem("lod"), sem("lon"), sem("degr"), sem("degt"), sem("deg"))
        s_act = sem("actc")
        full = (ET - 1) * P
        HALF = ET // 2

        with nc.Block() as block:
            @block.sync
            def _(sp):
                tab = k.tab.ap()
                parts = [dst, src, ew.bitcast(I32)]
                for n, a in enumerate(parts):
                    sp.dma_start(tab[0:ET - 1, n * P:(n + 1) * P],
                                 a[0:full].rearrange("(i p) -> i p", p=P)).then_inc(s_tab, 16)
                    sp.dma_start(tab[ET - 1:ET, (n + 1) * P - TAIL:(n + 1) * P],
                                 a[full:E].rearrange("(i p) -> i p", i=1)).then_inc(s_tab, 16)
                sp.dma_start(last_dst[0:1, 0:ET - 1],
                             dst[0:full].rearrange("(i p) -> p i", p=P)[P - 1:P, :]).then_inc(s_last, 16)
                sp.dma_start(last_dst[0:1, ET - 1:ET],
                             dst[E - 1:E].rearrange("(a b) -> a b", a=1)).then_inc(s_last, 16)
                sp.wait_ge(s_pad, 4)
                for n in range(3):
                    sp.dma_start(tab[ET - 1:ET, n * P:(n + 1) * P - TAIL],
                                 pad_row[0:1, n * P:(n + 1) * P - TAIL]).then_inc(s_tab, 16)
                sp.dma_start(tab[ET:ET + 1, :], pad_row[0:1, :]).then_inc(s_tab, 16)
                sp.dma_start(k.keys.ap()[0:P].rearrange("(a b) -> a b", a=1),
                             pad_key[:, :]).then_inc(s_key0, 16)
                sp.wait_ge(s_ijrow, 1)
                sp.dma_start(k.ij.ap().rearrange("a (b p) -> b a p", p=P), ij_row[:, :, :]).then_inc(s_ij, 16)
                sp.wait_ge(s_ij, 16)
                sp.dma_start(k.step_base[0:1, :], k.ij.ap()[0:1, 0:NS]).then_inc(s_ijback, 16)
                sp.dma_start(k.step_j[0:1, :], k.ij.ap()[1:2, 0:NS]).then_inc(s_ijback, 16)
                sp.dma_start(same_i[:, :], k.ij.ap()[1:2, 0:NS].to_broadcast([P, NS])).then_inc(s_ijback, 16)
                for b in range(SB):
                    sp.wait_ge(s_rowf, b + 1)
                    sp.dma_start(k.keys.ap()[P + b * P * P:P + (b + 1) * P * P].rearrange("(s e) -> s e", e=P),
                                 rowf[:, b % 2, 4, :]).then_inc(s_key[b % 2], 16)
                sp.wait_ge(s_lor, 2)
                sp.dma_start(k.lod.ap()[0:NPAD].rearrange("(t p) -> t p", p=P), lo_row[:, :]).then_inc(s_lod, 16)
                sp.dma_start(k.lod.ap()[NPAD:NPAD + P].rearrange("(t p) -> t p", p=P),
                             end_row[:, :]).then_inc(s_lod, 16)
                sp.wait_ge(s_lod, 32)
                sp.dma_start(lo_next[:, :], k.lod.ap()[1:NPAD + 1].rearrange("(t p) -> t p", p=P)).then_inc(s_lon, 16)
                sp.wait_ge(s_key0, 16)
                sp.wait_ge(s_ijback, 48)
                sp.wait_ge(s_key[0], 16 * ((SB + 1) // 2))
                sp.wait_ge(s_key[1], 16 * (SB // 2))

            @block.gpsimd
            def _(pool):
                nc.gpsimd.memset(pad_row[:, :], 0).then_inc(s_pad, 1)
                pool.wait_ge(s_pad, 1)
                nc.gpsimd.memset(pad_row[:, 0:P], NOWHERE).then_inc(s_pad, 1)
                nc.gpsimd.memset(pad_key[:, :], -5.0).then_inc(s_pad, 1)
                nc.gpsimd.memset(end_row[:, :], float(E)).then_inc(s_pad, 1)
                nc.gpsimd.iota(tile_i[:, :], [[1, ET]], base=0, channel_multiplier=0).then_inc(s_io, 1)
                nc.gpsimd.iota(step_i[:, :], [[P, SB]], base=0, channel_multiplier=1).then_inc(s_io, 1)
                nc.gpsimd.iota(node_i[:, :], [[P, NT]], base=0, channel_multiplier=1).then_inc(s_io, 1)
                nc.gpsimd.iota(k.iota_i[:, :], [[1, P]], base=0, channel_multiplier=0).then_inc(s_io, 1)
                nc.gpsimd.memset(k.ident[:, :], 0.0).then_inc(s_io, 1)
                nc.gpsimd.memset(k.ones[:, :], 1.0).then_inc(s_io, 1)
                pool.wait_ge(s_io, 6)
                nc.gpsimd.affine_select(out=k.ident[:, :], in_=k.ident[:, :], compare_op=ALU.not_equal, fill=1.0,
                                        base=0, pattern=[[-1, P]], channel_multiplier=1).then_inc(s_io, 1)
                pool.wait_ge(s_tab, 160)
                pool.wait_ge(s_idx, 1)
                for b in range(SB):
                    if b >= 2:
                        pool.wait_ge(s_rowf, b - 1)
                    pool.indirect_dma_start(rows[:, b % 2, :], None, k.tab.ap(),
                                            bass.IndirectOffsetOnAxis(i_idx[:, b:b + 1], 0)).then_inc(k.got[b % 2], 16)
                pool.wait_ge(s_bidx, 1)
                for t in range(NT):
                    if t >= 4:
                        pool.wait_ge(s_ncnt, t - 3)
                    pool.indirect_dma_start(nrows[:, t % 4, :], None, k.tab.ap(),
                                            bass.IndirectOffsetOnAxis(before_idx[:, t:t + 1], 0)).then_inc(k.got[4 + t % 4], 16)

            @block.tensor
            def _(pe):
                pe.wait_ge(s_io, 7)
                pe.wait_ge(s_v, 1)
                for n in range(2):
                    for h in range(2):
                        last = nc.tensor.matmul(pv[:, n, h, 0:HALF], k.ones[0:1, :],
                                                last_f[0:1, n, h * HALF:(h + 1) * HALF], start=True, stop=True)
                last.then_inc(s_bcast, 1)
                pe.wait_ge(s_idx, 1)
                nc.tensor.transpose(pt[0][0:SB, 0, :], base_col[:, :], k.ident[:, :])
                nc.tensor.transpose(pt[0][0:SB, 1, :], j_col[:, :], k.ident[:, :]).then_inc(s_bcast, 1)
                pe.wait_ge(s_ijrow, 1)
                for b in range(SB):
                    pe.wait_ge(s_rowf, b + 1)
                    if b >= 2:
                        pe.wait_ge(s_rowc, b - 1)
                    for n in range(4):
                        last = nc.tensor.transpose(pt[b % 2][:, n, :], rowf[:, b % 2, n, :], k.ident[:, :])
                    last.then_inc(s_rowt, 1)
                pe.wait_ge(s_lo, 1)
                pe.wait_ge(s_rowc, SB)
                nc.tensor.transpose(pt[0][0:NT, 0, :], lo[:, :], k.ident[:, :]).then_inc(s_lot, 1)
                pe.wait_ge(s_degr, 1)
                nc.tensor.transpose(pt[1][:, 0, 0:NT], deg_row[:, :], k.ident[0:NT, 0:NT]).then_inc(s_degt, 1)

            @block.scalar
            def _(act):
                act.wait_ge(s_bcast, 2)
                nc.scalar.activation(ij_row[:, :, :], pt[0][0:SB, 0:2, :], ACT.Copy).then_inc(s_ijrow, 1)
                for b in range(SB):
                    act.wait_ge(s_rowt, b + 1)
                    w = min(P, NS - b * P)
                    for n, to in enumerate((k.drel, k.neg, k.weight, k.src)):
                        last = nc.scalar.activation(to[:, b * P:b * P + w], pt[b % 2][:, n, 0:w], ACT.Copy)
                    last.then_inc(s_rowc, 1)
                act.wait_ge(s_lot, 1)
                nc.scalar.activation(lo_row[:, :], pt[0][0:NT, 0, :], ACT.Copy).then_inc(s_lor, 1)
                act.wait_ge(s_pad, 4)
                act.sem_inc(s_lor, 1)
                act.wait_ge(s_degt, 1)
                nc.scalar.activation(k.deg[:, :], pt[1][:, 0, 0:NT], ACT.Copy).then_inc(s_deg, 1)

            @block.vector
            def _(dve):
                v = Chain(dve, s_vec)
                dve.wait_ge(s_io, 4)
                v(nc.vector.tensor_copy(k.iota[:, :], k.iota_i[:, :]))
                v(nc.vector.tensor_copy(step_col[:, :], step_i[:, :]))
                v(nc.vector.tensor_copy(node_col[:, :], node_i[:, :]))
                dve.wait_ge(s_last, 32)
                v(nc.vector.tensor_single_scalar(last_shr[:, :], last_dst[:, :], 7, op=ALU.logical_shift_right))
                v(nc.vector.tensor_copy(last_f[:, 0, :], last_shr[:, :]))
                v(nc.vector.tensor_copy(last_f[:, 1, :], tile_i[:, :]))
                v(nc.vector.tensor_tensor(last_f[:, 0, :], last_f[:, 0, :], last_f[:, 1, :], ALU.add))
                v(nc.vector.tensor_copy(last_f[:, 1, :], last_dst[:, :]))
                dve.sem_inc(s_v, 1)
                dve.wait_ge(s_bcast, 1)
                less2 = less[:, :].rearrange("p (h n) -> p h n", h=2)
                for b in range(SB):
                    v(nc.vector.tensor_scalar(less2, pv[:, 0, :, 0:HALF], step_col[:, b:b + 1], None, ALU.is_lt))
                    v(nc.vector.tensor_reduce(i_col[:, b:b + 1], less[:, :], AX.X, ALU.add))
                v(nc.vector.tensor_tensor(j_col[:, :], step_col[:, :], i_col[:, :], ALU.subtract))
                v(nc.vector.tensor_scalar_min(j_col[:, :], j_col[:, :], float(NT - 1)))
                v(nc.vector.tensor_scalar(base_col[:, :], i_col[:, :], float(P), float(E - P), ALU.mult, ALU.min))
                v(nc.vector.tensor_scalar(jbase[:, :], j_col[:, :], float(P), None, ALU.mult))
                v(nc.vector.tensor_copy(i_idx[:, :], i_col[:, :]))
                dve.sem_inc(s_idx, 1)
                for b in range(SB):
                    dve.wait_ge(k.got[b % 2], 16 * (b // 2 + 1))
                    if b >= 2:
                        dve.wait_ge(s_key[b % 2], 16 * (b // 2))
                        dve.wait_ge(s_rowt, b - 1)
                    r, f = rows[:, b % 2, :], rowf[:, b % 2, :, :]
                    v(nc.vector.tensor_scalar(f[:, 0, :], r[:, 0:P], jbase[:, b:b + 1], None, ALU.subtract))
                    v(nc.vector.tensor_scalar(d1[:, :], r[:, 0:P], 1.0, None, ALU.add))
                    v(nc.vector.tensor_scalar(ge0[:, :], f[:, 0, :], 0.0, None, ALU.is_ge))
                    v(nc.vector.scalar_tensor_tensor(out=valid[:, :], in0=f[:, 0, :], scalar=float(P), in1=ge0[:, :],
                                                     op0=ALU.is_lt, op1=ALU.mult))
                    v(nc.vector.tensor_tensor(f[:, 4, :], d1[:, :], valid[:, :], ALU.mult))
                    v(nc.vector.tensor_scalar(f[:, 1, :], valid[:, :], BIG, -BIG, ALU.mult, ALU.add))
                    v(nc.vector.tensor_scalar(f[:, 2, :], r[:, 2 * P:3 * P].bitcast(F32), float(C) ** -0.5, None, ALU.mult))
                    v(nc.vector.tensor_copy(f[:, 3, :], r[:, P:2 * P]))
                    dve.sem_inc(s_rowf, 1)
                dve.wait_ge(s_ijback, 48)
                v(nc.vector.tensor_tensor(k.same[:, 1:NS], same_i[:, 1:NS], same_i[:, 0:NS - 1], ALU.is_equal))
                v(nc.vector.memset(k.same[:, 0:1], 0.0))
                for t in range(NT):
                    v(nc.vector.tensor_scalar(less2, pv[:, 1, :, 0:HALF], node_col[:, t:t + 1], None, ALU.is_lt))
                    v(nc.vector.tensor_reduce(before[:, t:t + 1], less[:, :], AX.X, ALU.add))
                v(nc.vector.tensor_copy(before_idx[:, :], before[:, :]))
                dve.sem_inc(s_bidx, 1)
                for t in range(NT):
                    dve.wait_ge(k.got[4 + t % 4], 16 * (t // 4 + 1))
                    v(nc.vector.tensor_scalar(ncmp[:, :], nrows[:, t % 4, 0:P], node_col[:, t:t + 1], None, ALU.is_lt))
                    v(nc.vector.tensor_reduce(lo[:, t:t + 1], ncmp[:, :], AX.X, ALU.add))
                    dve.sem_inc(s_ncnt, 1)
                v(nc.vector.scalar_tensor_tensor(out=lo[:, :], in0=before[:, :], scalar=float(P), in1=lo[:, :],
                                                 op0=ALU.mult, op1=ALU.add))
                v(nc.vector.tensor_scalar_min(lo[:, :], lo[:, :], float(E)))
                dve.sem_inc(s_lo, 1)
                dve.wait_ge(s_lon, 16)
                v(nc.vector.tensor_tensor(deg_row[:, :], lo_next[:, :], lo_row[:, :], ALU.subtract))
                dve.sem_inc(s_degr, 1)
                dve.wait_ge(s_deg, 1)
                v(nc.vector.tensor_scalar_max(k.deg1[:, :], k.deg[:, :], 1.0))

    for n in range(2):
        k.seen[n] += 16 * len(range(n, SB, 2))
    for n in range(4):
        k.seen[4 + n] += 16 * len(range(n, NT, 4))
    with ExitStack() as c:
        s_sq, s_di = c.enter_context(nc.semaphore("sq")), c.enter_context(nc.semaphore("di"))
        with nc.Block() as block:
            @block.scalar
            def _(act):
                nc.scalar.activation(k.dis[:, :], k.deg1[:, :], ACT.Sqrt).then_inc(s_sq, 1)

            @block.vector
            def _(dve):
                v = Chain(dve, s_di)
                dve.wait_ge(s_sq, 1)
                v(nc.vector.reciprocal(k.dis[:, :], k.dis[:, :]))
                v(nc.vector.tensor_scalar_min(k.deg1[:, :], k.deg[:, :], 1.0))
                v(nc.vector.tensor_tensor(k.dis[:, :], k.dis[:, :], k.deg1[:, :], ALU.mult))


def globals_of(nc, c):
    sb = lambda name, shape, dt=F32: c.enter_context(nc.sbuf_tensor(name, shape, dt))
    c.enter_context(nc.allow_non_contiguous_dma(reason="a few small strided loads of indices and columns"))
    k = Kept()
    k.got = [c.enter_context(nc.semaphore(f"got{n}")) for n in range(8)]
    k.seen = [0] * 8
    k.tab = nc.dram_tensor("edge_rows", [ET + 1, 3 * P], I32)
    k.keys = nc.dram_tensor("keys", [P + SB * P * P], F32)
    k.ij = nc.dram_tensor("steps_ij", [2, SB * P], I32)
    k.lod = nc.dram_tensor("first_edge", [NPAD + P], F32)
    k.ident = sb("ident", [P, P])
    k.iota = sb("iota", [P, P])
    k.iota_i = sb("iota_i", [P, P], I32)
    k.ones = sb("ones", [1, P])
    k.drel = sb("drel", [P, NS])
    k.neg = sb("neg", [P, NS])
    k.weight = sb("weight", [P, NS])
    k.src = sb("srct", [P, NS], I32)
    k.same = sb("same", [P, NS])
    k.step_j = sb("step_j", [1, NS], I32)
    k.step_base = sb("step_base", [1, NS], I32)
    k.deg = sb("deg_", [P, NT])
    k.deg1 = sb("deg1", [P, NT])
    k.dis = sb("dis", [P, NT])
    k.eps = sb("eps", [P, 1])
    k.rs = sb("rs", [P, NT])
    k.nb = sb("nb", [P, NT])
    k.acc = sb("acc", [P, 2 * SEQ])
    return k


def row_stats(nc, tag, k, x):
    G = 7
    with ExitStack() as c:
        sb = lambda name, shape, dt=F32: c.enter_context(nc.sbuf_tensor(f"{tag}_{name}", shape, dt))
        sem = lambda name: c.enter_context(nc.semaphore(f"{tag}_{name}"))
        st = sb("bn_st", [P, NT * 6])
        mv = sb("bn_mv", [P, NT, 2])
        s_vec, s_var, s_std = sem("rs_vec"), sem("rs_var"), sem("rs_std")
        with nc.Block() as block:
            @block.vector
            def _(dve):
                v = Chain(dve, s_vec)
                xf = x.rearrange("p t d -> p (t d)")
                with dve.Fori(0, NT // G) as it:
                    for u in range(G):
                        nc.vector.bn_stats(st[:, ds(it * (6 * G) + 6 * u, 6)], xf[:, ds(it * (G * D) + u * D, D)])
                dve.drain()
                v(nc.vector.memset(k.eps[:, :], EPS))
                for t in range(NT):
                    last = nc.vector.bn_aggr(mv[:, t, :], st[:, 6 * t:6 * t + 6])
                last.then_inc(s_var, 1)
                dve.wait_ge(s_std, 1)
                v(nc.vector.reciprocal(k.rs[:, :], k.rs[:, :]))
                v(nc.vector.scalar_tensor_tensor(out=k.nb[:, :], in0=mv[:, :, 0], scalar=-1.0, in1=k.rs[:, :],
                                                 op0=ALU.mult, op1=ALU.mult))

            @block.scalar
            def _(act):
                act.wait_ge(s_var, 1)
                nc.scalar.activation(k.rs[:, :], mv[:, :, 1], ACT.Sqrt, bias=k.eps[:, 0:1]).then_inc(s_std, 1)


def normalized(nc, tag, k, x, y, func):
    with nc.semaphore(f"{tag}_norm") as s_norm, nc.Block() as block:
        @block.scalar
        def _(act):
            def body(it, u):
                t = it * 7 + u
                nc.scalar.activation(y[:, ds(t * D, D)], x[:, ds(t * D, D)], func, bias=k.nb[:, ds(t, 1)],
                                     scale=k.rs[:, ds(t, 1)]).then_inc(s_norm, 1)
            ticks(act, NT, 7, 0, body)
            act.wait_ge(s_norm, NT)


def project(nc, tag, k, x, func, outs):
    U = 4
    nout = len(outs)
    PB = 2
    with ExitStack() as c:
        sb = lambda name, shape, dt=F32: c.enter_context(nc.sbuf_tensor(f"{tag}_{name}", shape, dt))
        sem = lambda name: c.enter_context(nc.semaphore(f"{tag}_{name}"))
        z = sb("pj_z", [P, 2, D])
        zt = sb("pj_zt", [P, 2, D])
        pt = [c.enter_context(nc.psum_tensor(f"{tag}_pj_t{n}", [P, 512], F32)) for n in range(2)]
        po = [[c.enter_context(nc.psum_tensor(f"{tag}_pj_o{m}_{n}", [P, 512], F32)) for n in range(PB)] for m in range(nout)]
        ob = [sb(f"pj_b{m}", [P, 2, o[2]]) for m, o in enumerate(outs)]
        s_z, s_t, s_zt, s_o, s_ev = sem("pj_sz"), sem("pj_st"), sem("pj_szt"), sem("pj_so"), sem("pj_ev")
        stored = [sem(f"pj_store{n}") for n in range(2)]
        nst = sum(len(o[4]) for o in outs)
        with nc.Block() as block:
            @block.scalar
            def _(act):
                def body(it, u):
                    t = it * U + u
                    if live(it, u, U, NT):
                        wait(act, s_t, t - 1)
                        nc.scalar.activation(z[:, u % 2, :], x[:, ds(t * D, D)], func, bias=k.nb[:, ds(t, 1)],
                                             scale=k.rs[:, ds(t, 1)]).then_inc(s_z, 1)
                    r = u - 1
                    if live(it, r, U, NT):
                        s = it * U + r
                        act.wait_ge(s_o, s + 1)
                        if nst:
                            wait(act, stored[r % 2], (it * (U // 2) + (r // 2)) * (16 * nst))
                        for m, (w, b, width, col, st, target) in enumerate(outs):
                            scale = 1.0 if col is None else col[:, ds(s, 1)]
                            o = ob[m][:, r % 2, :] if target is None else target[:, ds(s * width, width)]
                            last = nc.scalar.activation(o, po[m][r % PB][:, 0:width], ACT.Copy, scale=scale)
                        last.then_inc(s_ev, 1)
                ticks(act, NT, U, 1, body)
                act.wait_ge(s_ev, NT)

            @block.vector
            def _(dve):
                def body(it, u):
                    t = it * U + u
                    if live(it, u, U, NT):
                        dve.wait_ge(s_t, t + 1)
                        wait(dve, s_o, t - 1)
                        nc.vector.tensor_copy(zt[:, u % 2, :], pt[u % 2][:, 0:D]).then_inc(s_zt, 1)
                ticks(dve, NT, U, 0, body)

            @block.tensor
            def _(pe):
                def body(it, u):
                    t = it * U + u
                    if live(it, u, U, NT):
                        pe.wait_ge(s_z, t + 1)
                        wait(pe, s_zt, t - 1)
                        for n in range(KT):
                            last = nc.tensor.transpose(pt[u % 2][:, n * P:(n + 1) * P], z[:, u % 2, n * P:(n + 1) * P],
                                                       k.ident[:, :])
                        last.then_inc(s_t, 1)
                    r = u - 1
                    if live(it, r, U, NT):
                        s = it * U + r
                        pe.wait_ge(s_zt, s + 1)
                        wait(pe, s_ev, s - PB + 1)
                        for m, (w, b, width, col, st, target) in enumerate(outs):
                            o = po[m][r % PB][:, 0:width]
                            for n in range(KT):
                                last = nc.tensor.matmul(o, zt[:, r % 2, n * P:(n + 1) * P], w[:, n, :],
                                                        start=(n == 0), stop=(n == KT - 1 and b is None))
                            if b is not None:
                                last = nc.tensor.matmul(o, k.ones[0:1, :], b, start=False, stop=True)
                        last.then_inc(s_o, 1)
                ticks(pe, NT, U, 1, body)

            @block.sync
            def _(sp):
                def body(it, u):
                    t = it * U + u
                    if nst and live(it, u, U, NT):
                        sp.wait_ge(s_ev, t + 1)
                        for m, (w, b, width, col, st, target) in enumerate(outs):
                            for first, cols, table in st:
                                sp.dma_start(table[ds(t * P, P), :],
                                             ob[m][:, u % 2, first:first + cols]).then_inc(stored[u % 2], 16)
                if nst:
                    ticks(sp, NT, U, 0, body)
                    sp.wait_ge(stored[0], 16 * nst * ((NT + 1) // 2))
                    sp.wait_ge(stored[1], 16 * nst * (NT // 2))


def aggregate(nc, tag, k, table, weights):
    R, W, LAG = 8, 4, 2
    with ExitStack() as c:
        sb = lambda name, shape, dt=F32: c.enter_context(nc.sbuf_tensor(f"{tag}_{name}", shape, dt))
        sem = lambda name: c.enter_context(nc.semaphore(f"{tag}_{name}"))
        idx = sb("ag_idx", [P, 2, UNROLL // 2], I32)
        got = sb("ag_got", [P, R, D])
        sel = sb("ag_sel", [P, W, P])
        wgt = sb("ag_wgt", [P, W, D]) if weights else None
        cur = sb("ag_cur", [P, W, AW])
        pa = [c.enter_context(nc.psum_tensor(f"{tag}_ag_p{n}", [P, 512], F32)) for n in range(W)]
        width = AW if weights else D
        s_idx, s_turn, s_got = sem("ag_si"), sem("ag_turn"), k.got
        s_rhs, s_mm, s_cur, s_acc, s_init = (sem("ag_rhs"), sem("ag_mm"), sem("ag_scur"), sem("ag_acc"),
                                             sem("ag_init"))
        s_used = s_rhs if weights else s_mm
        with nc.Block() as block:
            @block.gpsimd
            def _(pool):
                half = UNROLL // 2

                def body(it, u):
                    t = it * UNROLL + u
                    if u % half == 0:
                        h = u // half
                        nc.gpsimd.tensor_copy(idx[:, h, :], k.src[:, ds(t, half)]).then_inc(s_idx, 1)
                        pool.wait_ge(s_idx, it * 2 + h + 1)
                    wait(pool, s_used, t - R + 1)
                    pool.sem_inc(s_turn, 1)
                    pool.indirect_dma_start(got[:, u % R, :], None, table,
                                            bass.IndirectOffsetOnAxis(idx[:, u // half, u % half:u % half + 1], 0)
                                            ).then_inc(s_got[u % R], 16)
                ticks(pool, NS, UNROLL, 0, body)

            @block.vector
            def _(dve):
                for n in range(W):
                    last = nc.vector.memset(cur[:, n, :], 0.0)
                last.then_inc(s_init, 1)
                dve.wait_ge(s_init, 1)

                def body(it, u):
                    t = it * UNROLL + u
                    if live(it, u, UNROLL, NS):
                        wait(dve, s_mm, t - W + 1)
                        last = nc.vector.tensor_scalar(sel[:, u % W, :], k.iota[:, :], k.drel[:, ds(t, 1)], None,
                                                       ALU.is_equal)
                        if weights:
                            dve.wait_ge(s_got[u % R], 16 * fills(it, u, UNROLL, R) + k.seen[u % R])
                            last = nc.vector.tensor_tensor(
                                wgt[:, u % W, :].rearrange("p (h c) -> p h c", h=H),
                                got[:, u % R, :].rearrange("p (h c) -> p h c", h=H),
                                k.edge[:, ds(t * H, H)].unsqueeze(2).to_broadcast([P, H, C]), ALU.mult)
                        last.then_inc(s_rhs, 1)
                    r = u - LAG
                    if live(it, r, UNROLL, NS):
                        s = it * UNROLL + r
                        dve.wait_ge(s_mm, s + 1)
                        wait(dve, s_cur, s)
                        wait(dve, s_acc, s - W + 1)
                        nc.vector.scalar_tensor_tensor(
                            out=cur[:, r % W, 0:width], in0=cur[:, (r - 1) % W, 0:width], scalar=k.same[:, ds(s, 1)],
                            in1=pa[r % W][:, 0:width], op0=ALU.mult, op1=ALU.add).then_inc(s_cur, 1)
                ticks(dve, NS, UNROLL, LAG, body)

            @block.tensor
            def _(pe):
                def body(it, u):
                    t = it * UNROLL + u
                    pe.wait_ge(s_rhs, t + 1)
                    wait(pe, s_cur, t - W + 1)
                    if weights:
                        nc.tensor.matmul(pa[u % W][:, 0:D], sel[:, u % W, :], wgt[:, u % W, :], start=True, stop=True)
                        nc.tensor.matmul(pa[u % W][:, D:AW], sel[:, u % W, :], k.edge[:, ds(t * H, H)],
                                         start=True, stop=True).then_inc(s_mm, 1)
                    else:
                        pe.wait_ge(s_got[u % R], 16 * fills(it, u, UNROLL, R) + k.seen[u % R])
                        nc.tensor.matmul(pa[u % W][:, 0:D], sel[:, u % W, :], got[:, u % R, :],
                                         start=True, stop=True).then_inc(s_mm, 1)
                ticks(pe, NS, UNROLL, 0, body)

            @block.scalar
            def _(act):
                def body(it, u):
                    s = it * UNROLL + u
                    if u % 4 == 0:
                        _, act_j[0] = nc.values_load_multi_w_load_instructions(
                            k.step_j[0:1, ds(s, 4)], engines=(mybir.EngineType.Activation,), min_val=0, max_val=NT - 1,
                            skip_runtime_bounds_check_because="j(s) is clamped to the last node tile")
                    act.wait_ge(s_cur, s + 1)
                    wait(act, s_acc, s)
                    nc.scalar.activation(k.acc[:, ds(act_j[0][u % 4] * AW, width)], cur[:, u % W, 0:width],
                                         ACT.Copy).then_inc(s_acc, 1)
                act_j = [None]
                ticks(act, NS, UNROLL, 0, body)
                act.wait_ge(s_acc, NS)
    for n in range(R):
        k.seen[n] += 16 * (NS // R)


def layer0_edges(nc, k, xr, src, dst, t0, al0):
    G = 7
    W0 = D + H0
    with ExitStack() as c:
        sb = lambda name, shape, dt=F32: c.enter_context(nc.sbuf_tensor(name, shape, dt))
        sem = lambda name: c.enter_context(nc.semaphore(name))
        er = sb("l0_er", [NT, 2, P], I32)
        erf = sb("l0_erf", [NT, 2, P])
        ei = sb("l0_ei", [P, 2, NT], I32)
        al = sb("l0_al", [P, NT, H0])
        lg = sb("l0_lg", [P, NT, H0])
        mx = sb("l0_mx", [P, NT])
        tmp = sb("l0_tmp", [P, G, C0])
        got = k.acc[:, 0:NT * W0].rearrange("p (t w) -> p t w", w=W0)
        pt = c.enter_context(nc.psum_tensor("l0_pt", [P, 2, P], F32))
        s_ld, s_f, s_t, s_i = sem("l0_ld"), sem("l0_sf"), sem("l0_st"), sem("l0_si")
        s_al, s_got, s_ex, s_v, s_lg = k.got[NT // G], k.got[0:NT // G], sem("l0_ex"), sem("l0_v"), sem("l0_slg")
        with nc.Block() as block:
            @block.sync
            def _(sp):
                for n, a in enumerate((src, dst)):
                    sp.dma_start(er[:, n, :], a[0:NPAD].rearrange("(t p) -> t p", p=P)).then_inc(s_ld, 16)

            @block.tensor
            def _(pe):
                pe.wait_ge(s_f, 1)
                nc.tensor.transpose(pt[:, 0, 0:NT], erf[:, 0, :], k.ident[0:NT, 0:NT])
                nc.tensor.transpose(pt[:, 1, 0:NT], erf[:, 1, :], k.ident[0:NT, 0:NT]).then_inc(s_t, 1)

            @block.gpsimd
            def _(pool):
                pool.wait_ge(s_i, 1)
                for t in range(NT):
                    pool.indirect_dma_start(al[:, t, :], None, al0, bass.IndirectOffsetOnAxis(ei[:, 0, t:t + 1], 0)
                                            ).then_inc(s_al, 16)
                    pool.indirect_dma_start(got[:, t, :], None, t0, bass.IndirectOffsetOnAxis(ei[:, 1, t:t + 1], 0)
                                            ).then_inc(s_got[t // G], 16)

            @block.scalar
            def _(act):
                act.wait_ge(s_lg, 1)
                nc.scalar.activation(lg[:, :, :], lg[:, :, :], ACT.Exp).then_inc(s_ex, 1)

            @block.vector
            def _(dve):
                v = Chain(dve, s_v)
                dve.wait_ge(s_ld, 32)
                v(nc.vector.tensor_copy(erf[:, :, :], er[:, :, :]))
                dve.sem_inc(s_f, 1)
                dve.wait_ge(s_t, 1)
                v(nc.vector.tensor_copy(ei[:, :, :], pt[:, :, 0:NT]))
                dve.sem_inc(s_i, 1)
                dve.wait_ge(s_al, k.seen[NT // G] + 16 * NT)
                for g in range(NT // G):
                    dve.wait_ge(s_got[g], k.seen[g] + 16 * G)
                bc = lambda a: a.unsqueeze(2).to_broadcast([P, NT, H0])
                v(nc.vector.tensor_tensor(lg[:, :, :], al[:, :, :], got[:, :, D:W0], ALU.add))
                v(nc.vector.scalar_tensor_tensor(out=lg[:, :, :], in0=lg[:, :, :], scalar=0.01, in1=lg[:, :, :],
                                                 op0=ALU.mult, op1=ALU.max))
                v(nc.vector.tensor_reduce(mx[:, :], lg[:, :, :], AX.X, ALU.max))
                v(nc.vector.tensor_tensor(lg[:, :, :], lg[:, :, :], bc(mx[:, :]), ALU.subtract))
                dve.sem_inc(s_lg, 1)
                dve.wait_ge(s_ex, 1)
                v(nc.vector.tensor_reduce(mx[:, :], lg[:, :, :], AX.X, ALU.add))
                v(nc.vector.reciprocal(mx[:, :], mx[:, :]))
                v(nc.vector.tensor_tensor(lg[:, :, :], lg[:, :, :], bc(mx[:, :]), ALU.mult))
                for g in range(NT // G):
                    ts = slice(g * G, (g + 1) * G)
                    rows = got[:, ts, 0:D].rearrange("p t (h d) -> p t h d", h=H0)
                    v(nc.vector.tensor_tensor(rows, rows, lg[:, ts, :].unsqueeze(3).to_broadcast([P, G, H0, C0]), ALU.mult))
                    v(nc.vector.tensor_reduce(tmp[:, :, :], got[:, ts, 0:D].rearrange("p t (h d) -> p t d h", h=H0),
                                              AX.X, ALU.add))
                    xv = xr[:, g * G * D:(g + 1) * G * D].rearrange("p (t h d) -> p t h d", t=G, h=H0)
                    v(nc.vector.tensor_tensor(xv, xv, tmp[:, :, :].unsqueeze(2).to_broadcast([P, G, H0, C0]), ALU.add))
    for g in range(NT // G):
        k.seen[g] += 16 * G
    k.seen[NT // G] += 16 * NT


def add_scaled(nc, k, xr):
    with nc.semaphore("as_v") as s_v, nc.Block() as block:
        @block.vector
        def _(dve):
            def body(it, u):
                t = it * 7 + u
                nc.vector.scalar_tensor_tensor(out=xr[:, ds(t * D, D)], in0=k.acc[:, ds(t * AW, D)],
                                               scalar=k.dis[:, ds(t, 1)], in1=xr[:, ds(t * D, D)],
                                               op0=ALU.mult, op1=ALU.add).then_inc(s_v, 1)
            ticks(dve, NT, 7, 0, body)
            dve.wait_ge(s_v, NT)


def layer2_scores(nc, k, keys, queries, we, ef):
    R, W, EB = 8, 4, 4
    with ExitStack() as c:
        sb = lambda name, shape, dt=F32: c.enter_context(nc.sbuf_tensor(name, shape, dt))
        sem = lambda name: c.enter_context(nc.semaphore(name))
        half = UNROLL // 2
        idx = sb("sc_idx", [P, 2, half], I32)
        got = sb("sc_got", [P, R, D])
        sel = sb("sc_sel", [P, W, P])
        efr = sb("sc_ef", [P, EB, P])
        tr = sb("sc_tr", [P, 2, 2 * P])
        prod = sb("sc_prod", [P, W, D])
        epr = sb("sc_ep", [P, W, C])
        pt = [c.enter_context(nc.psum_tensor(f"sc_t{n}", [P, 512], F32)) for n in range(2)]
        pq = [c.enter_context(nc.psum_tensor(f"sc_q{n}", [P, 512], F32)) for n in range(W)]
        pw = [c.enter_context(nc.psum_tensor(f"sc_w{n}", [P, 512], F32)) for n in range(2)]
        s_idx, s_turn, s_got, s_ef = sem("sc_idx_"), sem("sc_turn"), k.got, [sem(f"sc_efs{n}") for n in range(EB)]
        s_init, s_sel, s_tr, s_cp, s_q, s_key, s_prod, s_sc, s_ae = (
            sem("sc_init"), sem("sc_ssel"), sem("sc_str"), sem("sc_cp"), sem("sc_sq"), sem("sc_key"),
            sem("sc_sprod"), sem("sc_sc"), sem("sc_ae"))
        with nc.Block() as block:
            @block.gpsimd
            def _(pool):
                nc.gpsimd.memset(efr[:, :, :], 0.0).then_inc(s_init, 1)
                pool.wait_ge(s_init, 1)
                nc.gpsimd.memset(efr[:, :, ED:ED + 1], 1.0).then_inc(s_init, 1)

                def body(it, u):
                    t = it * UNROLL + u
                    if u % half == 0:
                        h = u // half
                        nc.gpsimd.tensor_copy(idx[:, h, :], k.src[:, ds(t, half)]).then_inc(s_idx, 1)
                        pool.wait_ge(s_idx, it * 2 + h + 1)
                    wait(pool, s_key, t - R + 1)
                    pool.sem_inc(s_turn, 1)
                    pool.indirect_dma_start(got[:, u % R, :], None, keys,
                                            bass.IndirectOffsetOnAxis(idx[:, u // half, u % half:u % half + 1], 0)
                                            ).then_inc(s_got[u % R], 16)
                ticks(pool, NS, UNROLL, 0, body)

            @block.sync
            def _(sp):
                base = [None]
                sp.wait_ge(s_init, 2)

                def body(it, u):
                    t = it * UNROLL + u
                    if u % 4 == 0:
                        _, base[0] = nc.values_load_multi_w_load_instructions(
                            k.step_base[0:1, ds(t, 4)], engines=(mybir.EngineType.SP,), min_val=0, max_val=E - P,
                            skip_runtime_bounds_check_because="the first edge of a tile is clamped to E - P")
                    wait(sp, s_tr, t - EB + 1)
                    sp.dma_start(efr[:, u % EB, 0:ED], ef[ds(base[0][u % 4], P), :]).then_inc(s_ef[u % EB], 16)
                ticks(sp, NS, UNROLL, 0, body)

            @block.vector
            def _(dve):
                heads = lambda a: a.rearrange("p (h c) -> p h c", h=H)

                def body(it, u):
                    t = it * UNROLL + u
                    if live(it, u, UNROLL, NS):
                        wait(dve, s_tr, t - W + 1)
                        nc.vector.tensor_scalar(sel[:, u % W, :], k.iota[:, :], k.drel[:, ds(t, 1)], None,
                                                ALU.is_equal).then_inc(s_sel, 1)
                    a = u - 3
                    if live(it, a, UNROLL, NS):
                        s = it * UNROLL + a
                        dve.wait_ge(s_ae, s + 1)
                        dve.wait_ge(s_got[a % R], 16 * fills(it, a, UNROLL, R) + k.seen[a % R])
                        wait(dve, s_sc, s - W + 1)
                        nc.vector.tensor_tensor(
                            heads(prod[:, a % W, :]), heads(got[:, a % R, :]),
                            epr[:, a % W, :].unsqueeze(1).to_broadcast([P, H, C]), ALU.add).then_inc(s_key, 1)
                    b = u - 4
                    if live(it, b, UNROLL, NS):
                        s = it * UNROLL + b
                        dve.wait_ge(s_key, s + 1)
                        dve.wait_ge(s_q, s + 1)
                        nc.vector.tensor_tensor(prod[:, b % W, :], prod[:, b % W, :], pq[b % W][:, 0:D],
                                                ALU.mult).then_inc(s_prod, 1)
                    e = u - 5
                    if live(it, e, UNROLL, NS):
                        s = it * UNROLL + e
                        dve.wait_ge(s_prod, s + 1)
                        nc.vector.tensor_reduce(k.edge[:, ds(s * H, H)], heads(prod[:, e % W, :]), AX.X,
                                                ALU.add).then_inc(s_sc, 1)
                ticks(dve, NS, UNROLL, 5, body)
                dve.wait_ge(s_sc, NS)

            @block.tensor
            def _(pe):
                j = [None]

                def body(it, u):
                    t = it * UNROLL + u
                    if live(it, u, UNROLL, NS):
                        pe.wait_ge(s_sel, t + 1)
                        pe.wait_ge(s_ef[u % EB], 16 * fills(it, u, UNROLL, EB))
                        wait(pe, s_cp, t - 1)
                        nc.tensor.transpose(pt[u % 2][:, 0:P], sel[:, u % W, :], k.ident[:, :])
                        nc.tensor.transpose(pt[u % 2][:, P:2 * P], efr[:, u % EB, :], k.ident[:, :]).then_inc(s_tr, 1)
                    r = u - 1
                    if live(it, r, UNROLL, NS):
                        s = it * UNROLL + r
                        if r % 4 == 0 or j[0] is None or (u == 0):
                            first = s - r % 4
                            _, j[0] = nc.values_load_multi_w_load_instructions(
                                k.step_j[0:1, ds(first, 4)], engines=(mybir.EngineType.PE,), min_val=0, max_val=NT - 1,
                                skip_runtime_bounds_check_because="j(s) is clamped to the last node tile")
                        pe.wait_ge(s_cp, s + 1)
                        wait(pe, s_prod, s - W + 1)
                        wait(pe, s_ae, s - 1)
                        nc.tensor.matmul(pq[r % W][:, 0:D], tr[:, r % 2, 0:P], queries[:, ds(j[0][r % 4] * D, D)],
                                         start=True, stop=True)
                        nc.tensor.matmul(pw[r % 2][:, 0:EW], tr[:, r % 2, P:2 * P], we, start=True,
                                         stop=True).then_inc(s_q, 1)
                ticks(pe, NS, UNROLL, 1, body)

            @block.scalar
            def _(act):
                def body(it, u):
                    t = it * UNROLL + u
                    if live(it, u, UNROLL, NS):
                        act.wait_ge(s_tr, t + 1)
                        wait(act, s_q, t - 1)
                        nc.scalar.activation(tr[:, u % 2, :], pt[u % 2][:, 0:2 * P], ACT.Copy).then_inc(s_cp, 1)
                    r = u - 2
                    if live(it, r, UNROLL, NS):
                        s = it * UNROLL + r
                        act.wait_ge(s_q, s + 1)
                        wait(act, s_key, s - W + 1)
                        nc.scalar.activation(k.ae[:, ds(s * H, H)], pw[r % 2][:, C:EW], ACT.Copy)
                        nc.scalar.activation(epr[:, r % W, :], pw[r % 2][:, 0:C], ACT.Copy).then_inc(s_ae, 1)
                ticks(act, NS, UNROLL, 2, body)
                act.wait_ge(s_ae, NS)
    for n in range(R):
        k.seen[n] += 16 * (NS // R)


def layer3_logits(nc, k, a_src, a_dst):
    R, W = 8, 4
    with ExitStack() as c:
        sb = lambda name, shape, dt=F32: c.enter_context(nc.sbuf_tensor(name, shape, dt))
        sem = lambda name: c.enter_context(nc.semaphore(name))
        half = UNROLL // 2
        idx = sb("lg_idx", [P, 2, half], I32)
        got = sb("lg_got", [P, R, H])
        sel = sb("lg_sel", [P, W, P])
        tr = sb("lg_tr", [P, 2, P])
        pt = [c.enter_context(nc.psum_tensor(f"lg_t{n}", [P, 512], F32)) for n in range(2)]
        pq = [c.enter_context(nc.psum_tensor(f"lg_q{n}", [P, 512], F32)) for n in range(W)]
        s_idx, s_turn, s_got = sem("lg_idx_"), sem("lg_turn"), k.got
        s_sel, s_tr, s_cp, s_q, s_sc = sem("lg_ssel"), sem("lg_str"), sem("lg_cp"), sem("lg_sq"), sem("lg_sc")
        with nc.Block() as block:
            @block.gpsimd
            def _(pool):
                def body(it, u):
                    t = it * UNROLL + u
                    if u % half == 0:
                        h = u // half
                        nc.gpsimd.tensor_copy(idx[:, h, :], k.src[:, ds(t, half)]).then_inc(s_idx, 1)
                        pool.wait_ge(s_idx, it * 2 + h + 1)
                    wait(pool, s_sc, t - R + 1)
                    pool.sem_inc(s_turn, 1)
                    pool.indirect_dma_start(got[:, u % R, :], None, a_src,
                                            bass.IndirectOffsetOnAxis(idx[:, u // half, u % half:u % half + 1], 0)
                                            ).then_inc(s_got[u % R], 16)
                ticks(pool, NS, UNROLL, 0, body)

            @block.vector
            def _(dve):
                def body(it, u):
                    t = it * UNROLL + u
                    if live(it, u, UNROLL, NS):
                        wait(dve, s_tr, t - W + 1)
                        nc.vector.tensor_scalar(sel[:, u % W, :], k.iota[:, :], k.drel[:, ds(t, 1)], None,
                                                ALU.is_equal).then_inc(s_sel, 1)
                    a = u - 3
                    if live(it, a, UNROLL, NS):
                        s = it * UNROLL + a
                        dve.wait_ge(s_q, s + 1)
                        dve.wait_ge(s_got[a % R], 16 * fills(it, a, UNROLL, R) + k.seen[a % R])
                        nc.vector.tensor_tensor(k.edge[:, ds(s * H, H)], got[:, a % R, :], pq[a % W][:, 0:H],
                                                ALU.add).then_inc(s_sc, 1)
                ticks(dve, NS, UNROLL, 3, body)
                dve.wait_ge(s_sc, NS)

            @block.tensor
            def _(pe):
                j = [None]

                def body(it, u):
                    t = it * UNROLL + u
                    if live(it, u, UNROLL, NS):
                        pe.wait_ge(s_sel, t + 1)
                        wait(pe, s_cp, t - 1)
                        nc.tensor.transpose(pt[u % 2][:, 0:P], sel[:, u % W, :], k.ident[:, :]).then_inc(s_tr, 1)
                    r = u - 1
                    if live(it, r, UNROLL, NS):
                        s = it * UNROLL + r
                        if r % 4 == 0 or j[0] is None or (u == 0):
                            first = s - r % 4
                            _, j[0] = nc.values_load_multi_w_load_instructions(
                                k.step_j[0:1, ds(first, 4)], engines=(mybir.EngineType.PE,), min_val=0, max_val=NT - 1,
                                skip_runtime_bounds_check_because="j(s) is clamped to the last node tile")
                        pe.wait_ge(s_cp, s + 1)
                        wait(pe, s_sc, s - W + 1)
                        nc.tensor.matmul(pq[r % W][:, 0:H], tr[:, r % 2, :], a_dst[:, ds(j[0][r % 4] * H, H)],
                                         start=True, stop=True).then_inc(s_q, 1)
                ticks(pe, NS, UNROLL, 1, body)

            @block.scalar
            def _(act):
                def body(it, u):
                    t = it * UNROLL + u
                    act.wait_ge(s_tr, t + 1)
                    wait(act, s_q, t - 1)
                    nc.scalar.activation(tr[:, u % 2, :], pt[u % 2][:, 0:P], ACT.Copy).then_inc(s_cp, 1)
                ticks(act, NS, UNROLL, 0, body)
    for n in range(R):
        k.seen[n] += 16 * (NS // R)


def segment_softmax(nc, tag, k, leaky):
    NB4 = CB // 4
    with ExitStack() as c:
        sb = lambda name, shape, dt=F32: c.enter_context(nc.sbuf_tensor(f"{tag}_{name}", shape, dt))
        sem = lambda name: c.enter_context(nc.semaphore(f"{tag}_{name}"))
        seq, run = k.acc[:, 0:SEQ], k.acc[:, SEQ:2 * SEQ]
        kraw = k.acc[:, 0:SEQ + 2]
        new = sb("sm_new", [P, SEQ + 1])
        per = sb("sm_per", [P, CB * P])
        tail = sb("sm_tail", [P, 2])
        ct = sb("sm_ct", [H, CH, 2])
        chain = sb("sm_chain", [H, CH + 1])
        init = sb("sm_init", [P, 1])
        dt_ = [nc.dram_tensor(f"{tag}_sm_tail{n}", [P, 2], F32) for n in range(2)]
        dc_ = [nc.dram_tensor(f"{tag}_sm_chain{n}", [P, 1], F32) for n in range(2)]
        pt = [c.enter_context(nc.psum_tensor(f"{tag}_sm_p{n}", [P, 512], F32)) for n in range(4)]
        s_key, s_v, s_per, s_t, s_seq, s_max, s_b, s_sub, s_ex = (
            sem("sm_key"), sem("sm_v"), sem("sm_sper"), sem("sm_st"), sem("sm_sseq"), sem("sm_max"), sem("sm_b"),
            sem("sm_sub"), sem("sm_ex"))
        s_ae = sem("sm_ae")
        s_tail, s_ct, s_chain, s_in, s_td = sem("sm_stail"), sem("sm_sct"), sem("sm_schain"), sem("sm_sin"), sem("sm_std")
        bch = lambda a: a.rearrange("p (c b h) -> p c b h", c=CH, h=H)
        perm = per[:, :].rearrange("p (b c h) -> p c b h", c=CH, h=H)
        perh = lambda a: a.rearrange("p (c b) -> p c b", c=CH).unsqueeze(3).to_broadcast([P, CH, CB, H])
        edge4 = bch(k.edge[:, :])
        with nc.Block() as block:
            @block.sync
            def _(sp):
                if leaky:
                    sp.dma_start(new[:, 0:SEQ], k.ae_dram.ap()).then_inc(s_ae, 16)
                for ch in range(CH):
                    sp.dma_start(kraw[ch * H:(ch + 1) * H, :],
                                 k.keys.ap()[P - 1 + ch * SEQ:P + 1 + (ch + 1) * SEQ]
                                 .rearrange("(a n) -> a n", a=1).to_broadcast([H, SEQ + 2])).then_inc(s_key, 16)
                for n in range(2):
                    sp.wait_ge(s_tail, n + 1)
                    sp.dma_start(dt_[n].ap(), tail[:, :]).then_inc(s_td, 16)
                    sp.wait_ge(s_td, 16 * (4 * n + 1))
                    sp.dma_start(ct[:, :, :], dt_[n].ap().rearrange("(c h) w -> h c w", h=H)).then_inc(s_td, 16)
                    sp.wait_ge(s_td, 16 * (4 * n + 2))
                    sp.sem_inc(s_ct, 1)
                    sp.wait_ge(s_chain, n + 1)
                    sp.dma_start(dc_[n].ap().rearrange("(c h) w -> h (c w)", h=H),
                                 chain[:, n:n + CH]).then_inc(s_td, 16)
                    sp.wait_ge(s_td, 16 * (4 * n + 3))
                    sp.dma_start(init[:, :], dc_[n].ap()).then_inc(s_td, 16)
                    sp.wait_ge(s_td, 16 * (4 * n + 4))
                    sp.sem_inc(s_in, 1)

            @block.vector
            def _(dve):
                v = Chain(dve, s_v)
                if leaky:
                    dve.wait_ge(s_ae, 16)
                    v(nc.vector.tensor_tensor(k.edge[:, :], k.edge[:, :], new[:, 0:SEQ], ALU.add))
                    v(nc.vector.scalar_tensor_tensor(out=k.edge[:, :], in0=k.edge[:, :], scalar=0.2, in1=k.edge[:, :],
                                                     op0=ALU.mult, op1=ALU.max))
                    v(nc.vector.tensor_tensor(perm, edge4, perh(k.neg[:, :]), ALU.add))
                else:
                    v(nc.vector.tensor_tensor(perm, edge4, perh(k.weight[:, :]), ALU.mult))
                    v(nc.vector.tensor_tensor(perm, perm, perh(k.neg[:, :]), ALU.add))
                dve.sem_inc(s_per, 1)
                dve.wait_ge(s_key, 16 * CH)
                v(nc.vector.tensor_tensor(new[:, :], kraw[:, 1:SEQ + 2], kraw[:, 0:SEQ + 1], ALU.not_equal))
                v(nc.vector.tensor_scalar(new[:, :], new[:, :], -BIG, None, ALU.mult))
                dve.sem_inc(s_per, 1)
                dve.wait_ge(s_seq, NB4)
                rev = lambda a: a[:, ::-1]
                v(nc.vector.tensor_tensor_scan(run, new[:, 0:SEQ], seq, -BIG, ALU.add, ALU.max))
                v(nc.vector.tensor_copy(tail[:, 1:2], run[:, SEQ - 1:SEQ]))
                v(nc.vector.tensor_reduce(tail[:, 0:1], new[:, 0:SEQ], AX.X, ALU.min))
                dve.sem_inc(s_tail, 1)
                v(nc.vector.memset(chain[:, :], -BIG))
                dve.wait_ge(s_ct, 1)
                v(nc.vector.tensor_tensor_scan(chain[:, 1:CH + 1], ct[:, :, 0], ct[:, :, 1], -BIG, ALU.add, ALU.max))
                dve.sem_inc(s_chain, 1)
                dve.wait_ge(s_in, 1)
                v(nc.vector.tensor_tensor_scan(run, new[:, 0:SEQ], seq, init[:, 0:1], ALU.add, ALU.max))
                v(nc.vector.tensor_tensor_scan(rev(seq), rev(new[:, 1:SEQ + 1]), rev(run), -BIG, ALU.add, ALU.max))
                v(nc.vector.tensor_copy(tail[:, 1:2], seq[:, 0:1]))
                v(nc.vector.tensor_reduce(tail[:, 0:1], new[:, 1:SEQ + 1], AX.X, ALU.min))
                dve.sem_inc(s_tail, 1)
                v(nc.vector.memset(chain[:, :], -BIG))
                dve.wait_ge(s_ct, 2)
                v(nc.vector.tensor_tensor_scan(chain[:, 0:CH][:, ::-1], ct[:, ::-1, 0], ct[:, ::-1, 1], -BIG,
                                               ALU.add, ALU.max))
                dve.sem_inc(s_chain, 1)
                dve.wait_ge(s_in, 2)
                v(nc.vector.tensor_tensor_scan(rev(seq), rev(new[:, 1:SEQ + 1]), rev(run), init[:, 0:1], ALU.add, ALU.max))
                dve.sem_inc(s_max, 1)
                for g in range(NB4):
                    dve.wait_ge(s_b, g + 1)
                    nc.vector.tensor_tensor(per[:, g * 512:(g + 1) * 512], per[:, g * 512:(g + 1) * 512], pt[g % 4][:, :],
                                            ALU.subtract).then_inc(s_sub, 1)

            @block.tensor
            def _(pe):
                pe.wait_ge(s_per, 1)
                for g in range(NB4):
                    wait(pe, s_seq, g - 3)
                    for n in range(4):
                        b = g * 4 + n
                        last = nc.tensor.transpose(pt[g % 4][:, n * P:(n + 1) * P], per[:, b * P:(b + 1) * P], k.ident[:, :])
                    last.then_inc(s_t, 1)
                pe.wait_ge(s_max, 1)
                for g in range(NB4):
                    wait(pe, s_sub, g - 3)
                    for n in range(4):
                        b = g * 4 + n
                        last = nc.tensor.transpose(pt[g % 4][:, n * P:(n + 1) * P], k.acc[:, b * P:(b + 1) * P], k.ident[:, :])
                    last.then_inc(s_b, 1)

            @block.scalar
            def _(act):
                act.wait_ge(s_per, 2)
                for g in range(NB4):
                    act.wait_ge(s_t, g + 1)
                    nc.scalar.activation(k.acc[:, g * 512:(g + 1) * 512], pt[g % 4][:, :], ACT.Copy).then_inc(s_seq, 1)
                for g in range(NB4):
                    act.wait_ge(s_sub, g + 1)
                    nc.scalar.activation(edge4[:, :, g * 4:(g + 1) * 4, :],
                                         per[:, g * 512:(g + 1) * 512].rearrange("p (b c h) -> p c b h", c=CH, h=H),
                                         ACT.Exp).then_inc(s_ex, 1)
                act.wait_ge(s_ex, NB4)




def recycle(nc):
    used = sorted(nc.released_uncleared_semaphores)
    with nc.Block() as block:
        @block.gpsimd
        def _(pool):
            pool.sem_clear(range(used[0], used[-1] + 1))


def load(nc, name, pairs):
    with nc.semaphore(name) as s, nc.Block() as block:
        @block.sync
        def _(sp):
            for tile, source in pairs:
                sp.dma_start(tile, source).then_inc(s, 16)
            sp.wait_ge(s, 16 * len(pairs))


def store(nc, name, target, tile):
    with nc.semaphore(name) as s, nc.Block() as block:
        @block.sync
        def _(sp):
            sp.dma_start(target, tile).then_inc(s, 16)
            sp.wait_ge(s, 16)


def rows_of(w, kt=KT):
    return w.rearrange("(k p) n -> p k n", k=kt)


def spread(a, rows=P):
    return a.rearrange("(a n) -> a n", a=1).to_broadcast([rows, a.shape[0]])


def column(a):
    return a.rearrange("(k p) -> p k", p=P)


def fold_gain(nc, k, name, w, width, gain, shift, bias, cols):
    with ExitStack() as c:
        sem = lambda n: c.enter_context(nc.semaphore(name + n))
        pb = [c.enter_context(nc.psum_tensor(f"{name}p{n}", [P, 512], F32)) for n in range(2)]
        s_mm, s_v = sem("mm"), sem("v")
        with nc.Block() as block:
            @block.tensor
            def _(pe):
                if cols:
                    for f in range(width // P):
                        for n in range(KT):
                            last = nc.tensor.matmul(pb[0][:, f:f + 1], w[:, n, f * P:(f + 1) * P], shift[:, n:n + 1],
                                                    start=(n == 0), stop=(n == KT - 1))
                else:
                    for n in range(KT):
                        last = nc.tensor.matmul(pb[0][0:1, 0:width], shift[:, n:n + 1], w[:, n, :], start=(n == 0),
                                                stop=(n == KT - 1))
                last.then_inc(s_mm, 1)

            @block.vector
            def _(dve):
                v = Chain(dve, s_v)
                dve.wait_ge(s_mm, 1)
                if cols:
                    v(nc.vector.tensor_tensor(bias, bias, pb[0][:, 0:width // P], ALU.add))
                else:
                    v(nc.vector.tensor_tensor(bias, bias, pb[0][0:1, 0:width], ALU.add))
                for n in range(KT):
                    v(nc.vector.tensor_scalar(w[:, n, :], w[:, n, :], gain[:, n:n + 1], None, ALU.mult))


def attention_output(nc, k, y, wo, bo, alpha, rd):
    U = 4
    with ExitStack() as c:
        sb = lambda name, shape, dt=F32: c.enter_context(nc.sbuf_tensor(name, shape, dt))
        sem = lambda name: c.enter_context(nc.semaphore(name))
        a = sb("ao_a", [P, 2, D])
        at = sb("ao_at", [P, 2, D])
        pt = [c.enter_context(nc.psum_tensor(f"ao_t{n}", [P, 512], F32)) for n in range(2)]
        po = [c.enter_context(nc.psum_tensor(f"ao_o{n}", [P, 512], F32)) for n in range(2)]
        s_a, s_t, s_at, s_o, s_y = sem("ao_sa"), sem("ao_st"), sem("ao_sat"), sem("ao_so"), sem("ao_sy")
        with nc.Block() as block:
            @block.vector
            def _(dve):
                def body(it, u):
                    t = it * U + u
                    if live(it, u, U, NT):
                        wait(dve, s_t, t - 1)
                        nc.vector.tensor_tensor(
                            a[:, u % 2, :].rearrange("p (h c) -> p h c", h=H),
                            k.acc[:, ds(t * AW, D)].rearrange("p (h c) -> p h c", h=H),
                            rd[:, ds(t * H, H)].unsqueeze(2).to_broadcast([P, H, C]), ALU.mult).then_inc(s_a, 1)
                    r = u - 2
                    if live(it, r, U, NT):
                        s = it * U + r
                        dve.wait_ge(s_o, s + 1)
                        nc.vector.scalar_tensor_tensor(out=y[:, ds(s * D, D)], in0=po[r % 2][:, 0:D], scalar=alpha,
                                                       in1=y[:, ds(s * D, D)], op0=ALU.mult, op1=ALU.add).then_inc(s_y, 1)
                ticks(dve, NT, U, 2, body)
                dve.wait_ge(s_y, NT)

            @block.scalar
            def _(act):
                def body(it, u):
                    t = it * U + u
                    act.wait_ge(s_t, t + 1)
                    wait(act, s_o, t - 1)
                    nc.scalar.activation(at[:, u % 2, :], pt[u % 2][:, 0:D], ACT.Copy).then_inc(s_at, 1)
                ticks(act, NT, U, 0, body)

            @block.tensor
            def _(pe):
                def body(it, u):
                    t = it * U + u
                    if live(it, u, U, NT):
                        pe.wait_ge(s_a, t + 1)
                        wait(pe, s_at, t - 1)
                        for n in range(KT):
                            last = nc.tensor.transpose(pt[u % 2][:, n * P:(n + 1) * P], a[:, u % 2, n * P:(n + 1) * P],
                                                       k.ident[:, :])
                        last.then_inc(s_t, 1)
                    r = u - 1
                    if live(it, r, U, NT):
                        s = it * U + r
                        pe.wait_ge(s_at, s + 1)
                        wait(pe, s_y, s - 1)
                        for n in range(KT):
                            nc.tensor.matmul(po[r % 2][:, 0:D], at[:, r % 2, n * P:(n + 1) * P], wo[:, n, :],
                                             start=(n == 0), stop=False)
                        nc.tensor.matmul(po[r % 2][:, 0:D], k.ones[0:1, :], bo, start=False, stop=True).then_inc(s_o, 1)
                ticks(pe, NT, U, 1, body)


def feed_forward(nc, k, y, xr, wf1, bf1, wf2, bf2, beta):
    U = 4
    with ExitStack() as c:
        sb = lambda name, shape, dt=F32: c.enter_context(nc.sbuf_tensor(name, shape, dt))
        sem = lambda name: c.enter_context(nc.semaphore(name))
        z = sb("ff_z", [P, 2, D])
        zt = sb("ff_zt", [P, 2, D])
        g = k.acc[:, 0:2 * FF].rearrange("p (s f) -> p s f", s=2)
        pt = [c.enter_context(nc.psum_tensor(f"ff_t{n}", [P, 512], F32)) for n in range(2)]
        ph = [[c.enter_context(nc.psum_tensor(f"ff_h{n}{m}", [P, 512], F32)) for m in range(2)] for n in range(2)]
        po = [c.enter_context(nc.psum_tensor(f"ff_o{n}", [P, 512], F32)) for n in range(2)]
        s_z, s_t, s_zt, s_h, s_g, s_o, s_y, s_x = (sem("ff_sz"), sem("ff_st"), sem("ff_szt"), sem("ff_sh"), sem("ff_sg"),
                                                   sem("ff_so"), sem("ff_sy"), sem("ff_sx"))
        with nc.Block() as block:
            @block.scalar
            def _(act):
                def body(it, u):
                    t = it * U + u
                    if live(it, u, U, NT):
                        wait(act, s_t, t - 1)
                        nc.scalar.activation(z[:, u % 2, :], y[:, ds(t * D, D)], ACT.Identity, bias=k.nb[:, ds(t, 1)],
                                             scale=k.rs[:, ds(t, 1)]).then_inc(s_z, 1)
                    r = u - 1
                    if live(it, r, U, NT):
                        s = it * U + r
                        act.wait_ge(s_h, s + 1)
                        wait(act, s_o, s - 1)
                        for f in range(FT):
                            last = nc.scalar.activation(g[:, r % 2, f * P:(f + 1) * P],
                                                        ph[r % 2][f // 4][:, (f % 4) * P:(f % 4 + 1) * P], ACT.Gelu,
                                                        bias=bf1[:, f:f + 1])
                        last.then_inc(s_g, 1)
                ticks(act, NT, U, 1, body)

            @block.vector
            def _(dve):
                def body(it, u):
                    t = it * U + u
                    if live(it, u, U, NT):
                        dve.wait_ge(s_t, t + 1)
                        wait(dve, s_h, t - 1)
                        nc.vector.tensor_copy(zt[:, u % 2, :], pt[u % 2][:, 0:D]).then_inc(s_zt, 1)
                    r = u - 3
                    if live(it, r, U, NT):
                        s = it * U + r
                        dve.wait_ge(s_o, s + 1)
                        nc.vector.scalar_tensor_tensor(out=y[:, ds(s * D, D)], in0=po[r % 2][:, 0:D], scalar=beta,
                                                       in1=y[:, ds(s * D, D)], op0=ALU.mult, op1=ALU.add).then_inc(s_y, 1)
                        dve.wait_ge(s_y, s + 1)
                        nc.vector.tensor_tensor(xr[:, ds(s * D, D)], xr[:, ds(s * D, D)], y[:, ds(s * D, D)],
                                                ALU.add).then_inc(s_x, 1)
                ticks(dve, NT, U, 3, body)
                dve.wait_ge(s_x, NT)

            @block.tensor
            def _(pe):
                def body(it, u):
                    t = it * U + u
                    if live(it, u, U, NT):
                        pe.wait_ge(s_z, t + 1)
                        wait(pe, s_zt, t - 1)
                        for n in range(KT):
                            last = nc.tensor.transpose(pt[u % 2][:, n * P:(n + 1) * P], z[:, u % 2, n * P:(n + 1) * P],
                                                       k.ident[:, :])
                        last.then_inc(s_t, 1)
                    q = u - 2
                    if live(it, q, U, NT):
                        s = it * U + q
                        pe.wait_ge(s_g, s + 1)
                        wait(pe, s_y, s - 1)
                        for f in range(FT):
                            nc.tensor.matmul(po[q % 2][:, 0:D], g[:, q % 2, f * P:(f + 1) * P], wf2[:, f, :],
                                             start=(f == 0), stop=False)
                        nc.tensor.matmul(po[q % 2][:, 0:D], k.ones[0:1, :], bf2, start=False, stop=True).then_inc(s_o, 1)
                    r = u - 1
                    if live(it, r, U, NT):
                        s = it * U + r
                        pe.wait_ge(s_zt, s + 1)
                        wait(pe, s_g, s - 1)
                        for f in range(FT):
                            for n in range(KT):
                                last = nc.tensor.matmul(ph[r % 2][f // 4][:, (f % 4) * P:(f % 4 + 1) * P],
                                                        wf1[:, n, f * P:(f + 1) * P], zt[:, r % 2, n * P:(n + 1) * P],
                                                        start=(n == 0), stop=(n == KT - 1))
                        last.then_inc(s_h, 1)
                ticks(pe, NT, U, 2, body)


def layer3_rows(nc, k, y, rd, bias):
    with ExitStack() as c:
        a = c.enter_context(nc.sbuf_tensor("l3_a", [P, 2, D], F32))
        s_a, s_b, s_y = (c.enter_context(nc.semaphore(n)) for n in ("l3_sa", "l3_sb", "l3_sy"))
        with nc.Block() as block:
            @block.vector
            def _(dve):
                def body(it, u):
                    t = it * 4 + u
                    if live(it, u, 4, NT):
                        nc.vector.tensor_tensor(
                            a[:, u % 2, :].rearrange("p (h c) -> p h c", h=H),
                            k.acc[:, ds(t * AW, D)].rearrange("p (h c) -> p h c", h=H),
                            rd[:, ds(t * H, H)].unsqueeze(2).to_broadcast([P, H, C]), ALU.mult).then_inc(s_a, 1)
                        nc.vector.tensor_tensor(y[:, ds(t * D, D)], y[:, ds(t * D, D)], bias, ALU.add).then_inc(s_b, 1)
                    r = u - 1
                    if live(it, r, 4, NT):
                        s = it * 4 + r
                        dve.wait_ge(s_a, s + 1)
                        dve.wait_ge(s_b, s + 1)
                        nc.vector.tensor_tensor(y[:, ds(s * D, D)], y[:, ds(s * D, D)], a[:, r % 2, :],
                                                ALU.add).then_inc(s_y, 1)
                        dve.wait_ge(s_y, s + 1)
                ticks(dve, NT, 4, 1, body)


def final_output(nc, k, xr, y, gamma, beta, out):
    with ExitStack() as c:
        z = c.enter_context(nc.sbuf_tensor("fo_z", [P, 4, D], F32))
        sem = lambda n: c.enter_context(nc.semaphore(n))
        s_z, s_1, s_2, s_3, s_out = sem("fo_z_"), sem("fo_1"), sem("fo_2"), sem("fo_3"), [sem(f"fo_out{n}") for n in range(4)]
        with nc.Block() as block:
            @block.scalar
            def _(act):
                def body(it, u):
                    t = it * 4 + u
                    wait(act, s_out[u % 4], it * 16 if u < 4 else 0)
                    nc.scalar.activation(z[:, u % 4, :], y[:, ds(t * D, D)], ACT.Identity, bias=k.nb[:, ds(t, 1)],
                                         scale=k.rs[:, ds(t, 1)]).then_inc(s_z, 1)
                ticks(act, NT, 4, 0, body)

            @block.vector
            def _(dve):
                def body(it, u):
                    for lag, sem_in, sem_out in ((0, s_z, s_1), (1, s_1, s_2), (2, s_2, s_3)):
                        r = u - lag
                        if live(it, r, 4, NT):
                            s = it * 4 + r
                            dve.wait_ge(sem_in, s + 1)
                            zz = z[:, r % 4, :]
                            if lag == 0:
                                ins = nc.vector.tensor_tensor(zz, zz, gamma, ALU.mult)
                            elif lag == 1:
                                ins = nc.vector.tensor_tensor(zz, zz, beta, ALU.add)
                            else:
                                ins = nc.vector.tensor_tensor(zz, zz, xr[:, ds(s * D, D)], ALU.add)
                            ins.then_inc(sem_out, 1)
                ticks(dve, NT, 4, 2, body)

            @block.sync
            def _(sp):
                def body(it, u):
                    t = it * 4 + u
                    sp.wait_ge(s_3, t + 1)
                    if isinstance(t, int) and t == NT - 1:
                        sp.dma_start(out[t * P:N, :], z[0:LAST_ROWS, u % 4, :]).then_inc(s_out[u % 4], 16)
                    else:
                        sp.dma_start(out[ds(t * P, P), :], z[:, u % 4, :]).then_inc(s_out[u % 4], 16)
                ticks(sp, NT, 4, 0, body)
                for n in range(4):
                    sp.wait_ge(s_out[n], 16 * len(range(n, NT, 4)))


def denominators(nc, tag, k, rd):
    with nc.semaphore(f"{tag}_dn") as s_v, nc.Block() as block:
        @block.vector
        def _(dve):
            v = Chain(dve, s_v)
            r3 = rd.rearrange("p (t h) -> p t h", h=H)
            v(nc.vector.tensor_scalar(r3, k.acc[:, 0:NT * AW].rearrange("p (t w) -> p t w", w=AW)[:, :, D:AW], 1e-16,
                                      None, ALU.add))
            v(nc.vector.reciprocal(rd, rd))


def fold_attention(nc, name, tmp, jobs):
    with nc.semaphore(name) as s_v, nc.Block() as block:
        @block.vector
        def _(dve):
            v = Chain(dve, s_v)
            for w, att, out, heads in jobs:
                v(nc.vector.tensor_tensor(tmp, w, att, ALU.mult))
                v(nc.vector.tensor_reduce(out, tmp.rearrange("p (h c) -> p h c", h=heads), AX.X, ALU.add))


def gnn_kernel(nc, x, src, dst, edge_attr, edge_weight, w0, att_l, att_r, w1, wq, bq, wk, bk, wv, bv, we, be, wo, bo,
               ln1_g, ln1_b, ln2_g, ln2_b, wf1, bf1, wf2, bf2, alpha, beta, w3, we3, att_src, att_dst, att_edge,
               bias3, gamma3, beta3, out):
    flat = lambda a: a.rearrange("h c -> (h c)")
    table = lambda name, w: nc.dram_tensor(name, [NPAD, w], F32).ap()
    with ExitStack() as c:
        k = globals_of(nc, c)
        k.ae_dram = nc.dram_tensor("layer3_edge_part", [P, SEQ], F32)
        walk_tables(nc, k, src, dst, edge_weight)
        xr = c.enter_context(nc.sbuf_tensor("xr", [P, NT * D], F32))
        xrv = xr[:, :]

        t0, al0 = table("t0", D + H0), table("al0", H0)
        with ExitStack() as s:
            sb = lambda name, shape, dt=F32: s.enter_context(nc.sbuf_tensor(name, shape, dt))
            w0t = sb("w0t", [P, KT, D + 2 * H0])
            att = sb("att0", [P, 2, D])
            tmp = sb("tmp0", [P, D])
            with nc.semaphore("xpad") as s_p, nc.Block() as block:
                @block.gpsimd
                def _(pool):
                    nc.gpsimd.memset(xr[:, (NT - 1) * D:NT * D], 0.0).then_inc(s_p, 1)
                    pool.wait_ge(s_p, 1)
            whole = (NT - 1) * P
            load(nc, "ld0", [(xr[:, 0:(NT - 1) * D].rearrange("p (t d) -> p t d", d=D),
                              x[0:whole, :].rearrange("(t p) d -> p t d", p=P)),
                             (xr[0:LAST_ROWS, (NT - 1) * D:NT * D], x[whole:N, :]),
                             (w0t[:, :, 0:D], rows_of(w0)), (att[:, 0, :], spread(flat(att_r))),
                             (att[:, 1, :], spread(flat(att_l)))])
            fold_attention(nc, "fold0", tmp[:, :],
                           [(w0t[:, kt, 0:D], att[:, n, :], w0t[:, kt, D + n * H0:D + (n + 1) * H0], H0)
                            for kt in range(KT) for n in range(2)])
            row_stats(nc, "p1", k, xr[:, :].rearrange("p (t d) -> p t d", d=D))
            project(nc, "p2", k, xrv, ACT.Relu, [(w0t, None, D + 2 * H0, None, [(0, D + H0, t0), (D + H0, H0, al0)], None)])
        layer0_edges(nc, k, xrv, src, dst, t0, al0)

        t1 = table("t1", D)
        with ExitStack() as s:
            w1t = s.enter_context(nc.sbuf_tensor("w1t", [P, KT, D], F32))
            load(nc, "ld1", [(w1t[:, :, :], rows_of(w1))])
            row_stats(nc, "p3", k, xr[:, :].rearrange("p (t d) -> p t d", d=D))
            project(nc, "p4", k, xrv, ACT.Relu, [(w1t, None, D, k.dis, [(0, D, t1)], None)])
        aggregate(nc, "p5", k, t1, False)
        add_scaled(nc, k, xrv)
        recycle(nc)

        t_k, t_v = table("t_k", D), table("t_v", D)
        with ExitStack() as s:
            sb = lambda name, shape, dt=F32: s.enter_context(nc.sbuf_tensor(name, shape, dt))
            h2 = sb("h2", [P, NT * D])
            w = [sb(f"w2_{n}", [P, KT, D]) for n in range(3)]
            b = [sb(f"b2_{n}", [1, D]) for n in range(3)]
            gain, shift = sb("gain1", [P, KT]), sb("shift1", [P, KT])
            load(nc, "ld2", [(w[n][:, :, :], rows_of(a)) for n, a in enumerate((wq, wk, wv))] +
                 [(b[n][:, :], spread(a, 1)) for n, a in enumerate((bq, bk, bv))] +
                 [(gain[:, :], column(ln1_g)), (shift[:, :], column(ln1_b))])
            for n in range(3):
                fold_gain(nc, k, f"fg{n}", w[n], D, gain, shift, b[n][:, :], False)
            row_stats(nc, "p6", k, xr[:, :].rearrange("p (t d) -> p t d", d=D))
            normalized(nc, "p7", k, xrv, h2[:, :], ACT.Relu)
            row_stats(nc, "p8", k, h2[:, :].rearrange("p (t d) -> p t d", d=D))
            project(nc, "p9", k, h2[:, :], ACT.Identity,
                    [(w[0], b[0][0:1, :], D, None, [], k.acc[:, :]), (w[1], b[1][0:1, :], D, None, [(0, D, t_k)], None),
                     (w[2], b[2][0:1, :], D, None, [(0, D, t_v)], None)])
        with ExitStack() as s:
            sb = lambda name, shape, dt=F32: s.enter_context(nc.sbuf_tensor(name, shape, dt))
            k.edge = sb("edge2", [P, SEQ])
            with ExitStack() as s2:
                sb2 = lambda name, shape, dt=F32: s2.enter_context(nc.sbuf_tensor(name, shape, dt))
                k.ae = sb2("ae", [P, SEQ])
                wet = sb2("wet", [P, EW])
                we3t, atte, tmp = sb2("we3t", [ED, D]), sb2("atte", [ED, D]), sb2("tmp2", [ED, D])
                with nc.semaphore("wepad") as s_p, nc.Block() as block:
                    @block.gpsimd
                    def _(pool):
                        nc.gpsimd.memset(wet[:, :], 0.0).then_inc(s_p, 1)
                        pool.wait_ge(s_p, 1)
                load(nc, "ld2e", [(wet[0:ED, 0:C], we), (wet[ED:ED + 1, 0:C], spread(be, 1)), (we3t[:, :], we3),
                                  (atte[:, :], spread(flat(att_edge), ED))])
                fold_attention(nc, "fold2", tmp[:, :], [(we3t[:, :], atte[:, :], wet[0:ED, C:EW], H)])
                layer2_scores(nc, k, t_k, k.acc, wet[:, :], edge_attr)
                store(nc, "st_ae", k.ae_dram.ap(), k.ae[:, :])
            segment_softmax(nc, "p10", k, False)
            aggregate(nc, "p11", k, t_v, True)
        with ExitStack() as s:
            sb = lambda name, shape, dt=F32: s.enter_context(nc.sbuf_tensor(name, shape, dt))
            recycle(nc)
            y = sb("y2", [P, NT * D])
            wot, bot = sb("wot", [P, KT, D]), sb("bot", [1, D])
            wf1t, bf1t = sb("wf1t", [P, KT, FF]), sb("bf1t", [P, FT])
            wf2t, bf2t = sb("wf2t", [P, FT, D]), sb("bf2t", [1, D])
            gain, shift = sb("gain2", [P, KT]), sb("shift2", [P, KT])
            al_, be_ = sb("alpha_", [P, 1]), sb("beta_", [P, 1])
            rd = sb("rd2", [P, NT * H])
            load(nc, "ld3", [(wot[:, :, :], rows_of(wo)), (bot[:, :], spread(bo, 1)), (wf1t[:, :, :], rows_of(wf1)),
                             (bf1t[:, :], column(bf1)), (wf2t[:, :, :], rows_of(wf2, FT)), (bf2t[:, :], spread(bf2, 1)),
                             (gain[:, :], column(ln2_g)), (shift[:, :], column(ln2_b)), (al_[:, :], spread(alpha)),
                             (be_[:, :], spread(beta))])
            fold_gain(nc, k, "fgf", wf1t, FF, gain, shift, bf1t[:, :], True)
            denominators(nc, "p12", k, rd[:, :])
            row_stats(nc, "p13", k, xr[:, :].rearrange("p (t d) -> p t d", d=D))
            normalized(nc, "p14", k, xrv, y[:, :], ACT.Relu)
            attention_output(nc, k, y[:, :], wot, bot[0:1, :], al_[:, 0:1], rd[:, :])
            row_stats(nc, "p15", k, y[:, :].rearrange("p (t d) -> p t d", d=D))
            feed_forward(nc, k, y[:, :], xrv, wf1t, bf1t, wf2t, bf2t[0:1, :], be_[:, 0:1])

        recycle(nc)
        t_as, t_xp = table("t_as", H), table("t_xp", D)
        with ExitStack() as s:
            sb = lambda name, shape, dt=F32: s.enter_context(nc.sbuf_tensor(name, shape, dt))
            a_dst = sb("a_dst", [P, NT * H])
            with ExitStack() as s2:
                sb2 = lambda name, shape, dt=F32: s2.enter_context(nc.sbuf_tensor(name, shape, dt))
                w3t, w3d = sb2("w3t", [P, KT, AW]), sb2("w3d", [P, KT, H])
                att, tmp = sb2("att3", [P, 2, D]), sb2("tmp3", [P, D])
                load(nc, "ld4", [(w3t[:, :, 0:D], rows_of(w3)), (att[:, 0, :], spread(flat(att_src))),
                                 (att[:, 1, :], spread(flat(att_dst)))])
                fold_attention(nc, "fold3", tmp[:, :],
                               [(w3t[:, kt, 0:D], att[:, n, :], to[:, kt, -H:], H)
                                for kt in range(KT) for n, to in enumerate((w3t, w3d))])
                row_stats(nc, "p16", k, xr[:, :].rearrange("p (t d) -> p t d", d=D))
                project(nc, "p17", k, xrv, ACT.Relu, [(w3t, None, AW, None, [(0, D, t_xp), (D, H, t_as)], None),
                                               (w3d, None, H, None, [], a_dst[:, :])])
            k.edge = sb("edge3", [P, SEQ])
            layer3_logits(nc, k, t_as, a_dst)
            segment_softmax(nc, "p18", k, True)
            aggregate(nc, "p19", k, t_xp, True)
        with ExitStack() as s:
            sb = lambda name, shape, dt=F32: s.enter_context(nc.sbuf_tensor(name, shape, dt))
            y = sb("y3", [P, NT * D])
            b3, g3, be3 = sb("bias3t", [P, D]), sb("gamma3t", [P, D]), sb("beta3t", [P, D])
            rd = sb("rd3", [P, NT * H])
            load(nc, "ld5", [(b3[:, :], spread(bias3)), (g3[:, :], spread(gamma3)), (be3[:, :], spread(beta3))])
            denominators(nc, "p20", k, rd[:, :])
            row_stats(nc, "p21", k, xr[:, :].rearrange("p (t d) -> p t d", d=D))
            normalized(nc, "p22", k, xrv, y[:, :], ACT.Relu)
            layer3_rows(nc, k, y[:, :], rd[:, :], b3[:, :])
            row_stats(nc, "p23", k, y[:, :].rearrange("p (t d) -> p t d", d=D))
            final_output(nc, k, xrv, y[:, :], g3[:, :], be3[:, :], out)


_INS = ['x', 'src', 'dst', 'edge_attr_64', 'edge_weight', 'L0_gnn_weight', 'L0_gnn_attn_l', 'L0_gnn_attn_r',
        'L1_gnn_W', 'L2_gnn_Wq', 'L2_gnn_bq', 'L2_gnn_Wk', 'L2_gnn_bk', 'L2_gnn_Wv', 'L2_gnn_bv', 'L2_gnn_We',
        'L2_gnn_be', 'L2_gnn_Wo', 'L2_gnn_bo', 'L2_gnn_ln1_g', 'L2_gnn_ln1_b', 'L2_gnn_ln2_g', 'L2_gnn_ln2_b',
        'L2_gnn_W1', 'L2_gnn_b1', 'L2_gnn_W2', 'L2_gnn_b2', 'L2_gnn_alpha', 'L2_gnn_beta', 'L3_gnn_W', 'L3_gnn_W_e',
        'L3_gnn_att_src', 'L3_gnn_att_dst', 'L3_gnn_att_edge', 'L3_gnn_bias', 'L3_gnn_gamma', 'L3_gnn_beta']


def kernel(**inputs):
    import numpy as _np
    import concourse.bacc as _bacc
    from concourse import mybir as _mybir
    from concourse.bass_utils import run_bass_kernel_spmd as _run

    nc = _bacc.Bacc("TRN2", target_bir_lowering=False, num_devices=1)
    arrays, args = {}, []
    for name in _INS:
        a = _np.ascontiguousarray(inputs[name])
        arrays[f"in_{name}_dram"] = a
        args.append(nc.dram_tensor(f"in_{name}_dram", a.shape, _mybir.dt.from_np(a.dtype), kind="ExternalInput").ap())
    args.append(nc.dram_tensor("out_dram", (N, D), F32, kind="ExternalOutput").ap())
    gnn_kernel(nc, *args)
    r = _run(nc, [arrays], core_ids=[0])
    return r.results[0]["out_dram"]
```

```python
from contextlib import ExitStack

import numpy as np

import concourse.bass as bass
from concourse import mybir

P = 128
N, E, D, ED = 6250, 100000, 256, 64
NT = -(-N // P)
NPAD = NT * P
LAST_ROWS = N - (NT - 1) * P
ET = -(-E // P)
TAIL = E - (ET - 1) * P
UNROLL = 16
NS = -(-(ET + NT - 1) // UNROLL) * UNROLL
SB = -(-NS // P)
H, C = 8, D // 8
H0, C0 = 4, D // 4
C1 = C + 1
AW = H * C1
CH = P // H
CB = NS // CH
SEQ = CB * P
G = P // H
NG = NS // G
CF = 8
RW = P + 3
KT = D // P
FF = 4 * D
FT = FF // P
EW = 32 + H
EPS = 1e-5
BIG = 1e30
NOWHERE = 1 << 20

F32 = mybir.dt.float32
BF16 = mybir.dt.bfloat16
I32 = mybir.dt.int32
ALU = mybir.AluOpType
ACT = mybir.ActivationFunctionType
AX = mybir.AxisListType
ds = bass.ds


class Kept:
    pass


def wait(eng, sem, value):
    if not isinstance(value, int) or value > 0:
        eng.wait_ge(sem, value)


def ticks(eng, total, unroll, lag, body, peel=1):
    groups = total // unroll
    for it in range(peel):
        for u in range(unroll):
            body(it, u)
    with eng.Fori(peel, groups) as it:
        for u in range(unroll):
            body(it, u)
    for u in range(total - groups * unroll + lag):
        body(groups, u)


def live(it, c, unroll, total):
    return not isinstance(it, int) or 0 <= it * unroll + c < total


def fills(it, c, unroll, ring):
    return it * (unroll // ring) + c // ring + 1


class Chain:

    def __init__(self, eng, sem):
        self.eng, self.sem, self.n = eng, sem, 0

    def __call__(self, ins):
        self.n += 1
        ins.then_inc(self.sem, 1)
        self.eng.wait_ge(self.sem, self.n)


def walk_tables(nc, k, src, dst, ew):
    with ExitStack() as c:
        sb = lambda name, shape, dt=F32: c.enter_context(nc.sbuf_tensor(name, shape, dt))
        sem = lambda name: c.enter_context(nc.semaphore(name))
        pad_row = sb("pad_row", [2, 4 * P], I32)
        same_i = sb("same_i", [P, NS], I32)
        pad_key = sb("pad_key", [1, P])
        last_dst = sb("last_dst", [1, ET], I32)
        last_shr = sb("last_shr", [1, ET], I32)
        last_f = sb("last_f", [1, 2, ET])
        tile_i = sb("tile_i", [1, ET], I32)
        step_i = sb("step_i", [P, SB], I32)
        step_col = sb("step_col", [P, SB])
        node_i = sb("node_i", [P, NT], I32)
        node_col = sb("node_col", [P, NT])
        less = sb("less", [P, ET])
        i_col = sb("i_col", [P, SB])
        j_col = sb("j_col", [P, SB])
        base_col = sb("base_col", [P, SB])
        jbase = sb("jbase", [P, SB])
        i_idx = sb("i_idx", [P, SB], I32)
        ij_row = sb("ij_row", [SB, 2, P], I32)
        before = sb("before", [P, NT])
        before_idx = sb("before_idx", [P, NT], I32)
        lo = sb("lo", [P, NT])
        lo_row = sb("lo_row", [NT, P])
        lo_next = sb("lo_next", [NT, P])
        deg_row = sb("deg_row", [NT, P])
        end_row = sb("end_row", [1, P])
        rows = sb("rows", [P, 2, 4 * P], I32)
        nrows = sb("nrows", [P, 4, 4 * P], I32)
        ncmp = sb("ncmp", [P, P])
        rowf = sb("rowf", [P, 2, 5, P])
        d1 = sb("d1", [P, P])
        ge0 = sb("ge0", [P, P])
        valid = sb("valid", [P, P])
        pv = c.enter_context(nc.psum_tensor("pv", [P, 2, 2, 512], F32))
        pt = [c.enter_context(nc.psum_tensor(f"ptab{n}", [P, 4, P], F32)) for n in range(2)]

        s_pad, s_tail, s_last, s_tab, s_io = sem("pad"), sem("tail"), sem("last"), sem("tab"), sem("io")
        s_key0 = sem("padkey")
        s_ij, s_ijrow, s_ijback = sem("ij"), sem("ijrow"), sem("ijback")
        s_v, s_bcast, s_vec = sem("v"), sem("bcast"), sem("vec")
        s_idx = sem("idx")
        s_rowf, s_rowt, s_rowc, s_key = sem("rowf"), sem("rowt"), sem("rowc"), [sem(f"key{n}") for n in range(2)]
        s_bidx, s_ncnt = sem("bidx"), sem("ncnt")
        s_lo, s_lot, s_lor, s_lod, s_lon, s_degr, s_degt, s_deg = (
            sem("lo_"), sem("lot"), sem("lor"), sem("lod"), sem("lon"), sem("degr"), sem("degt"), sem("deg"))
        s_act = sem("actc")
        full = (ET - 1) * P
        HALF = ET // 2

        with nc.Block() as block:
            @block.sync
            def _(sp):
                tab = k.tab.ap()
                parts = [dst, src, ew.bitcast(I32), dst]
                for n, a in enumerate(parts):
                    sp.dma_start(tab[0:ET - 1, n * P:(n + 1) * P],
                                 a[0:full].rearrange("(i p) -> i p", p=P)).then_inc(s_tab, 16)
                    sp.dma_start(tab[ET - 1:ET, (n + 1) * P - TAIL:(n + 1) * P],
                                 a[full:E].rearrange("(i p) -> i p", i=1)).then_inc(s_tab, 16)
                sp.dma_start(last_dst[0:1, 0:ET - 1],
                             dst[0:full].rearrange("(i p) -> p i", p=P)[P - 1:P, :]).then_inc(s_last, 16)
                sp.dma_start(last_dst[0:1, ET - 1:ET],
                             dst[E - 1:E].rearrange("(a b) -> a b", a=1)).then_inc(s_last, 16)
                sp.wait_ge(s_pad, 4)
                for n in range(3):
                    sp.dma_start(tab[ET - 1:ET, n * P:(n + 1) * P - TAIL],
                                 pad_row[0:1, n * P:(n + 1) * P - TAIL]).then_inc(s_tab, 16)
                sp.dma_start(tab[ET - 1:ET, 3 * P:4 * P - TAIL].rearrange("a b -> b a"),
                             dst[full - 1:full].rearrange("(a b) -> a b", a=1).to_broadcast([P - TAIL, 1])
                             ).then_inc(s_tab, 16)
                sp.dma_start(tab[ET:ET + 1, :], pad_row[0:1, :]).then_inc(s_tab, 16)
                sp.dma_start(k.keys.ap()[0:P].rearrange("(a b) -> a b", a=1),
                             pad_key[:, :]).then_inc(s_key0, 16)
                sp.wait_ge(s_ijrow, 1)
                sp.dma_start(k.ij.ap().rearrange("a (b p) -> b a p", p=P), ij_row[:, :, :]).then_inc(s_ij, 16)
                sp.wait_ge(s_ij, 16)
                sp.dma_start(k.step_base[0:1, :], k.ij.ap()[0:1, 0:NS]).then_inc(s_ijback, 16)
                sp.dma_start(k.step_j[0:1, :], k.ij.ap()[1:2, 0:NS]).then_inc(s_ijback, 16)
                sp.dma_start(same_i[:, :], k.ij.ap()[1:2, 0:NS].to_broadcast([P, NS])).then_inc(s_ijback, 16)
                for b in range(SB):
                    sp.wait_ge(s_rowf, b + 1)
                    sp.dma_start(k.keys.ap()[P + b * P * P:P + (b + 1) * P * P].rearrange("(s e) -> s e", e=P),
                                 rowf[:, b % 2, 4, :]).then_inc(s_key[b % 2], 16)
                sp.wait_ge(s_lor, 2)
                sp.dma_start(k.lod.ap()[0:NPAD].rearrange("(t p) -> t p", p=P), lo_row[:, :]).then_inc(s_lod, 16)
                sp.dma_start(k.lod.ap()[NPAD:NPAD + P].rearrange("(t p) -> t p", p=P),
                             end_row[:, :]).then_inc(s_lod, 16)
                sp.wait_ge(s_lod, 32)
                sp.dma_start(lo_next[:, :], k.lod.ap()[1:NPAD + 1].rearrange("(t p) -> t p", p=P)).then_inc(s_lon, 16)
                sp.wait_ge(s_key0, 16)
                sp.wait_ge(s_ijback, 48)
                sp.wait_ge(s_key[0], 16 * ((SB + 1) // 2))
                sp.wait_ge(s_key[1], 16 * (SB // 2))

            @block.gpsimd
            def _(pool):
                nc.gpsimd.memset(pad_row[:, :], 0).then_inc(s_pad, 1)
                pool.wait_ge(s_pad, 1)
                nc.gpsimd.memset(pad_row[:, 0:P], NOWHERE)
                nc.gpsimd.memset(pad_row[:, 3 * P:4 * P], NOWHERE).then_inc(s_pad, 1)
                nc.gpsimd.memset(pad_key[:, :], -5.0).then_inc(s_pad, 1)
                nc.gpsimd.memset(end_row[:, :], float(E)).then_inc(s_pad, 1)
                nc.gpsimd.iota(tile_i[:, :], [[1, ET]], base=0, channel_multiplier=0).then_inc(s_io, 1)
                nc.gpsimd.iota(step_i[:, :], [[P, SB]], base=0, channel_multiplier=1).then_inc(s_io, 1)
                nc.gpsimd.iota(node_i[:, :], [[P, NT]], base=0, channel_multiplier=1).then_inc(s_io, 1)
                nc.gpsimd.iota(k.iota_i[:, :], [[1, P]], base=0, channel_multiplier=0).then_inc(s_io, 1)
                nc.gpsimd.memset(k.ident[:, :], 0.0).then_inc(s_io, 1)
                nc.gpsimd.memset(k.ones[:, :], 1.0).then_inc(s_io, 1)
                pool.wait_ge(s_io, 6)
                nc.gpsimd.affine_select(out=k.ident[:, :], in_=k.ident[:, :], compare_op=ALU.not_equal, fill=1.0,
                                        base=0, pattern=[[-1, P]], channel_multiplier=1).then_inc(s_io, 1)
                pool.wait_ge(s_tab, 16 * 13)
                pool.wait_ge(s_idx, 1)
                for b in range(SB):
                    if b >= 2:
                        pool.wait_ge(s_rowf, b - 1)
                    pool.indirect_dma_start(rows[:, b % 2, :], None, k.tab.ap(),
                                            bass.IndirectOffsetOnAxis(i_idx[:, b:b + 1], 0)).then_inc(k.got[b % 2], 16)
                pool.wait_ge(s_bidx, 1)
                for t in range(NT):
                    if t >= 4:
                        pool.wait_ge(s_ncnt, t - 3)
                    pool.indirect_dma_start(nrows[:, t % 4, :], None, k.tab.ap(),
                                            bass.IndirectOffsetOnAxis(before_idx[:, t:t + 1], 0)).then_inc(k.got[4 + t % 4], 16)

            @block.tensor
            def _(pe):
                pe.wait_ge(s_io, 7)
                pe.wait_ge(s_v, 1)
                for n in range(2):
                    for h in range(2):
                        last = nc.tensor.matmul(pv[:, n, h, 0:HALF], k.ones[0:1, :],
                                                last_f[0:1, n, h * HALF:(h + 1) * HALF], start=True, stop=True)
                last.then_inc(s_bcast, 1)
                pe.wait_ge(s_idx, 1)
                nc.tensor.transpose(pt[0][0:SB, 0, :], base_col[:, :], k.ident[:, :])
                nc.tensor.transpose(pt[0][0:SB, 1, :], j_col[:, :], k.ident[:, :]).then_inc(s_bcast, 1)
                pe.wait_ge(s_ijrow, 1)
                for b in range(SB):
                    pe.wait_ge(s_rowf, b + 1)
                    if b >= 2:
                        pe.wait_ge(s_rowc, b - 1)
                    for n in range(4):
                        last = nc.tensor.transpose(pt[b % 2][:, n, :], rowf[:, b % 2, n, :], k.ident[:, :])
                    last.then_inc(s_rowt, 1)
                pe.wait_ge(s_lo, 1)
                pe.wait_ge(s_rowc, SB)
                nc.tensor.transpose(pt[0][0:NT, 0, :], lo[:, :], k.ident[:, :]).then_inc(s_lot, 1)
                pe.wait_ge(s_degr, 1)
                nc.tensor.transpose(pt[1][:, 0, 0:NT], deg_row[:, :], k.ident[0:NT, 0:NT]).then_inc(s_degt, 1)

            @block.scalar
            def _(act):
                act.wait_ge(s_bcast, 2)
                nc.scalar.activation(ij_row[:, :, :], pt[0][0:SB, 0:2, :], ACT.Copy).then_inc(s_ijrow, 1)
                for b in range(SB):
                    act.wait_ge(s_rowt, b + 1)
                    w = min(P, NS - b * P)
                    for n, to in enumerate((k.drel, k.neg, k.weight, k.src)):
                        last = nc.scalar.activation(to[:, b * P:b * P + w], pt[b % 2][:, n, 0:w], ACT.Copy)
                    last.then_inc(s_rowc, 1)
                act.wait_ge(s_lot, 1)
                nc.scalar.activation(lo_row[:, :], pt[0][0:NT, 0, :], ACT.Copy).then_inc(s_lor, 1)
                act.wait_ge(s_pad, 4)
                act.sem_inc(s_lor, 1)
                act.wait_ge(s_degt, 1)
                nc.scalar.activation(k.deg[:, :], pt[1][:, 0, 0:NT], ACT.Copy).then_inc(s_deg, 1)

            @block.vector
            def _(dve):
                v = Chain(dve, s_vec)
                dve.wait_ge(s_io, 4)
                v(nc.vector.tensor_copy(k.iota[:, :], k.iota_i[:, :]))
                v(nc.vector.tensor_copy(step_col[:, :], step_i[:, :]))
                v(nc.vector.tensor_copy(node_col[:, :], node_i[:, :]))
                dve.wait_ge(s_last, 32)
                v(nc.vector.tensor_single_scalar(last_shr[:, :], last_dst[:, :], 7, op=ALU.logical_shift_right))
                v(nc.vector.tensor_copy(last_f[:, 0, :], last_shr[:, :]))
                v(nc.vector.tensor_copy(last_f[:, 1, :], tile_i[:, :]))
                v(nc.vector.tensor_tensor(last_f[:, 0, :], last_f[:, 0, :], last_f[:, 1, :], ALU.add))
                v(nc.vector.tensor_copy(last_f[:, 1, :], last_dst[:, :]))
                dve.sem_inc(s_v, 1)
                dve.wait_ge(s_bcast, 1)
                less2 = less[:, :].rearrange("p (h n) -> p h n", h=2)
                for b in range(SB):
                    v(nc.vector.tensor_scalar(less2, pv[:, 0, :, 0:HALF], step_col[:, b:b + 1], None, ALU.is_lt))
                    v(nc.vector.tensor_reduce(i_col[:, b:b + 1], less[:, :], AX.X, ALU.add))
                v(nc.vector.tensor_tensor(j_col[:, :], step_col[:, :], i_col[:, :], ALU.subtract))
                v(nc.vector.tensor_scalar_min(j_col[:, :], j_col[:, :], float(NT - 1)))
                v(nc.vector.tensor_scalar(base_col[:, :], i_col[:, :], float(P), float(E - P), ALU.mult, ALU.min))
                v(nc.vector.tensor_scalar(jbase[:, :], j_col[:, :], float(P), None, ALU.mult))
                v(nc.vector.tensor_copy(i_idx[:, :], i_col[:, :]))
                dve.sem_inc(s_idx, 1)
                for b in range(SB):
                    dve.wait_ge(k.got[b % 2], 16 * (b // 2 + 1))
                    if b >= 2:
                        dve.wait_ge(s_key[b % 2], 16 * (b // 2))
                        dve.wait_ge(s_rowt, b - 1)
                    r, f = rows[:, b % 2, :], rowf[:, b % 2, :, :]
                    v(nc.vector.tensor_scalar(f[:, 0, :], r[:, 0:P], jbase[:, b:b + 1], None, ALU.subtract))
                    v(nc.vector.tensor_scalar(ge0[:, :], f[:, 0, :], 0.0, None, ALU.is_ge))
                    v(nc.vector.scalar_tensor_tensor(out=valid[:, :], in0=f[:, 0, :], scalar=float(P), in1=ge0[:, :],
                                                     op0=ALU.is_lt, op1=ALU.mult))
                    v(nc.vector.tensor_scalar(f[:, 1, :], valid[:, :], BIG, -BIG, ALU.mult, ALU.add))
                    v(nc.vector.tensor_scalar(d1[:, :], r[:, 3 * P:4 * P], jbase[:, b:b + 1], None, ALU.subtract))
                    v(nc.vector.tensor_scalar(ge0[:, :], d1[:, :], 0.0, None, ALU.is_ge))
                    v(nc.vector.scalar_tensor_tensor(out=valid[:, :], in0=d1[:, :], scalar=float(P), in1=ge0[:, :],
                                                     op0=ALU.is_lt, op1=ALU.mult))
                    v(nc.vector.tensor_scalar(d1[:, :], r[:, 3 * P:4 * P], 1.0, None, ALU.add))
                    v(nc.vector.tensor_tensor(f[:, 4, :], d1[:, :], valid[:, :], ALU.mult))
                    v(nc.vector.tensor_scalar(f[:, 2, :], r[:, 2 * P:3 * P].bitcast(F32), float(C) ** -0.5, None, ALU.mult))
                    v(nc.vector.tensor_copy(f[:, 3, :], r[:, P:2 * P]))
                    dve.sem_inc(s_rowf, 1)
                dve.wait_ge(s_ijback, 48)
                v(nc.vector.tensor_tensor(k.same[:, 1:NS], same_i[:, 1:NS], same_i[:, 0:NS - 1], ALU.is_equal))
                v(nc.vector.memset(k.same[:, 0:1], 0.0))
                for t in range(NT):
                    v(nc.vector.tensor_scalar(less2, pv[:, 1, :, 0:HALF], node_col[:, t:t + 1], None, ALU.is_lt))
                    v(nc.vector.tensor_reduce(before[:, t:t + 1], less[:, :], AX.X, ALU.add))
                v(nc.vector.tensor_copy(before_idx[:, :], before[:, :]))
                dve.sem_inc(s_bidx, 1)
                for t in range(NT):
                    dve.wait_ge(k.got[4 + t % 4], 16 * (t // 4 + 1))
                    v(nc.vector.tensor_scalar(ncmp[:, :], nrows[:, t % 4, 0:P], node_col[:, t:t + 1], None, ALU.is_lt))
                    v(nc.vector.tensor_reduce(lo[:, t:t + 1], ncmp[:, :], AX.X, ALU.add))
                    dve.sem_inc(s_ncnt, 1)
                v(nc.vector.scalar_tensor_tensor(out=lo[:, :], in0=before[:, :], scalar=float(P), in1=lo[:, :],
                                                 op0=ALU.mult, op1=ALU.add))
                v(nc.vector.tensor_scalar_min(lo[:, :], lo[:, :], float(E)))
                dve.sem_inc(s_lo, 1)
                dve.wait_ge(s_lon, 16)
                v(nc.vector.tensor_tensor(deg_row[:, :], lo_next[:, :], lo_row[:, :], ALU.subtract))
                dve.sem_inc(s_degr, 1)
                dve.wait_ge(s_deg, 1)
                v(nc.vector.tensor_scalar_max(k.deg1[:, :], k.deg[:, :], 1.0))

    for n in range(2):
        k.seen[n] += 16 * len(range(n, SB, 2))
    for n in range(4):
        k.seen[4 + n] += 16 * len(range(n, NT, 4))
    with ExitStack() as c:
        s_sq, s_di = c.enter_context(nc.semaphore("sq")), c.enter_context(nc.semaphore("di"))
        with nc.Block() as block:
            @block.scalar
            def _(act):
                nc.scalar.activation(k.dis[:, :], k.deg1[:, :], ACT.Sqrt).then_inc(s_sq, 1)

            @block.vector
            def _(dve):
                v = Chain(dve, s_di)
                dve.wait_ge(s_sq, 1)
                v(nc.vector.reciprocal(k.dis[:, :], k.dis[:, :]))
                v(nc.vector.tensor_scalar_min(k.deg1[:, :], k.deg[:, :], 1.0))
                v(nc.vector.tensor_tensor(k.dis[:, :], k.dis[:, :], k.deg1[:, :], ALU.mult))


def globals_of(nc, c):
    sb = lambda name, shape, dt=F32: c.enter_context(nc.sbuf_tensor(name, shape, dt))
    c.enter_context(nc.allow_non_contiguous_dma(reason="a few small strided loads of indices and columns"))
    k = Kept()
    k.got = [c.enter_context(nc.semaphore(f"got{n}")) for n in range(8)]
    k.seen = [0] * 8
    k.tab = nc.dram_tensor("edge_rows", [ET + 1, 4 * P], I32)
    k.keys = nc.dram_tensor("keys", [P + SB * P * P], F32)
    k.runs = nc.dram_tensor("runs", [NS * H, RW], F32)
    k.ij = nc.dram_tensor("steps_ij", [2, SB * P], I32)
    k.lod = nc.dram_tensor("first_edge", [NPAD + P], F32)
    k.ident = sb("ident", [P, P])
    k.iota = sb("iota", [P, P])
    k.iota_i = sb("iota_i", [P, P], I32)
    k.ones = sb("ones", [1, P])
    k.drel = sb("drel", [P, NS])
    k.neg = sb("neg", [P, NS])
    k.weight = sb("weight", [P, NS])
    k.src = sb("srct", [P, NS], I32)
    k.same = sb("same", [P, NS])
    k.step_j = sb("step_j", [1, NS], I32)
    k.step_base = sb("step_base", [1, NS], I32)
    k.smask = sb("smask", [P, G])
    k.hmask = sb("hmask", [P, H])
    k.hmask_t = sb("hmask_t", [H, P])
    k.deg = sb("deg_", [P, NT])
    k.deg1 = sb("deg1", [P, NT])
    k.dis = sb("dis", [P, NT])
    k.eps = sb("eps", [P, 1])
    k.rs = sb("rs", [P, NT])
    k.nb = sb("nb", [P, NT])
    k.acc = sb("acc", [P, 2 * SEQ])
    return k


def row_stats(nc, tag, k, x):
    TG = 7
    with ExitStack() as c:
        sb = lambda name, shape, dt=F32: c.enter_context(nc.sbuf_tensor(f"{tag}_{name}", shape, dt))
        sem = lambda name: c.enter_context(nc.semaphore(f"{tag}_{name}"))
        st = sb("bn_st", [P, NT * 6])
        mv = sb("bn_mv", [P, NT, 2])
        s_vec, s_var, s_std = sem("rs_vec"), sem("rs_var"), sem("rs_std")
        with nc.Block() as block:
            @block.vector
            def _(dve):
                v = Chain(dve, s_vec)
                xf = x.rearrange("p t d -> p (t d)")
                with dve.Fori(0, NT // TG) as it:
                    for u in range(TG):
                        nc.vector.bn_stats(st[:, ds(it * (6 * TG) + 6 * u, 6)], xf[:, ds(it * (TG * D) + u * D, D)])
                dve.drain()
                v(nc.vector.memset(k.eps[:, :], EPS))
                for t in range(NT):
                    last = nc.vector.bn_aggr(mv[:, t, :], st[:, 6 * t:6 * t + 6])
                last.then_inc(s_var, 1)
                dve.wait_ge(s_std, 1)
                v(nc.vector.reciprocal(k.rs[:, :], k.rs[:, :]))
                v(nc.vector.scalar_tensor_tensor(out=k.nb[:, :], in0=mv[:, :, 0], scalar=-1.0, in1=k.rs[:, :],
                                                 op0=ALU.mult, op1=ALU.mult))

            @block.scalar
            def _(act):
                act.wait_ge(s_var, 1)
                nc.scalar.activation(k.rs[:, :], mv[:, :, 1], ACT.Sqrt, bias=k.eps[:, 0:1]).then_inc(s_std, 1)


def normalized(nc, tag, k, x, y, func):
    with nc.semaphore(f"{tag}_norm") as s_norm, nc.Block() as block:
        @block.scalar
        def _(act):
            def body(it, u):
                t = it * 7 + u
                nc.scalar.activation(y[:, ds(t * D, D)], x[:, ds(t * D, D)], func, bias=k.nb[:, ds(t, 1)],
                                     scale=k.rs[:, ds(t, 1)]).then_inc(s_norm, 1)
            ticks(act, NT, 7, 0, body)
            act.wait_ge(s_norm, NT)


def project(nc, tag, k, x, func, outs):
    U = 4
    nout = len(outs)
    PB = 2
    OB = 4
    with ExitStack() as c:
        sb = lambda name, shape, dt=F32: c.enter_context(nc.sbuf_tensor(f"{tag}_{name}", shape, dt))
        sem = lambda name: c.enter_context(nc.semaphore(f"{tag}_{name}"))
        z = sb("pj_z", [P, 2, D])
        zt = sb("pj_zt", [P, 2, D])
        pt = [c.enter_context(nc.psum_tensor(f"{tag}_pj_t{n}", [P, 512], F32)) for n in range(2)]
        po = [[c.enter_context(nc.psum_tensor(f"{tag}_pj_o{m}_{n}", [P, 512], F32)) for n in range(PB)] for m in range(nout)]
        ob = [sb(f"pj_b{m}", [P, OB, o[2]]) if o[5] is None else None for m, o in enumerate(outs)]
        s_z, s_t, s_zt, s_o, s_ev = sem("pj_sz"), sem("pj_st"), sem("pj_szt"), sem("pj_so"), sem("pj_ev")
        stored = [sem(f"pj_store{n}") for n in range(OB)]
        nst = sum(len(o[4]) for o in outs)
        with nc.Block() as block:
            @block.scalar
            def _(act):
                def body(it, u):
                    t = it * U + u
                    if live(it, u, U, NT):
                        wait(act, s_t, t - 1)
                        nc.scalar.activation(z[:, u % 2, :], x[:, ds(t * D, D)], func, bias=k.nb[:, ds(t, 1)],
                                             scale=k.rs[:, ds(t, 1)]).then_inc(s_z, 1)
                    r = u - 2
                    if live(it, r, U, NT):
                        s = it * U + r
                        act.wait_ge(s_o, s + 1)
                        if nst:
                            wait(act, stored[r % OB], (it + r // OB) * (16 * nst))
                        for m, (w, b, width, col, st, target) in enumerate(outs):
                            scale = 1.0 if col is None else col[:, ds(s, 1)]
                            o = ob[m][:, r % OB, :] if target is None else target[:, ds(s * width, width)]
                            last = nc.scalar.activation(o, po[m][r % PB][:, 0:width], ACT.Copy, scale=scale)
                        last.then_inc(s_ev, 1)
                ticks(act, NT, U, 2, body)
                act.wait_ge(s_ev, NT)

            @block.vector
            def _(dve):
                def body(it, u):
                    t = it * U + u
                    if live(it, u, U, NT):
                        dve.wait_ge(s_t, t + 1)
                        wait(dve, s_o, t - 1)
                        nc.vector.tensor_copy(zt[:, u % 2, :], pt[u % 2][:, 0:D]).then_inc(s_zt, 1)
                ticks(dve, NT, U, 0, body)

            @block.tensor
            def _(pe):
                def body(it, u):
                    t = it * U + u
                    if live(it, u, U, NT):
                        pe.wait_ge(s_z, t + 1)
                        wait(pe, s_zt, t - 1)
                        for n in range(KT):
                            last = nc.tensor.transpose(pt[u % 2][:, n * P:(n + 1) * P], z[:, u % 2, n * P:(n + 1) * P],
                                                       k.ident[:, :])
                        last.then_inc(s_t, 1)
                    r = u - 1
                    if live(it, r, U, NT):
                        s = it * U + r
                        pe.wait_ge(s_zt, s + 1)
                        wait(pe, s_ev, s - PB + 1)
                        for m, (w, b, width, col, st, target) in enumerate(outs):
                            o = po[m][r % PB][:, 0:width]
                            for n in range(KT):
                                last = nc.tensor.matmul(o, zt[:, r % 2, n * P:(n + 1) * P], w[:, n, :],
                                                        start=(n == 0), stop=(n == KT - 1 and b is None))
                            if b is not None:
                                last = nc.tensor.matmul(o, k.ones[0:1, :], b, start=False, stop=True)
                        last.then_inc(s_o, 1)
                ticks(pe, NT, U, 1, body)

            @block.sync
            def _(sp):
                def body(it, u):
                    t = it * U + u
                    if nst and live(it, u, U, NT):
                        sp.wait_ge(s_ev, t + 1)
                        for m, (w, b, width, col, st, target) in enumerate(outs):
                            for first, cols, table in st:
                                sp.dma_start(table[ds(t * P, P), :],
                                             ob[m][:, u % OB, first:first + cols]).then_inc(stored[u % OB], 16)
                if nst:
                    ticks(sp, NT, U, 0, body)
                    for n in range(OB):
                        sp.wait_ge(stored[n], 16 * nst * len(range(n, NT, OB)))


def aggregate(nc, tag, k, table, weights):
    R, W, LAG = 8, 4, 2
    width = AW if weights else D
    with ExitStack() as c:
        sb = lambda name, shape, dt=F32: c.enter_context(nc.sbuf_tensor(f"{tag}_{name}", shape, dt))
        sem = lambda name: c.enter_context(nc.semaphore(f"{tag}_{name}"))
        idx = sb("ag_idx", [P, 2, UNROLL // 2], I32)
        got = sb("ag_got", [P, R, width])
        sel = sb("ag_sel", [P, W, P])
        wgt = sb("ag_wgt", [P, W, AW]) if weights else None
        cur = sb("ag_cur", [P, W, AW])
        pa = [c.enter_context(nc.psum_tensor(f"{tag}_ag_p{n}", [P, 512], F32)) for n in range(W)]
        s_idx, s_turn, s_got = sem("ag_si"), sem("ag_turn"), k.got
        s_rhs, s_mm, s_cur, s_acc, s_init = (sem("ag_rhs"), sem("ag_mm"), sem("ag_scur"), sem("ag_acc"),
                                             sem("ag_init"))
        s_used = s_rhs if weights else s_mm
        with nc.Block() as block:
            @block.gpsimd
            def _(pool):
                half = UNROLL // 2

                def body(it, u):
                    t = it * UNROLL + u
                    if u % half == 0:
                        h = u // half
                        nc.gpsimd.tensor_copy(idx[:, h, :], k.src[:, ds(t, half)]).then_inc(s_idx, 1)
                        pool.wait_ge(s_idx, it * 2 + h + 1)
                    wait(pool, s_used, t - R + 1)
                    pool.sem_inc(s_turn, 1)
                    pool.indirect_dma_start(got[:, u % R, :], None, table,
                                            bass.IndirectOffsetOnAxis(idx[:, u // half, u % half:u % half + 1], 0)
                                            ).then_inc(s_got[u % R], 16)
                ticks(pool, NS, UNROLL, 0, body)

            @block.vector
            def _(dve):
                for n in range(W):
                    last = nc.vector.memset(cur[:, n, :], 0.0)
                last.then_inc(s_init, 1)
                dve.wait_ge(s_init, 1)

                def body(it, u):
                    t = it * UNROLL + u
                    if live(it, u, UNROLL, NS):
                        wait(dve, s_mm, t - W + 1)
                        last = nc.vector.tensor_scalar(sel[:, u % W, :], k.iota[:, :], k.drel[:, ds(t, 1)], None,
                                                       ALU.is_equal)
                        if weights:
                            dve.wait_ge(s_got[u % R], 16 * fills(it, u, UNROLL, R) + k.seen[u % R])
                            last = nc.vector.tensor_tensor(
                                wgt[:, u % W, :].rearrange("p (h c) -> p h c", h=H),
                                got[:, u % R, :].rearrange("p (h c) -> p h c", h=H),
                                k.edge[:, ds(t * H, H)].unsqueeze(2).to_broadcast([P, H, C1]), ALU.mult)
                        last.then_inc(s_rhs, 1)
                    r = u - LAG
                    if live(it, r, UNROLL, NS):
                        s = it * UNROLL + r
                        dve.wait_ge(s_mm, s + 1)
                        wait(dve, s_cur, s)
                        wait(dve, s_acc, s - W + 1)
                        nc.vector.scalar_tensor_tensor(
                            out=cur[:, r % W, 0:width], in0=cur[:, (r - 1) % W, 0:width], scalar=k.same[:, ds(s, 1)],
                            in1=pa[r % W][:, 0:width], op0=ALU.mult, op1=ALU.add).then_inc(s_cur, 1)
                ticks(dve, NS, UNROLL, LAG, body)

            @block.tensor
            def _(pe):
                def body(it, u):
                    t = it * UNROLL + u
                    pe.wait_ge(s_rhs, t + 1)
                    wait(pe, s_cur, t - W + 1)
                    if weights:
                        nc.tensor.matmul(pa[u % W][:, 0:AW], sel[:, u % W, :], wgt[:, u % W, :],
                                         start=True, stop=True).then_inc(s_mm, 1)
                    else:
                        pe.wait_ge(s_got[u % R], 16 * fills(it, u, UNROLL, R) + k.seen[u % R])
                        nc.tensor.matmul(pa[u % W][:, 0:D], sel[:, u % W, :], got[:, u % R, :],
                                         start=True, stop=True).then_inc(s_mm, 1)
                ticks(pe, NS, UNROLL, 0, body)

            @block.scalar
            def _(act):
                def body(it, u):
                    s = it * UNROLL + u
                    if u % 4 == 0:
                        _, act_j[0] = nc.values_load_multi_w_load_instructions(
                            k.step_j[0:1, ds(s, 4)], engines=(mybir.EngineType.Activation,), min_val=0, max_val=NT - 1,
                            skip_runtime_bounds_check_because="j(s) is clamped to the last node tile")
                    act.wait_ge(s_cur, s + 1)
                    wait(act, s_acc, s)
                    nc.scalar.activation(k.acc[:, ds(act_j[0][u % 4] * AW, width)], cur[:, u % W, 0:width],
                                         ACT.Copy).then_inc(s_acc, 1)
                act_j = [None]
                ticks(act, NS, UNROLL, 0, body)
                act.wait_ge(s_acc, NS)
    for n in range(R):
        k.seen[n] += 16 * (NS // R)


def layer0_edges(nc, k, xr, src, dst, t0, al0):
    TG = 7
    W0 = D + H0
    with ExitStack() as c:
        sb = lambda name, shape, dt=F32: c.enter_context(nc.sbuf_tensor(name, shape, dt))
        sem = lambda name: c.enter_context(nc.semaphore(name))
        er = sb("l0_er", [NT, 2, P], I32)
        erf = sb("l0_erf", [NT, 2, P])
        ei = sb("l0_ei", [P, 2, NT], I32)
        al = sb("l0_al", [P, NT, H0])
        lg = sb("l0_lg", [P, NT, H0])
        mx = sb("l0_mx", [P, NT])
        tmp = sb("l0_tmp", [P, TG, C0])
        got = k.acc[:, 0:NT * W0].rearrange("p (t w) -> p t w", w=W0)
        pt = c.enter_context(nc.psum_tensor("l0_pt", [P, 2, P], F32))
        s_ld, s_f, s_t, s_i = sem("l0_ld"), sem("l0_sf"), sem("l0_st"), sem("l0_si")
        s_al, s_got, s_ex, s_v, s_lg = k.got[NT // TG], k.got[0:NT // TG], sem("l0_ex"), sem("l0_v"), sem("l0_slg")
        with nc.Block() as block:
            @block.sync
            def _(sp):
                for n, a in enumerate((src, dst)):
                    sp.dma_start(er[:, n, :], a[0:NPAD].rearrange("(t p) -> t p", p=P)).then_inc(s_ld, 16)

            @block.tensor
            def _(pe):
                pe.wait_ge(s_f, 1)
                nc.tensor.transpose(pt[:, 0, 0:NT], erf[:, 0, :], k.ident[0:NT, 0:NT])
                nc.tensor.transpose(pt[:, 1, 0:NT], erf[:, 1, :], k.ident[0:NT, 0:NT]).then_inc(s_t, 1)

            @block.gpsimd
            def _(pool):
                pool.wait_ge(s_i, 1)
                for t in range(NT):
                    pool.indirect_dma_start(al[:, t, :], None, al0, bass.IndirectOffsetOnAxis(ei[:, 0, t:t + 1], 0)
                                            ).then_inc(s_al, 16)
                    pool.indirect_dma_start(got[:, t, :], None, t0, bass.IndirectOffsetOnAxis(ei[:, 1, t:t + 1], 0)
                                            ).then_inc(s_got[t // TG], 16)

            @block.scalar
            def _(act):
                act.wait_ge(s_lg, 1)
                nc.scalar.activation(lg[:, :, :], lg[:, :, :], ACT.Exp).then_inc(s_ex, 1)

            @block.vector
            def _(dve):
                v = Chain(dve, s_v)
                dve.wait_ge(s_ld, 32)
                v(nc.vector.tensor_copy(erf[:, :, :], er[:, :, :]))
                dve.sem_inc(s_f, 1)
                dve.wait_ge(s_t, 1)
                v(nc.vector.tensor_copy(ei[:, :, :], pt[:, :, 0:NT]))
                dve.sem_inc(s_i, 1)
                dve.wait_ge(s_al, k.seen[NT // TG] + 16 * NT)
                for g in range(NT // TG):
                    dve.wait_ge(s_got[g], k.seen[g] + 16 * TG)
                bc = lambda a: a.unsqueeze(2).to_broadcast([P, NT, H0])
                v(nc.vector.tensor_tensor(lg[:, :, :], al[:, :, :], got[:, :, D:W0], ALU.add))
                v(nc.vector.scalar_tensor_tensor(out=lg[:, :, :], in0=lg[:, :, :], scalar=0.01, in1=lg[:, :, :],
                                                 op0=ALU.mult, op1=ALU.max))
                v(nc.vector.tensor_reduce(mx[:, :], lg[:, :, :], AX.X, ALU.max))
                v(nc.vector.tensor_tensor(lg[:, :, :], lg[:, :, :], bc(mx[:, :]), ALU.subtract))
                dve.sem_inc(s_lg, 1)
                dve.wait_ge(s_ex, 1)
                v(nc.vector.tensor_reduce(mx[:, :], lg[:, :, :], AX.X, ALU.add))
                v(nc.vector.reciprocal(mx[:, :], mx[:, :]))
                v(nc.vector.tensor_tensor(lg[:, :, :], lg[:, :, :], bc(mx[:, :]), ALU.mult))
                for g in range(NT // TG):
                    ts = slice(g * TG, (g + 1) * TG)
                    rows = got[:, ts, 0:D].rearrange("p t (h d) -> p t h d", h=H0)
                    v(nc.vector.tensor_tensor(rows, rows, lg[:, ts, :].unsqueeze(3).to_broadcast([P, TG, H0, C0]), ALU.mult))
                    v(nc.vector.tensor_reduce(tmp[:, :, :], got[:, ts, 0:D].rearrange("p t (h d) -> p t d h", h=H0),
                                              AX.X, ALU.add))
                    xv = xr[:, g * TG * D:(g + 1) * TG * D].rearrange("p (t h d) -> p t h d", t=TG, h=H0)
                    v(nc.vector.tensor_tensor(xv, xv, tmp[:, :, :].unsqueeze(2).to_broadcast([P, TG, H0, C0]), ALU.add))
    for g in range(NT // TG):
        k.seen[g] += 16 * TG
    k.seen[NT // TG] += 16 * NT


def add_scaled(nc, k, xr):
    with nc.semaphore("as_v") as s_v, nc.Block() as block:
        @block.vector
        def _(dve):
            def body(it, u):
                t = it * 7 + u
                nc.vector.scalar_tensor_tensor(out=xr[:, ds(t * D, D)], in0=k.acc[:, ds(t * AW, D)],
                                               scalar=k.dis[:, ds(t, 1)], in1=xr[:, ds(t * D, D)],
                                               op0=ALU.mult, op1=ALU.add).then_inc(s_v, 1)
            ticks(dve, NT, 7, 0, body)
            dve.wait_ge(s_v, NT)


def layer2_scores(nc, k, keys, queries, we, ef):
    R, W, EB = 8, 4, 4
    with ExitStack() as c:
        sb = lambda name, shape, dt=F32: c.enter_context(nc.sbuf_tensor(name, shape, dt))
        sem = lambda name: c.enter_context(nc.semaphore(name))
        half = UNROLL // 2
        idx = sb("sc_idx", [P, 2, half], I32)
        got = sb("sc_got", [P, R, D])
        sel = sb("sc_sel", [P, W, P])
        efr = sb("sc_ef", [P, EB, P])
        tr = sb("sc_tr", [P, 2, 2 * P])
        prod = sb("sc_prod", [P, W, D])
        epr = sb("sc_ep", [P, W, C])
        pt = [c.enter_context(nc.psum_tensor(f"sc_t{n}", [P, 512], F32)) for n in range(2)]
        pq = [c.enter_context(nc.psum_tensor(f"sc_q{n}", [P, 512], F32)) for n in range(W)]
        pw = [c.enter_context(nc.psum_tensor(f"sc_w{n}", [P, 512], F32)) for n in range(2)]
        s_idx, s_turn, s_got, s_ef = sem("sc_idx_"), sem("sc_turn"), k.got, [sem(f"sc_efs{n}") for n in range(EB)]
        s_init, s_sel, s_tr, s_cp, s_q, s_key, s_prod, s_sc, s_ae = (
            sem("sc_init"), sem("sc_ssel"), sem("sc_str"), sem("sc_cp"), sem("sc_sq"), sem("sc_key"),
            sem("sc_sprod"), sem("sc_sc"), sem("sc_ae"))
        with nc.Block() as block:
            @block.gpsimd
            def _(pool):
                nc.gpsimd.memset(efr[:, :, :], 0.0).then_inc(s_init, 1)
                pool.wait_ge(s_init, 1)
                nc.gpsimd.memset(efr[:, :, ED:ED + 1], 1.0).then_inc(s_init, 1)

                def body(it, u):
                    t = it * UNROLL + u
                    if u % half == 0:
                        h = u // half
                        nc.gpsimd.tensor_copy(idx[:, h, :], k.src[:, ds(t, half)]).then_inc(s_idx, 1)
                        pool.wait_ge(s_idx, it * 2 + h + 1)
                    wait(pool, s_key, t - R + 1)
                    pool.sem_inc(s_turn, 1)
                    pool.indirect_dma_start(got[:, u % R, :], None, keys,
                                            bass.IndirectOffsetOnAxis(idx[:, u // half, u % half:u % half + 1], 0)
                                            ).then_inc(s_got[u % R], 16)
                ticks(pool, NS, UNROLL, 0, body)

            @block.sync
            def _(sp):
                base = [None]
                sp.wait_ge(s_init, 2)

                def body(it, u):
                    t = it * UNROLL + u
                    if u % 4 == 0:
                        _, base[0] = nc.values_load_multi_w_load_instructions(
                            k.step_base[0:1, ds(t, 4)], engines=(mybir.EngineType.SP,), min_val=0, max_val=E - P,
                            skip_runtime_bounds_check_because="the first edge of a tile is clamped to E - P")
                    wait(sp, s_tr, t - EB + 1)
                    sp.dma_start(efr[:, u % EB, 0:ED], ef[ds(base[0][u % 4], P), :]).then_inc(s_ef[u % EB], 16)
                ticks(sp, NS, UNROLL, 0, body)

            @block.vector
            def _(dve):
                heads = lambda a: a.rearrange("p (h c) -> p h c", h=H)

                def body(it, u):
                    t = it * UNROLL + u
                    if live(it, u, UNROLL, NS):
                        wait(dve, s_tr, t - W + 1)
                        nc.vector.tensor_scalar(sel[:, u % W, :], k.iota[:, :], k.drel[:, ds(t, 1)], None,
                                                ALU.is_equal).then_inc(s_sel, 1)
                    a = u - 3
                    if live(it, a, UNROLL, NS):
                        s = it * UNROLL + a
                        dve.wait_ge(s_ae, s + 1)
                        dve.wait_ge(s_got[a % R], 16 * fills(it, a, UNROLL, R) + k.seen[a % R])
                        wait(dve, s_sc, s - W + 1)
                        nc.vector.tensor_tensor(
                            heads(prod[:, a % W, :]), heads(got[:, a % R, :]),
                            epr[:, a % W, :].unsqueeze(1).to_broadcast([P, H, C]), ALU.add).then_inc(s_key, 1)
                    b = u - 4
                    if live(it, b, UNROLL, NS):
                        s = it * UNROLL + b
                        dve.wait_ge(s_key, s + 1)
                        dve.wait_ge(s_q, s + 1)
                        nc.vector.tensor_tensor(prod[:, b % W, :], prod[:, b % W, :], pq[b % W][:, 0:D],
                                                ALU.mult).then_inc(s_prod, 1)
                    e = u - 5
                    if live(it, e, UNROLL, NS):
                        s = it * UNROLL + e
                        dve.wait_ge(s_prod, s + 1)
                        nc.vector.tensor_reduce(k.edge[:, ds(s * H, H)], heads(prod[:, e % W, :]), AX.X,
                                                ALU.add).then_inc(s_sc, 1)
                ticks(dve, NS, UNROLL, 5, body)
                dve.wait_ge(s_sc, NS)

            @block.tensor
            def _(pe):
                j = [None]

                def body(it, u):
                    t = it * UNROLL + u
                    if live(it, u, UNROLL, NS):
                        pe.wait_ge(s_sel, t + 1)
                        pe.wait_ge(s_ef[u % EB], 16 * fills(it, u, UNROLL, EB))
                        wait(pe, s_cp, t - 1)
                        nc.tensor.transpose(pt[u % 2][:, 0:P], sel[:, u % W, :], k.ident[:, :])
                        nc.tensor.transpose(pt[u % 2][:, P:2 * P], efr[:, u % EB, :], k.ident[:, :]).then_inc(s_tr, 1)
                    r = u - 1
                    if live(it, r, UNROLL, NS):
                        s = it * UNROLL + r
                        if r % 4 == 0 or j[0] is None or (u == 0):
                            first = s - r % 4
                            _, j[0] = nc.values_load_multi_w_load_instructions(
                                k.step_j[0:1, ds(first, 4)], engines=(mybir.EngineType.PE,), min_val=0, max_val=NT - 1,
                                skip_runtime_bounds_check_because="j(s) is clamped to the last node tile")
                        pe.wait_ge(s_cp, s + 1)
                        wait(pe, s_prod, s - W + 1)
                        wait(pe, s_ae, s - 1)
                        nc.tensor.matmul(pq[r % W][:, 0:D], tr[:, r % 2, 0:P], queries[:, ds(j[0][r % 4] * D, D)],
                                         start=True, stop=True)
                        nc.tensor.matmul(pw[r % 2][:, 0:EW], tr[:, r % 2, P:2 * P], we, start=True,
                                         stop=True).then_inc(s_q, 1)
                ticks(pe, NS, UNROLL, 1, body)

            @block.scalar
            def _(act):
                def body(it, u):
                    t = it * UNROLL + u
                    if live(it, u, UNROLL, NS):
                        act.wait_ge(s_tr, t + 1)
                        wait(act, s_q, t - 1)
                        nc.scalar.activation(tr[:, u % 2, :], pt[u % 2][:, 0:2 * P], ACT.Copy).then_inc(s_cp, 1)
                    r = u - 2
                    if live(it, r, UNROLL, NS):
                        s = it * UNROLL + r
                        act.wait_ge(s_q, s + 1)
                        wait(act, s_key, s - W + 1)
                        nc.scalar.activation(k.ae[:, ds(s * H, H)], pw[r % 2][:, C:EW], ACT.Copy)
                        nc.scalar.activation(epr[:, r % W, :], pw[r % 2][:, 0:C], ACT.Copy).then_inc(s_ae, 1)
                ticks(act, NS, UNROLL, 2, body)
                act.wait_ge(s_ae, NS)
    for n in range(R):
        k.seen[n] += 16 * (NS // R)


def run_flags(nc, k):
    R, S = NS // CF, CF
    with ExitStack() as c:
        sb = lambda name, shape, dt=F32: c.enter_context(nc.sbuf_tensor(name, shape, dt))
        keys = [sb(f"rf_k{n}", [R, S, P]) for n in range(3)]
        flags = sb("rf_f", [R, S, RW])
        s_ld, s_v, s_st = (c.enter_context(nc.semaphore(n)) for n in ("rf_ld", "rf_v", "rf_st"))
        with nc.Block() as block:
            @block.vector
            def _(dve):
                v = Chain(dve, s_v)
                v(nc.vector.tensor_reduce(k.smask[:, :], k.ident[:, :].rearrange("p (s h) -> p s h", h=H), AX.X, ALU.add))
                v(nc.vector.tensor_reduce(k.hmask[:, :], k.ident[:, :].rearrange("p (s h) -> p h s", h=H), AX.X, ALU.add))
                v(nc.vector.tensor_copy(k.hmask_t[:, :].rearrange("p (s h) -> p s h", h=H),
                                        k.ident[0:H, 0:H].unsqueeze(1).to_broadcast([H, G, H])))
                dve.wait_ge(s_ld, 48)
                own, later = flags[:, :, 0:P], keys[2][:, :, :]
                v(nc.vector.tensor_tensor(own, keys[1][:, :, :], keys[0][:, :, :], ALU.not_equal))
                v(nc.vector.tensor_tensor(later, keys[2][:, :, :], keys[1][:, :, :], ALU.not_equal))
                v(nc.vector.tensor_scalar(own, own, -BIG, None, ALU.mult))
                v(nc.vector.tensor_scalar(later, later, -BIG, None, ALU.mult))
                v(nc.vector.tensor_copy(flags[:, :, P:P + 1], keys[2][:, :, P - 1:P]))
                v(nc.vector.tensor_reduce(flags[:, :, P + 1], own, AX.X, ALU.min))
                v(nc.vector.tensor_reduce(flags[:, :, P + 2], later, AX.X, ALU.min))

            @block.sync
            def _(sp):
                for n in range(3):
                    sp.dma_start(keys[n][:, :, :], k.keys.ap()[P - 1 + n:P - 1 + n + NS * P]
                                 .rearrange("(r s e) -> r s e", r=R, s=S)).then_inc(s_ld, 16)
                sp.wait_ge(s_v, 10)
                for h in range(H):
                    sp.dma_start(k.runs.ap().rearrange("(r s h) n -> r s h n", s=S, h=H)[:, :, h, :],
                                 flags[:, :, :]).then_inc(s_st, 16)
                sp.wait_ge(s_st, 16 * H)


def layer3_edges(nc, k, table, a_dst):
    U, LAG = 2 * G, 2
    FW = G * H
    half = 8
    with ExitStack() as c:
        sb = lambda name, shape, dt=F32: c.enter_context(nc.sbuf_tensor(name, shape, dt))
        sem = lambda name: c.enter_context(nc.semaphore(name))
        idx = sb("le_idx", [P, U // half, half], I32)
        got = sb("le_got", [P, U, AW])
        sel = sb("le_sel", [P, U, P])
        tr = sb("le_tr", [P, 2, 4 * P], BF16)
        ae = sb("le_ae", [P, 2, FW])
        flags = sb("le_flags", [P, 2, RW])
        lg = sb("le_lg", [P, FW])
        ex = sb("le_ex", [P, 2, FW])
        part = sb("le_part", [P, 2 * P])
        run = sb("le_run", [P, P])
        mx = sb("le_mx", [P, P])
        cols = sb("le_cols", [P, 4, G])
        heads = sb("le_heads", [H, 4, G])
        chain = sb("le_chain", [H, 2, 2, G + 1])
        ini = sb("le_ini", [P, 2, G])
        init = sb("le_init", [P, 2])
        rise = sb("le_rise", [H, 1])
        drop = sb("le_drop", [H, P])
        drop_row = sb("le_droprow", [1, H])
        fac_row = sb("le_facrow", [1, H])
        fac = sb("le_fac", [P, H])
        wgt = sb("le_wgt", [P, 2, AW])
        cur = sb("le_cur", [P, 4, AW])
        scaled = sb("le_scaled", [P, AW])
        ps = lambda name: c.enter_context(nc.psum_tensor(name, [P, 512], F32))
        pa = [ps(f"le_pa{n}") for n in range(4)]
        pt, pq, pb, px = ps("le_pt"), ps("le_pq"), ps("le_pb"), ps("le_px")
        s_idx, s_turn, s_got = sem("le_sidx"), sem("le_turn"), k.got[0:2]
        s_sel, s_tr, s_cp, s_q = sem("le_ssel"), sem("le_str"), sem("le_scp"), sem("le_sq")
        s_stat, s_pe, s_ex, s_f = sem("le_stat"), sem("le_spe"), sem("le_sex"), sem("le_sf")
        s_rhs, s_mm, s_cur, s_acc, s_init = sem("le_rhs"), sem("le_mm"), sem("le_scur"), sem("le_acc"), sem("le_sinit")
        s_scaled = sem("le_sscaled")
        s_ld = [sem(f"le_ld{n}") for n in range(2)]
        STATS = ["add_src", "add_edge", "cols_f", "ones", "leaky", "mask", "scan", "scan_b", "cols", "heads", "carry",
                 "chain", "chain_b", "ini", "init", "run", "whole", "rise", "drop", "subtract", "fac_row", "fac"]
        MOVES = ["logits", "tails", "starts", "maxima", "drop", "factor"]
        stat = lambda b, name: b * len(STATS) + STATS.index(name) + 1
        move = lambda b, name: b * len(MOVES) + MOVES.index(name) + 1
        per_step = lambda a: a.rearrange("p (s h) -> p s h", h=H)
        rev = lambda a: a[:, ::-1]

        def group(it, u, tick, back):
            b, n = it * 2 + u // G - back, u // G - back
            if u % G != tick or not (not isinstance(it, int) or 0 <= b < NG):
                return None
            return b, n % 2, it + n // 2

        with nc.Block() as block:
            @block.sync
            def _(sp):
                def body(it, u):
                    if g := group(it, u, 0, 0):
                        b, par, pair = g
                        wait(sp, s_stat, stat(b - 2, "whole"))
                        sp.dma_start(ae[:, par, :], k.ae_dram.ap()[:, ds(b * FW, FW)]).then_inc(s_ld[par], 16)
                        sp.dma_start(flags[:, par, 0:RW], k.runs.ap()[ds(b * FW, FW), :]).then_inc(s_ld[par], 16)
                ticks(sp, NS, U, 0, body, 2)
                for n in range(2):
                    sp.wait_ge(s_ld[n], 32 * (NG // 2))

            @block.gpsimd
            def _(pool):
                def body(it, u):
                    t = it * U + u
                    if u % half == 0:
                        h = u // half
                        if u % G == 0:
                            wait(pool, s_stat, stat(it * 2 + u // G - 2, "add_src"))
                        nc.gpsimd.tensor_copy(idx[:, h, :], k.src[:, ds(t, half)]).then_inc(s_idx, 1)
                        pool.wait_ge(s_idx, it * (U // half) + h + 1)
                    wait(pool, s_rhs, t - U + 1)
                    pool.sem_inc(s_turn, 1)
                    pool.indirect_dma_start(got[:, u, :], None, table,
                                            bass.IndirectOffsetOnAxis(idx[:, u // half, u % half:u % half + 1], 0)
                                            ).then_inc(s_got[u // G], 16)
                ticks(pool, NS, U, 0, body, 2)

            @block.vector
            def _(dve):
                for n in range(4):
                    nc.vector.memset(cur[:, n, :], 0.0)
                nc.vector.memset(chain[:, :, :, :], -BIG).then_inc(s_init, 1)
                dve.wait_ge(s_init, 1)

                def maxima(it, u, slot):
                    now = lambda tick, at, back=1: slot == at and group(it, u, tick, back)
                    own = lambda b, name: dve.wait_ge(s_stat, stat(b, name))
                    if g := now(6, 0):
                        b, par, pair = g
                        dve.wait_ge(s_got[par], pair * (16 * G) + (16 * G + k.seen[par]))
                        dve.wait_ge(s_q, b * 4 + 4)
                        wait(dve, s_ex, b)
                        last_cols = got[:, par * G:(par + 1) * G, :].rearrange("p s (h c) -> p s h c", h=H)[:, :, :, C]
                        nc.vector.tensor_tensor(per_step(lg[:, :]), last_cols, per_step(pq[:, 0:FW]),
                                                ALU.add).then_inc(s_stat, 1)
                    if g := now(6, 1):
                        b, par, pair = g
                        dve.wait_ge(s_ld[par], pair * 32 + 32)
                        own(b, "add_src")
                        nc.vector.tensor_tensor(lg[:, :], lg[:, :], ae[:, par, :], ALU.add).then_inc(s_stat, 1)
                        nc.vector.tensor_tensor(
                            cols[:, 0:2, :], flags[:, par, P + 1:RW].unsqueeze(2).to_broadcast([P, 2, G]),
                            k.smask[:, :].unsqueeze(1).to_broadcast([P, 2, G]), ALU.mult).then_inc(s_stat, 1)
                    if g := now(6, 2):
                        b, par, pair = g
                        last_cols = got[:, par * G:(par + 1) * G, :].rearrange("p s (h c) -> p s h c", h=H)[:, :, :, C]
                        nc.vector.memset(last_cols, 1.0).then_inc(s_stat, 1)
                        own(b, "add_edge")
                        nc.vector.scalar_tensor_tensor(out=lg[:, :], in0=lg[:, :], scalar=0.2, in1=lg[:, :],
                                                       op0=ALU.mult, op1=ALU.max).then_inc(s_stat, 1)
                    if g := now(7, 0):
                        b, par, pair = g
                        own(b, "leaky")
                        nc.vector.tensor_tensor(per_step(lg[:, :]), per_step(lg[:, :]),
                                                k.neg[:, ds(b * G, G)].unsqueeze(2).to_broadcast([P, G, H]),
                                                ALU.add).then_inc(s_stat, 1)
                    if g := now(8, 1):
                        b, par, pair = g
                        dve.wait_ge(s_pe, move(b, "logits"))
                        nc.vector.tensor_tensor_scan(part[:, 0:P], flags[:, par, 0:P], pb[:, 0:P], -BIG, ALU.add,
                                                     ALU.max).then_inc(s_stat, 1)
                    if g := now(8, 2):
                        b, par, pair = g
                        nc.vector.tensor_tensor_scan(rev(part[:, P:2 * P]), rev(flags[:, par, 1:P + 1]), rev(pb[:, 0:P]),
                                                     -BIG, ALU.add, ALU.max).then_inc(s_stat, 1)
                    if g := now(9, 0):
                        b, par, pair = g
                        own(b, "scan_b")
                        nc.vector.tensor_tensor(
                            cols[:, 2:4, :], part[:, P - 1:P + 1].unsqueeze(2).to_broadcast([P, 2, G]),
                            k.smask[:, :].unsqueeze(1).to_broadcast([P, 2, G]), ALU.mult).then_inc(s_stat, 1)
                    if g := now(10, 1):
                        b, par, pair = g
                        dve.wait_ge(s_pe, move(b, "tails"))
                        nc.vector.tensor_copy(heads[:, :, :], px[0:H, 0:4 * G].rearrange("p (a s) -> p a s", a=4)
                                              ).then_inc(s_stat, 1)
                        nc.vector.tensor_copy(chain[:, par, 0, 0:1], chain[:, 1 - par, 0, G:G + 1]).then_inc(s_stat, 1)
                    if g := now(10, 2):
                        b, par, pair = g
                        own(b, "carry")
                        nc.vector.tensor_tensor_scan(chain[:, par, 0, 1:G + 1], heads[:, 0, :], heads[:, 2, :],
                                                     chain[:, par, 0, 0:1], ALU.add, ALU.max).then_inc(s_stat, 1)
                        nc.vector.tensor_tensor_scan(rev(chain[:, par, 1, 0:G - 1]), rev(heads[:, 1, 1:G]),
                                                     rev(heads[:, 3, 1:G]), -BIG, ALU.add, ALU.max).then_inc(s_stat, 1)
                    if g := now(12, 0):
                        b, par, pair = g
                        dve.wait_ge(s_pe, move(b, "starts"))
                        nc.vector.tensor_tensor(
                            ini[:, :, :], px[:, 64:64 + 2 * G + 2].rearrange("p (a s) -> p a s", a=2)[:, :, 0:G],
                            k.smask[:, :].unsqueeze(1).to_broadcast([P, 2, G]), ALU.mult).then_inc(s_stat, 1)
                    if g := now(12, 1):
                        b, par, pair = g
                        own(b, "ini")
                        nc.vector.tensor_reduce(init[:, :], ini[:, :, :], AX.X, ALU.add).then_inc(s_stat, 1)
                    if g := now(12, 2):
                        b, par, pair = g
                        own(b, "init")
                        nc.vector.tensor_tensor_scan(run[:, :], flags[:, par, 0:P], pb[:, 0:P], init[:, 0:1], ALU.add,
                                                     ALU.max).then_inc(s_stat, 1)
                    if g := now(13, 0):
                        b, par, pair = g
                        own(b, "run")
                        nc.vector.tensor_tensor_scan(rev(mx[:, :]), rev(flags[:, par, 1:P + 1]), rev(run[:, :]),
                                                     init[:, 1:2], ALU.add, ALU.max).then_inc(s_stat, 1)
                    if g := now(13, 1):
                        b, par, pair = g
                        own(b, "whole")
                        nc.vector.tensor_tensor(rise[:, :], chain[:, par, 0, 0:1], mx[0:H, 0:1],
                                                ALU.subtract).then_inc(s_stat, 1)
                    if g := now(13, 2):
                        b, par, pair = g
                        own(b, "rise")
                        nc.vector.tensor_scalar_min(drop[:, :], rise[:, 0:1].to_broadcast([H, P]), 0.0
                                                    ).then_inc(s_stat, 1)
                    if g := now(15, 0):
                        b, par, pair = g
                        dve.wait_ge(s_pe, move(b, "maxima"))
                        nc.vector.tensor_tensor(lg[:, :], lg[:, :], pb[:, 0:FW], ALU.subtract).then_inc(s_stat, 1)
                    if g := now(15, 2):
                        b, par, pair = g
                        dve.wait_ge(s_f, b + 1)
                        nc.vector.tensor_scalar(fac_row[:, :], drop_row[:, :], 1.0, None, ALU.subtract).then_inc(s_stat, 1)
                    if g := now(1, 0, 2):
                        b, par, pair = g
                        dve.wait_ge(s_pe, move(b, "factor"))
                        nc.vector.tensor_scalar(fac[:, :], px[:, 192:192 + H], 1.0, None, ALU.add).then_inc(s_stat, 1)

                def body(it, u):
                    a = u - U
                    if live(it, a, U, NS):
                        t = it * U + a
                        if u % G == 0:
                            dve.wait_ge(s_ex, it * 2 + u // G - 1)
                        wait(dve, s_mm, t - 1)
                        nc.vector.tensor_tensor(
                            wgt[:, u % 2, :].rearrange("p (h c) -> p h c", h=H),
                            got[:, u, :].rearrange("p (h c) -> p h c", h=H),
                            ex[:, u // G, (u % G) * H:(u % G + 1) * H].unsqueeze(2).to_broadcast([P, H, C1]),
                            ALU.mult).then_inc(s_rhs, 1)
                    maxima(it, u, 0)
                    r = a - LAG
                    if live(it, r, U, NS):
                        s = it * U + r
                        before = cur[:, (r - 1) % 4, :]
                        wait(dve, s_cur, s)
                        if r % G == 0:
                            dve.wait_ge(s_stat, stat(it * 2 + r // G, "fac"))
                            nc.vector.tensor_tensor(
                                scaled[:, :].rearrange("p (h c) -> p h c", h=H),
                                before.rearrange("p (h c) -> p h c", h=H),
                                fac[:, :].unsqueeze(2).to_broadcast([P, H, C1]), ALU.mult).then_inc(s_scaled, 1)
                            dve.wait_ge(s_scaled, it * 2 + r // G + 1)
                            before = scaled[:, :]
                        dve.wait_ge(s_mm, s + 1)
                        wait(dve, s_acc, s - 3)
                        nc.vector.scalar_tensor_tensor(out=cur[:, r % 4, :], in0=before, scalar=k.same[:, ds(s, 1)],
                                                       in1=pa[r % 4][:, 0:AW], op0=ALU.mult,
                                                       op1=ALU.add).then_inc(s_cur, 1)
                    maxima(it, u, 1)
                    n = u - 2
                    if live(it, n, U, NS):
                        s = it * U + n
                        wait(dve, s_mm, s - U + 1)
                        nc.vector.tensor_scalar(sel[:, n % U, :], k.iota[:, :], k.drel[:, ds(s, 1)], None,
                                                ALU.is_equal).then_inc(s_sel, 1)
                    maxima(it, u, 2)
                ticks(dve, NS, U, U + LAG, body, 2)

            @block.tensor
            def _(pe):
                pe_j = [None]

                def body(it, u):
                    a = u - U
                    if live(it, a, U, NS):
                        t = it * U + a
                        pe.wait_ge(s_rhs, t + 1)
                        wait(pe, s_cur, t - 3)
                        nc.tensor.matmul(pa[u % 4][:, 0:AW], sel[:, u, :], wgt[:, u % 2, :], start=True,
                                         stop=True).then_inc(s_mm, 1)
                    if g := group(it, u, 7, 1):
                        pe.wait_ge(s_stat, stat(g[0], "mask"))
                        nc.tensor.transpose(pb[:, 0:P], lg[:, :], k.ident[:, :]).then_inc(s_pe, 1)
                    if g := group(it, u, 9, 1):
                        pe.wait_ge(s_stat, stat(g[0], "cols"))
                        nc.tensor.matmul(px[0:H, 0:4 * G], k.hmask[:, :], cols[:, :, :].rearrange("p a s -> p (a s)"),
                                         start=True, stop=True).then_inc(s_pe, 1)
                    if g := group(it, u, 13, 1):
                        pe.wait_ge(s_stat, stat(g[0], "whole"))
                        nc.tensor.transpose(pb[:, 0:P], mx[:, :], k.ident[:, :]).then_inc(s_pe, 1)
                    n = u - 2
                    if live(it, n, U, NS):
                        pe.wait_ge(s_sel, it * U + n + 1)
                        if n % 4 == 0:
                            wait(pe, s_cp, it * 8 + n // 4)
                        nc.tensor.transpose(pt[:, (n % 4) * P:(n % 4 + 1) * P], sel[:, n % U, :],
                                            k.ident[:, :]).then_inc(s_tr, 1)
                    q = u - 6
                    if q % 4 < 2 and live(it, q - q % 4, U, NS):
                        first = q - q % 4
                        f = it * 8 + first // 4
                        if q % 4 == 0 or u == 0:
                            _, pe_j[0] = nc.values_load_multi_w_load_instructions(
                                k.step_j[0:1, ds(it * U + first, 4)], engines=(mybir.EngineType.PE,), min_val=0,
                                max_val=NT - 1,
                                skip_runtime_bounds_check_because="j(s) is clamped to the last node tile")
                        if q % 4 == 0:
                            pe.wait_ge(s_cp, f + 1)
                        if q % G == 0:
                            wait(pe, s_stat, stat(it * 2 + q // G - 1, "add_src"))
                        for m in (q % 4 * 2, q % 4 * 2 + 1):
                            o = (first + m) % G * H
                            for n in range(3):
                                last = nc.tensor.matmul(pq[:, o:o + H], tr[:, (first // 4) % 2, m * P:(m + 1) * P],
                                                        a_dst[:, ds(pe_j[0][m] * H + n * (NT * H), H)],
                                                        start=(n == 0), stop=(n == 2))
                        if q % 4 == 1:
                            last.then_inc(s_q, 1)
                    if g := group(it, u, 10, 1):
                        pe.wait_ge(s_stat, stat(g[0], "chain_b"))
                        nc.tensor.matmul(px[:, 64:64 + 2 * G + 2], k.hmask_t[:, :],
                                         chain[:, g[1], :, :].rearrange("p a s -> p (a s)"), start=True,
                                         stop=True).then_inc(s_pe, 1)
                    if g := group(it, u, 13, 1):
                        pe.wait_ge(s_stat, stat(g[0], "drop"))
                        nc.tensor.matmul(px[:, 160:160 + H], drop[:, :], k.ident[0:H, 0:H], start=True,
                                         stop=True).then_inc(s_pe, 1)
                    if g := group(it, u, 15, 1):
                        pe.wait_ge(s_stat, stat(g[0], "fac_row"))
                        nc.tensor.matmul(px[:, 192:192 + H], sel[0:1, g[1] * G, :], fac_row[:, :], start=True,
                                         stop=True).then_inc(s_pe, 1)
                ticks(pe, NS, U, U, body, 2)

            @block.scalar
            def _(act):
                act_j = [None]

                def body(it, u):
                    e = u - 5
                    if e % 4 == 0 and live(it, e, U, NS):
                        f = it * 8 + e // 4
                        act.wait_ge(s_tr, f * 4 + 4)
                        wait(act, s_q, f - 1)
                        nc.scalar.activation(tr[:, (e // 4) % 2, :], pt[:, :], ACT.Copy).then_inc(s_cp, 1)
                    r = u - U - LAG
                    if live(it, r, U, NS):
                        s = it * U + r
                        if r % 4 == 0 or u == 0:
                            _, act_j[0] = nc.values_load_multi_w_load_instructions(
                                k.step_j[0:1, ds(s - r % 4, 4)], engines=(mybir.EngineType.Activation,), min_val=0,
                                max_val=NT - 1,
                                skip_runtime_bounds_check_because="j(s) is clamped to the last node tile")
                        act.wait_ge(s_cur, s + 1)
                        wait(act, s_acc, s)
                        nc.scalar.activation(k.acc[:, ds(act_j[0][r % 4] * AW, AW)], cur[:, r % 4, :],
                                             ACT.Copy).then_inc(s_acc, 1)
                    if g := group(it, u, 14, 1):
                        b, par, pair = g
                        act.wait_ge(s_pe, move(b, "drop"))
                        wait(act, s_stat, stat(b - 1, "fac_row"))
                        nc.scalar.activation(drop_row[:, :], px[0:1, 160:160 + H], ACT.Exp).then_inc(s_f, 1)
                    if g := group(it, u, 15, 1):
                        b, par, pair = g
                        act.wait_ge(s_stat, stat(b, "subtract"))
                        wait(act, s_mm, b * G - G)
                        nc.scalar.activation(ex[:, par, :], lg[:, :], ACT.Exp).then_inc(s_ex, 1)
                ticks(act, NS, U, U + LAG, body, 2)
                act.wait_ge(s_acc, NS)
    for n in range(2):
        k.seen[n] += 16 * G * (NG // 2)


def segment_softmax(nc, tag, k):
    NB4 = CB // 4
    with ExitStack() as c:
        sb = lambda name, shape, dt=F32: c.enter_context(nc.sbuf_tensor(f"{tag}_{name}", shape, dt))
        sem = lambda name: c.enter_context(nc.semaphore(f"{tag}_{name}"))
        seq, run = k.acc[:, 0:SEQ], k.acc[:, SEQ:2 * SEQ]
        kraw = k.acc[:, 0:SEQ + 2]
        new = sb("sm_new", [P, SEQ + 1])
        per = sb("sm_per", [P, CB * P])
        tail = sb("sm_tail", [P, 2])
        ct = sb("sm_ct", [H, CH, 2])
        chain = sb("sm_chain", [H, CH + 1])
        init = sb("sm_init", [P, 1])
        dt_ = [nc.dram_tensor(f"{tag}_sm_tail{n}", [P, 2], F32) for n in range(2)]
        dc_ = [nc.dram_tensor(f"{tag}_sm_chain{n}", [P, 1], F32) for n in range(2)]
        pt = [c.enter_context(nc.psum_tensor(f"{tag}_sm_p{n}", [P, 512], F32)) for n in range(4)]
        s_key, s_v, s_per, s_t, s_seq, s_max, s_b, s_sub, s_ex = (
            sem("sm_key"), sem("sm_v"), sem("sm_sper"), sem("sm_st"), sem("sm_sseq"), sem("sm_max"), sem("sm_b"),
            sem("sm_sub"), sem("sm_ex"))
        s_tail, s_ct, s_chain, s_in, s_td = sem("sm_stail"), sem("sm_sct"), sem("sm_schain"), sem("sm_sin"), sem("sm_std")
        bch = lambda a: a.rearrange("p (c b h) -> p c b h", c=CH, h=H)
        perm = per[:, :].rearrange("p (b c h) -> p c b h", c=CH, h=H)
        perh = lambda a: a.rearrange("p (c b) -> p c b", c=CH).unsqueeze(3).to_broadcast([P, CH, CB, H])
        edge4 = bch(k.edge[:, :])
        with nc.Block() as block:
            @block.sync
            def _(sp):
                for ch in range(CH):
                    sp.dma_start(kraw[ch * H:(ch + 1) * H, :],
                                 k.keys.ap()[P - 1 + ch * SEQ:P + 1 + (ch + 1) * SEQ]
                                 .rearrange("(a n) -> a n", a=1).to_broadcast([H, SEQ + 2])).then_inc(s_key, 16)
                for n in range(2):
                    sp.wait_ge(s_tail, n + 1)
                    sp.dma_start(dt_[n].ap(), tail[:, :]).then_inc(s_td, 16)
                    sp.wait_ge(s_td, 16 * (4 * n + 1))
                    sp.dma_start(ct[:, :, :], dt_[n].ap().rearrange("(c h) w -> h c w", h=H)).then_inc(s_td, 16)
                    sp.wait_ge(s_td, 16 * (4 * n + 2))
                    sp.sem_inc(s_ct, 1)
                    sp.wait_ge(s_chain, n + 1)
                    sp.dma_start(dc_[n].ap().rearrange("(c h) w -> h (c w)", h=H),
                                 chain[:, n:n + CH]).then_inc(s_td, 16)
                    sp.wait_ge(s_td, 16 * (4 * n + 3))
                    sp.dma_start(init[:, :], dc_[n].ap()).then_inc(s_td, 16)
                    sp.wait_ge(s_td, 16 * (4 * n + 4))
                    sp.sem_inc(s_in, 1)

            @block.vector
            def _(dve):
                v = Chain(dve, s_v)
                v(nc.vector.tensor_tensor(perm, edge4, perh(k.weight[:, :]), ALU.mult))
                v(nc.vector.tensor_tensor(perm, perm, perh(k.neg[:, :]), ALU.add))
                dve.sem_inc(s_per, 1)
                dve.wait_ge(s_key, 16 * CH)
                v(nc.vector.tensor_tensor(new[:, :], kraw[:, 1:SEQ + 2], kraw[:, 0:SEQ + 1], ALU.not_equal))
                v(nc.vector.tensor_scalar(new[:, :], new[:, :], -BIG, None, ALU.mult))
                dve.sem_inc(s_per, 1)
                dve.wait_ge(s_seq, NB4)
                rev = lambda a: a[:, ::-1]
                v(nc.vector.tensor_tensor_scan(run, new[:, 0:SEQ], seq, -BIG, ALU.add, ALU.max))
                v(nc.vector.tensor_copy(tail[:, 1:2], run[:, SEQ - 1:SEQ]))
                v(nc.vector.tensor_reduce(tail[:, 0:1], new[:, 0:SEQ], AX.X, ALU.min))
                dve.sem_inc(s_tail, 1)
                v(nc.vector.memset(chain[:, :], -BIG))
                dve.wait_ge(s_ct, 1)
                v(nc.vector.tensor_tensor_scan(chain[:, 1:CH + 1], ct[:, :, 0], ct[:, :, 1], -BIG, ALU.add, ALU.max))
                dve.sem_inc(s_chain, 1)
                dve.wait_ge(s_in, 1)
                v(nc.vector.tensor_tensor_scan(run, new[:, 0:SEQ], seq, init[:, 0:1], ALU.add, ALU.max))
                v(nc.vector.tensor_tensor_scan(rev(seq), rev(new[:, 1:SEQ + 1]), rev(run), -BIG, ALU.add, ALU.max))
                v(nc.vector.tensor_copy(tail[:, 1:2], seq[:, 0:1]))
                v(nc.vector.tensor_reduce(tail[:, 0:1], new[:, 1:SEQ + 1], AX.X, ALU.min))
                dve.sem_inc(s_tail, 1)
                v(nc.vector.memset(chain[:, :], -BIG))
                dve.wait_ge(s_ct, 2)
                v(nc.vector.tensor_tensor_scan(chain[:, 0:CH][:, ::-1], ct[:, ::-1, 0], ct[:, ::-1, 1], -BIG,
                                               ALU.add, ALU.max))
                dve.sem_inc(s_chain, 1)
                dve.wait_ge(s_in, 2)
                v(nc.vector.tensor_tensor_scan(rev(seq), rev(new[:, 1:SEQ + 1]), rev(run), init[:, 0:1], ALU.add, ALU.max))
                dve.sem_inc(s_max, 1)
                for g in range(NB4):
                    dve.wait_ge(s_b, g + 1)
                    nc.vector.tensor_tensor(per[:, g * 512:(g + 1) * 512], per[:, g * 512:(g + 1) * 512], pt[g % 4][:, :],
                                            ALU.subtract).then_inc(s_sub, 1)

            @block.tensor
            def _(pe):
                pe.wait_ge(s_per, 1)
                for g in range(NB4):
                    wait(pe, s_seq, g - 3)
                    for n in range(4):
                        b = g * 4 + n
                        last = nc.tensor.transpose(pt[g % 4][:, n * P:(n + 1) * P], per[:, b * P:(b + 1) * P], k.ident[:, :])
                    last.then_inc(s_t, 1)
                pe.wait_ge(s_max, 1)
                for g in range(NB4):
                    wait(pe, s_sub, g - 3)
                    for n in range(4):
                        b = g * 4 + n
                        last = nc.tensor.transpose(pt[g % 4][:, n * P:(n + 1) * P], k.acc[:, b * P:(b + 1) * P], k.ident[:, :])
                    last.then_inc(s_b, 1)

            @block.scalar
            def _(act):
                act.wait_ge(s_per, 2)
                for g in range(NB4):
                    act.wait_ge(s_t, g + 1)
                    nc.scalar.activation(k.acc[:, g * 512:(g + 1) * 512], pt[g % 4][:, :], ACT.Copy).then_inc(s_seq, 1)
                for g in range(NB4):
                    act.wait_ge(s_sub, g + 1)
                    nc.scalar.activation(edge4[:, :, g * 4:(g + 1) * 4, :],
                                         per[:, g * 512:(g + 1) * 512].rearrange("p (b c h) -> p c b h", c=CH, h=H),
                                         ACT.Exp).then_inc(s_ex, 1)
                act.wait_ge(s_ex, NB4)




def recycle(nc):
    used = sorted(nc.released_uncleared_semaphores)
    with nc.Block() as block:
        @block.gpsimd
        def _(pool):
            pool.sem_clear(range(used[0], used[-1] + 1))


def load(nc, name, pairs):
    with nc.semaphore(name) as s, nc.Block() as block:
        @block.sync
        def _(sp):
            for tile, source in pairs:
                sp.dma_start(tile, source).then_inc(s, 16)
            sp.wait_ge(s, 16 * len(pairs))


def store(nc, name, target, tile):
    with nc.semaphore(name) as s, nc.Block() as block:
        @block.sync
        def _(sp):
            sp.dma_start(target, tile).then_inc(s, 16)
            sp.wait_ge(s, 16)


def rows_of(w, kt=KT):
    return w.rearrange("(k p) n -> p k n", k=kt)


def by_head(a):
    return a.rearrange("p (h c) -> p h c", h=H)


def spread(a, rows=P):
    return a.rearrange("(a n) -> a n", a=1).to_broadcast([rows, a.shape[0]])


def column(a):
    return a.rearrange("(k p) -> p k", p=P)


def fold_gain(nc, k, name, w, width, gain, shift, bias, cols):
    with ExitStack() as c:
        sem = lambda n: c.enter_context(nc.semaphore(name + n))
        pb = [c.enter_context(nc.psum_tensor(f"{name}p{n}", [P, 512], F32)) for n in range(2)]
        s_mm, s_v = sem("mm"), sem("v")
        with nc.Block() as block:
            @block.tensor
            def _(pe):
                if cols:
                    for f in range(width // P):
                        for n in range(KT):
                            last = nc.tensor.matmul(pb[0][:, f:f + 1], w[:, n, f * P:(f + 1) * P], shift[:, n:n + 1],
                                                    start=(n == 0), stop=(n == KT - 1))
                else:
                    for n in range(KT):
                        last = nc.tensor.matmul(pb[0][0:1, 0:width], shift[:, n:n + 1], w[:, n, :], start=(n == 0),
                                                stop=(n == KT - 1))
                last.then_inc(s_mm, 1)

            @block.vector
            def _(dve):
                v = Chain(dve, s_v)
                dve.wait_ge(s_mm, 1)
                if cols:
                    v(nc.vector.tensor_tensor(bias, bias, pb[0][:, 0:width // P], ALU.add))
                else:
                    v(nc.vector.tensor_tensor(bias, bias, pb[0][0:1, 0:width], ALU.add))
                for n in range(KT):
                    v(nc.vector.tensor_scalar(w[:, n, :], w[:, n, :], gain[:, n:n + 1], None, ALU.mult))


def attention_output(nc, k, y, wo, bo, alpha, rd):
    U = 4
    with ExitStack() as c:
        sb = lambda name, shape, dt=F32: c.enter_context(nc.sbuf_tensor(name, shape, dt))
        sem = lambda name: c.enter_context(nc.semaphore(name))
        a = sb("ao_a", [P, 2, D])
        at = sb("ao_at", [P, 2, D])
        pt = [c.enter_context(nc.psum_tensor(f"ao_t{n}", [P, 512], F32)) for n in range(2)]
        po = [c.enter_context(nc.psum_tensor(f"ao_o{n}", [P, 512], F32)) for n in range(2)]
        s_a, s_t, s_at, s_o, s_y = sem("ao_sa"), sem("ao_st"), sem("ao_sat"), sem("ao_so"), sem("ao_sy")
        with nc.Block() as block:
            @block.vector
            def _(dve):
                def body(it, u):
                    t = it * U + u
                    if live(it, u, U, NT):
                        wait(dve, s_t, t - 1)
                        nc.vector.tensor_tensor(
                            a[:, u % 2, :].rearrange("p (h c) -> p h c", h=H),
                            k.acc[:, ds(t * AW, AW)].rearrange("p (h c) -> p h c", h=H)[:, :, 0:C],
                            rd[:, ds(t * H, H)].unsqueeze(2).to_broadcast([P, H, C]), ALU.mult).then_inc(s_a, 1)
                    r = u - 2
                    if live(it, r, U, NT):
                        s = it * U + r
                        dve.wait_ge(s_o, s + 1)
                        nc.vector.scalar_tensor_tensor(out=y[:, ds(s * D, D)], in0=po[r % 2][:, 0:D], scalar=alpha,
                                                       in1=y[:, ds(s * D, D)], op0=ALU.mult, op1=ALU.add).then_inc(s_y, 1)
                ticks(dve, NT, U, 2, body)
                dve.wait_ge(s_y, NT)

            @block.scalar
            def _(act):
                def body(it, u):
                    t = it * U + u
                    act.wait_ge(s_t, t + 1)
                    wait(act, s_o, t - 1)
                    nc.scalar.activation(at[:, u % 2, :], pt[u % 2][:, 0:D], ACT.Copy).then_inc(s_at, 1)
                ticks(act, NT, U, 0, body)

            @block.tensor
            def _(pe):
                def body(it, u):
                    t = it * U + u
                    if live(it, u, U, NT):
                        pe.wait_ge(s_a, t + 1)
                        wait(pe, s_at, t - 1)
                        for n in range(KT):
                            last = nc.tensor.transpose(pt[u % 2][:, n * P:(n + 1) * P], a[:, u % 2, n * P:(n + 1) * P],
                                                       k.ident[:, :])
                        last.then_inc(s_t, 1)
                    r = u - 1
                    if live(it, r, U, NT):
                        s = it * U + r
                        pe.wait_ge(s_at, s + 1)
                        wait(pe, s_y, s - 1)
                        for n in range(KT):
                            nc.tensor.matmul(po[r % 2][:, 0:D], at[:, r % 2, n * P:(n + 1) * P], wo[:, n, :],
                                             start=(n == 0), stop=False)
                        nc.tensor.matmul(po[r % 2][:, 0:D], k.ones[0:1, :], bo, start=False, stop=True).then_inc(s_o, 1)
                ticks(pe, NT, U, 1, body)


def feed_forward(nc, k, y, xr, wf1, bf1, wf2, bf2, beta):
    U = 4
    with ExitStack() as c:
        sb = lambda name, shape, dt=F32: c.enter_context(nc.sbuf_tensor(name, shape, dt))
        sem = lambda name: c.enter_context(nc.semaphore(name))
        z = sb("ff_z", [P, 2, D])
        zt = sb("ff_zt", [P, 2, D])
        g = k.acc[:, 0:2 * FF].rearrange("p (s f) -> p s f", s=2)
        pt = [c.enter_context(nc.psum_tensor(f"ff_t{n}", [P, 512], F32)) for n in range(2)]
        ph = [[c.enter_context(nc.psum_tensor(f"ff_h{n}{m}", [P, 512], F32)) for m in range(2)] for n in range(2)]
        po = [c.enter_context(nc.psum_tensor(f"ff_o{n}", [P, 512], F32)) for n in range(2)]
        s_z, s_t, s_zt, s_h, s_g, s_o, s_y, s_x = (sem("ff_sz"), sem("ff_st"), sem("ff_szt"), sem("ff_sh"), sem("ff_sg"),
                                                   sem("ff_so"), sem("ff_sy"), sem("ff_sx"))
        with nc.Block() as block:
            @block.scalar
            def _(act):
                def body(it, u):
                    t = it * U + u
                    if live(it, u, U, NT):
                        wait(act, s_t, t - 1)
                        nc.scalar.activation(z[:, u % 2, :], y[:, ds(t * D, D)], ACT.Identity, bias=k.nb[:, ds(t, 1)],
                                             scale=k.rs[:, ds(t, 1)]).then_inc(s_z, 1)
                    r = u - 2
                    if live(it, r, U, NT):
                        s = it * U + r
                        act.wait_ge(s_h, s + 1)
                        wait(act, s_o, s - 1)
                        for f in range(FT):
                            last = nc.scalar.activation(g[:, r % 2, f * P:(f + 1) * P],
                                                        ph[r % 2][f // 4][:, (f % 4) * P:(f % 4 + 1) * P], ACT.Gelu,
                                                        bias=bf1[:, f:f + 1])
                        last.then_inc(s_g, 1)
                ticks(act, NT, U, 2, body)

            @block.vector
            def _(dve):
                def body(it, u):
                    t = it * U + u
                    if live(it, u, U, NT):
                        dve.wait_ge(s_t, t + 1)
                        wait(dve, s_h, t - 1)
                        nc.vector.tensor_copy(zt[:, u % 2, :], pt[u % 2][:, 0:D]).then_inc(s_zt, 1)
                    r = u - 4
                    if live(it, r, U, NT):
                        s = it * U + r
                        dve.wait_ge(s_o, s + 1)
                        nc.vector.scalar_tensor_tensor(out=y[:, ds(s * D, D)], in0=po[r % 2][:, 0:D], scalar=beta,
                                                       in1=y[:, ds(s * D, D)], op0=ALU.mult, op1=ALU.add).then_inc(s_y, 1)
                        dve.wait_ge(s_y, s + 1)
                        nc.vector.tensor_tensor(xr[:, ds(s * D, D)], xr[:, ds(s * D, D)], y[:, ds(s * D, D)],
                                                ALU.add).then_inc(s_x, 1)
                ticks(dve, NT, U, 4, body)
                dve.wait_ge(s_x, NT)

            @block.tensor
            def _(pe):
                def body(it, u):
                    t = it * U + u
                    if live(it, u, U, NT):
                        pe.wait_ge(s_z, t + 1)
                        wait(pe, s_zt, t - 1)
                        for n in range(KT):
                            last = nc.tensor.transpose(pt[u % 2][:, n * P:(n + 1) * P], z[:, u % 2, n * P:(n + 1) * P],
                                                       k.ident[:, :])
                        last.then_inc(s_t, 1)
                    q = u - 3
                    if live(it, q, U, NT):
                        s = it * U + q
                        pe.wait_ge(s_g, s + 1)
                        wait(pe, s_y, s - 1)
                        for f in range(FT):
                            nc.tensor.matmul(po[q % 2][:, 0:D], g[:, q % 2, f * P:(f + 1) * P], wf2[:, f, :],
                                             start=(f == 0), stop=False)
                        nc.tensor.matmul(po[q % 2][:, 0:D], k.ones[0:1, :], bf2, start=False, stop=True).then_inc(s_o, 1)
                    r = u - 1
                    if live(it, r, U, NT):
                        s = it * U + r
                        pe.wait_ge(s_zt, s + 1)
                        wait(pe, s_g, s - 1)
                        for f in range(FT):
                            for n in range(KT):
                                last = nc.tensor.matmul(ph[r % 2][f // 4][:, (f % 4) * P:(f % 4 + 1) * P],
                                                        wf1[:, n, f * P:(f + 1) * P], zt[:, r % 2, n * P:(n + 1) * P],
                                                        start=(n == 0), stop=(n == KT - 1))
                        last.then_inc(s_h, 1)
                ticks(pe, NT, U, 3, body)


def layer3_rows(nc, k, y, rd, bias):
    with ExitStack() as c:
        a = c.enter_context(nc.sbuf_tensor("l3_a", [P, 2, D], F32))
        s_a, s_b, s_y = (c.enter_context(nc.semaphore(n)) for n in ("l3_sa", "l3_sb", "l3_sy"))
        with nc.Block() as block:
            @block.vector
            def _(dve):
                def body(it, u):
                    t = it * 4 + u
                    if live(it, u, 4, NT):
                        nc.vector.tensor_tensor(
                            a[:, u % 2, :].rearrange("p (h c) -> p h c", h=H),
                            k.acc[:, ds(t * AW, AW)].rearrange("p (h c) -> p h c", h=H)[:, :, 0:C],
                            rd[:, ds(t * H, H)].unsqueeze(2).to_broadcast([P, H, C]), ALU.mult).then_inc(s_a, 1)
                        nc.vector.tensor_tensor(y[:, ds(t * D, D)], y[:, ds(t * D, D)], bias, ALU.add).then_inc(s_b, 1)
                    r = u - 1
                    if live(it, r, 4, NT):
                        s = it * 4 + r
                        dve.wait_ge(s_a, s + 1)
                        dve.wait_ge(s_b, s + 1)
                        nc.vector.tensor_tensor(y[:, ds(s * D, D)], y[:, ds(s * D, D)], a[:, r % 2, :],
                                                ALU.add).then_inc(s_y, 1)
                        dve.wait_ge(s_y, s + 1)
                ticks(dve, NT, 4, 1, body)


def final_output(nc, k, xr, y, gamma, beta, out):
    with ExitStack() as c:
        z = c.enter_context(nc.sbuf_tensor("fo_z", [P, 4, D], F32))
        sem = lambda n: c.enter_context(nc.semaphore(n))
        s_z, s_1, s_2, s_3, s_out = sem("fo_z_"), sem("fo_1"), sem("fo_2"), sem("fo_3"), [sem(f"fo_out{n}") for n in range(4)]
        with nc.Block() as block:
            @block.scalar
            def _(act):
                def body(it, u):
                    t = it * 4 + u
                    wait(act, s_out[u % 4], it * 16 if u < 4 else 0)
                    nc.scalar.activation(z[:, u % 4, :], y[:, ds(t * D, D)], ACT.Identity, bias=k.nb[:, ds(t, 1)],
                                         scale=k.rs[:, ds(t, 1)]).then_inc(s_z, 1)
                ticks(act, NT, 4, 0, body)

            @block.vector
            def _(dve):
                def body(it, u):
                    for lag, sem_in, sem_out in ((0, s_z, s_1), (1, s_1, s_2), (2, s_2, s_3)):
                        r = u - lag
                        if live(it, r, 4, NT):
                            s = it * 4 + r
                            dve.wait_ge(sem_in, s + 1)
                            zz = z[:, r % 4, :]
                            if lag == 0:
                                ins = nc.vector.tensor_tensor(zz, zz, gamma, ALU.mult)
                            elif lag == 1:
                                ins = nc.vector.tensor_tensor(zz, zz, beta, ALU.add)
                            else:
                                ins = nc.vector.tensor_tensor(zz, zz, xr[:, ds(s * D, D)], ALU.add)
                            ins.then_inc(sem_out, 1)
                ticks(dve, NT, 4, 2, body)

            @block.sync
            def _(sp):
                def body(it, u):
                    t = it * 4 + u
                    sp.wait_ge(s_3, t + 1)
                    if isinstance(t, int) and t == NT - 1:
                        sp.dma_start(out[t * P:N, :], z[0:LAST_ROWS, u % 4, :]).then_inc(s_out[u % 4], 16)
                    else:
                        sp.dma_start(out[ds(t * P, P), :], z[:, u % 4, :]).then_inc(s_out[u % 4], 16)
                ticks(sp, NT, 4, 0, body)
                for n in range(4):
                    sp.wait_ge(s_out[n], 16 * len(range(n, NT, 4)))


def split3(nc, a, parts, n):
    with nc.semaphore("split3") as s_v, nc.Block() as block:
        @block.vector
        def _(dve):
            v = Chain(dve, s_v)
            for m in range(3):
                part = parts[:, m * n:(m + 1) * n]
                v(nc.vector.tensor_copy(part, a))
                v(nc.vector.tensor_tensor(a, a, part, ALU.subtract))


def denominators(nc, tag, k, rd):
    with nc.semaphore(f"{tag}_dn") as s_v, nc.Block() as block:
        @block.vector
        def _(dve):
            v = Chain(dve, s_v)
            r3 = rd.rearrange("p (t h) -> p t h", h=H)
            v(nc.vector.tensor_scalar(r3, k.acc[:, 0:NT * AW].rearrange("p (t h c) -> p t h c", h=H, c=C1)[:, :, :, C], 1e-16,
                                      None, ALU.add))
            v(nc.vector.reciprocal(rd, rd))


def fold_attention(nc, name, tmp, jobs):
    with nc.semaphore(name) as s_v, nc.Block() as block:
        @block.vector
        def _(dve):
            v = Chain(dve, s_v)
            for w, att, out, heads in jobs:
                v(nc.vector.tensor_tensor(tmp, w, att, ALU.mult))
                v(nc.vector.tensor_reduce(out, tmp.rearrange("p (h c) -> p h c", h=heads), AX.X, ALU.add))


def gnn_kernel(nc, x, src, dst, edge_attr, edge_weight, w0, att_l, att_r, w1, wq, bq, wk, bk, wv, bv, we, be, wo, bo,
               ln1_g, ln1_b, ln2_g, ln2_b, wf1, bf1, wf2, bf2, alpha, beta, w3, we3, att_src, att_dst, att_edge,
               bias3, gamma3, beta3, out):
    flat = lambda a: a.rearrange("h c -> (h c)")
    table = lambda name, w: nc.dram_tensor(name, [NPAD, w], F32).ap()
    with ExitStack() as c:
        k = globals_of(nc, c)
        k.ae_dram = nc.dram_tensor("layer3_edge_part", [P, SEQ], F32)
        walk_tables(nc, k, src, dst, edge_weight)
        run_flags(nc, k)
        xr = c.enter_context(nc.sbuf_tensor("xr", [P, NT * D], F32))
        xrv = xr[:, :]

        t0, al0 = table("t0", D + H0), table("al0", H0)
        with ExitStack() as s:
            sb = lambda name, shape, dt=F32: s.enter_context(nc.sbuf_tensor(name, shape, dt))
            w0t = sb("w0t", [P, KT, D + 2 * H0])
            att = sb("att0", [P, 2, D])
            tmp = sb("tmp0", [P, D])
            with nc.semaphore("xpad") as s_p, nc.Block() as block:
                @block.gpsimd
                def _(pool):
                    nc.gpsimd.memset(xr[:, (NT - 1) * D:NT * D], 0.0).then_inc(s_p, 1)
                    pool.wait_ge(s_p, 1)
            whole = (NT - 1) * P
            load(nc, "ld0", [(xr[:, 0:(NT - 1) * D].rearrange("p (t d) -> p t d", d=D),
                              x[0:whole, :].rearrange("(t p) d -> p t d", p=P)),
                             (xr[0:LAST_ROWS, (NT - 1) * D:NT * D], x[whole:N, :]),
                             (w0t[:, :, 0:D], rows_of(w0)), (att[:, 0, :], spread(flat(att_r))),
                             (att[:, 1, :], spread(flat(att_l)))])
            fold_attention(nc, "fold0", tmp[:, :],
                           [(w0t[:, kt, 0:D], att[:, n, :], w0t[:, kt, D + n * H0:D + (n + 1) * H0], H0)
                            for kt in range(KT) for n in range(2)])
            row_stats(nc, "p1", k, xr[:, :].rearrange("p (t d) -> p t d", d=D))
            project(nc, "p2", k, xrv, ACT.Relu, [(w0t, None, D + 2 * H0, None, [(0, D + H0, t0), (D + H0, H0, al0)], None)])
        layer0_edges(nc, k, xrv, src, dst, t0, al0)

        t1 = table("t1", D)
        with ExitStack() as s:
            w1t = s.enter_context(nc.sbuf_tensor("w1t", [P, KT, D], F32))
            load(nc, "ld1", [(w1t[:, :, :], rows_of(w1))])
            row_stats(nc, "p3", k, xr[:, :].rearrange("p (t d) -> p t d", d=D))
            project(nc, "p4", k, xrv, ACT.Relu, [(w1t, None, D, k.dis, [(0, D, t1)], None)])
        aggregate(nc, "p5", k, t1, False)
        add_scaled(nc, k, xrv)
        recycle(nc)

        t_k, t_v = table("t_k", D), table("t_v", AW)
        with ExitStack() as s:
            sb = lambda name, shape, dt=F32: s.enter_context(nc.sbuf_tensor(name, shape, dt))
            h2 = sb("h2", [P, NT * D])
            width = [D, D, AW]
            w = [sb(f"w2_{n}", [P, KT, m]) for n, m in enumerate(width)]
            b = [sb(f"b2_{n}", [1, m]) for n, m in enumerate(width)]
            gain, shift = sb("gain1", [P, KT]), sb("shift1", [P, KT])
            with nc.semaphore("ones2") as s_p, nc.Block() as block:
                @block.gpsimd
                def _(pool):
                    nc.gpsimd.memset(w[2][:, :, :], 0.0).then_inc(s_p, 1)
                    nc.gpsimd.memset(b[2][:, :], 1.0).then_inc(s_p, 1)
                    pool.wait_ge(s_p, 2)
            load(nc, "ld2", [(w[n][:, :, :], rows_of(a)) for n, a in enumerate((wq, wk))] +
                 [(by_head(w[2][:, n, :])[:, :, 0:C], by_head(wv[n * P:(n + 1) * P, :])) for n in range(KT)] +
                 [(b[n][:, :], spread(a, 1)) for n, a in enumerate((bq, bk))] +
                 [(by_head(b[2][:, :])[:, :, 0:C], by_head(spread(bv, 1)))] +
                 [(gain[:, :], column(ln1_g)), (shift[:, :], column(ln1_b))])
            for n in range(3):
                fold_gain(nc, k, f"fg{n}", w[n], width[n], gain, shift, b[n][:, :], False)
            row_stats(nc, "p6", k, xr[:, :].rearrange("p (t d) -> p t d", d=D))
            normalized(nc, "p7", k, xrv, h2[:, :], ACT.Relu)
            row_stats(nc, "p8", k, h2[:, :].rearrange("p (t d) -> p t d", d=D))
            project(nc, "p9", k, h2[:, :], ACT.Identity,
                    [(w[0], b[0][0:1, :], D, None, [], k.acc[:, :]), (w[1], b[1][0:1, :], D, None, [(0, D, t_k)], None),
                     (w[2], b[2][0:1, :], AW, None, [(0, AW, t_v)], None)])
        with ExitStack() as s:
            sb = lambda name, shape, dt=F32: s.enter_context(nc.sbuf_tensor(name, shape, dt))
            k.edge = sb("edge2", [P, SEQ])
            with ExitStack() as s2:
                sb2 = lambda name, shape, dt=F32: s2.enter_context(nc.sbuf_tensor(name, shape, dt))
                k.ae = sb2("ae", [P, SEQ])
                wet = sb2("wet", [P, EW])
                we3t, atte, tmp = sb2("we3t", [ED, D]), sb2("atte", [ED, D]), sb2("tmp2", [ED, D])
                with nc.semaphore("wepad") as s_p, nc.Block() as block:
                    @block.gpsimd
                    def _(pool):
                        nc.gpsimd.memset(wet[:, :], 0.0).then_inc(s_p, 1)
                        pool.wait_ge(s_p, 1)
                load(nc, "ld2e", [(wet[0:ED, 0:C], we), (wet[ED:ED + 1, 0:C], spread(be, 1)), (we3t[:, :], we3),
                                  (atte[:, :], spread(flat(att_edge), ED))])
                fold_attention(nc, "fold2", tmp[:, :], [(we3t[:, :], atte[:, :], wet[0:ED, C:EW], H)])
                layer2_scores(nc, k, t_k, k.acc, wet[:, :], edge_attr)
                store(nc, "st_ae", k.ae_dram.ap(), k.ae[:, :])
            segment_softmax(nc, "p10", k)
            aggregate(nc, "p11", k, t_v, True)
        with ExitStack() as s:
            sb = lambda name, shape, dt=F32: s.enter_context(nc.sbuf_tensor(name, shape, dt))
            recycle(nc)
            y = sb("y2", [P, NT * D])
            wot, bot = sb("wot", [P, KT, D]), sb("bot", [1, D])
            wf1t, bf1t = sb("wf1t", [P, KT, FF]), sb("bf1t", [P, FT])
            wf2t, bf2t = sb("wf2t", [P, FT, D]), sb("bf2t", [1, D])
            gain, shift = sb("gain2", [P, KT]), sb("shift2", [P, KT])
            al_, be_ = sb("alpha_", [P, 1]), sb("beta_", [P, 1])
            rd = sb("rd2", [P, NT * H])
            load(nc, "ld3", [(wot[:, :, :], rows_of(wo)), (bot[:, :], spread(bo, 1)), (wf1t[:, :, :], rows_of(wf1)),
                             (bf1t[:, :], column(bf1)), (wf2t[:, :, :], rows_of(wf2, FT)), (bf2t[:, :], spread(bf2, 1)),
                             (gain[:, :], column(ln2_g)), (shift[:, :], column(ln2_b)), (al_[:, :], spread(alpha)),
                             (be_[:, :], spread(beta))])
            fold_gain(nc, k, "fgf", wf1t, FF, gain, shift, bf1t[:, :], True)
            denominators(nc, "p12", k, rd[:, :])
            row_stats(nc, "p13", k, xr[:, :].rearrange("p (t d) -> p t d", d=D))
            normalized(nc, "p14", k, xrv, y[:, :], ACT.Relu)
            attention_output(nc, k, y[:, :], wot, bot[0:1, :], al_[:, 0:1], rd[:, :])
            row_stats(nc, "p15", k, y[:, :].rearrange("p (t d) -> p t d", d=D))
            feed_forward(nc, k, y[:, :], xrv, wf1t, bf1t, wf2t, bf2t[0:1, :], be_[:, 0:1])

        recycle(nc)
        t_xp = table("t_xp", AW)
        with ExitStack() as s:
            sb = lambda name, shape, dt=F32: s.enter_context(nc.sbuf_tensor(name, shape, dt))
            a_parts = sb("a_parts", [P, 3 * NT * H], BF16)
            with ExitStack() as s2:
                sb2 = lambda name, shape, dt=F32: s2.enter_context(nc.sbuf_tensor(name, shape, dt))
                a_dst = sb2("a_dst", [P, NT * H])
                w3t, w3d = sb2("w3t", [P, KT, AW]), sb2("w3d", [P, KT, H])
                att, tmp = sb2("att3", [P, 2, D]), sb2("tmp3", [P, D])
                w3p = sb2("w3p", [P, KT, D])
                load(nc, "ld4", [(w3p[:, :, :], rows_of(w3)), (att[:, 0, :], spread(flat(att_src))),
                                 (att[:, 1, :], spread(flat(att_dst)))])
                fold_attention(nc, "fold3", tmp[:, :],
                               [(w3p[:, kt, :], att[:, n, :], to, H) for kt in range(KT)
                                for n, to in enumerate((by_head(w3t[:, kt, :])[:, :, C], w3d[:, kt, :]))])
                with nc.semaphore("w3heads") as s_w, nc.Block() as block:
                    @block.vector
                    def _(dve):
                        for kt in range(KT):
                            nc.vector.tensor_copy(by_head(w3t[:, kt, :])[:, :, 0:C], by_head(w3p[:, kt, :])
                                                  ).then_inc(s_w, 1)
                        dve.wait_ge(s_w, KT)
                row_stats(nc, "p16", k, xr[:, :].rearrange("p (t d) -> p t d", d=D))
                project(nc, "p17", k, xrv, ACT.Relu, [(w3t, None, AW, None, [(0, AW, t_xp)], None),
                                               (w3d, None, H, None, [], a_dst[:, :])])
                split3(nc, a_dst[:, :], a_parts[:, :], NT * H)
            layer3_edges(nc, k, t_xp, a_parts)
        with ExitStack() as s:
            sb = lambda name, shape, dt=F32: s.enter_context(nc.sbuf_tensor(name, shape, dt))
            y = sb("y3", [P, NT * D])
            b3, g3, be3 = sb("bias3t", [P, D]), sb("gamma3t", [P, D]), sb("beta3t", [P, D])
            rd = sb("rd3", [P, NT * H])
            load(nc, "ld5", [(b3[:, :], spread(bias3)), (g3[:, :], spread(gamma3)), (be3[:, :], spread(beta3))])
            denominators(nc, "p20", k, rd[:, :])
            row_stats(nc, "p21", k, xr[:, :].rearrange("p (t d) -> p t d", d=D))
            normalized(nc, "p22", k, xrv, y[:, :], ACT.Relu)
            layer3_rows(nc, k, y[:, :], rd[:, :], b3[:, :])
            row_stats(nc, "p23", k, y[:, :].rearrange("p (t d) -> p t d", d=D))
            final_output(nc, k, xrv, y[:, :], g3[:, :], be3[:, :], out)


_INS = ['x', 'src', 'dst', 'edge_attr_64', 'edge_weight', 'L0_gnn_weight', 'L0_gnn_attn_l', 'L0_gnn_attn_r',
        'L1_gnn_W', 'L2_gnn_Wq', 'L2_gnn_bq', 'L2_gnn_Wk', 'L2_gnn_bk', 'L2_gnn_Wv', 'L2_gnn_bv', 'L2_gnn_We',
        'L2_gnn_be', 'L2_gnn_Wo', 'L2_gnn_bo', 'L2_gnn_ln1_g', 'L2_gnn_ln1_b', 'L2_gnn_ln2_g', 'L2_gnn_ln2_b',
        'L2_gnn_W1', 'L2_gnn_b1', 'L2_gnn_W2', 'L2_gnn_b2', 'L2_gnn_alpha', 'L2_gnn_beta', 'L3_gnn_W', 'L3_gnn_W_e',
        'L3_gnn_att_src', 'L3_gnn_att_dst', 'L3_gnn_att_edge', 'L3_gnn_bias', 'L3_gnn_gamma', 'L3_gnn_beta']


def kernel(**inputs):
    import numpy as _np
    import concourse.bacc as _bacc
    from concourse import mybir as _mybir
    from concourse.bass_utils import run_bass_kernel_spmd as _run

    nc = _bacc.Bacc("TRN2", target_bir_lowering=False, num_devices=1)
    arrays, args = {}, []
    for name in _INS:
        a = _np.ascontiguousarray(inputs[name])
        arrays[f"in_{name}_dram"] = a
        args.append(nc.dram_tensor(f"in_{name}_dram", a.shape, _mybir.dt.from_np(a.dtype), kind="ExternalInput").ap())
    args.append(nc.dram_tensor("out_dram", (N, D), F32, kind="ExternalOutput").ap())
    gnn_kernel(nc, *args)
    r = _run(nc, [arrays], core_ids=[0])
    return r.results[0]["out_dram"]
```

```python
from contextlib import ExitStack

import numpy as np

import concourse.bass as bass
from concourse import mybir

P = 128
N, E, D, ED = 6250, 100000, 256, 64
NT = -(-N // P)
NPAD = NT * P
LAST_ROWS = N - (NT - 1) * P
ET = -(-E // P)
TAIL = E - (ET - 1) * P
UNROLL = 16
NS = -(-(ET + NT - 1) // UNROLL) * UNROLL
SB = -(-NS // P)
H, C = 8, D // 8
H0, C0 = 4, D // 4
C1 = C + 1
AW = H * C1
CH = P // H
CB = NS // CH
SEQ = CB * P
G = P // H
NG = NS // G
CF = 8
RW = P + 3
KT = D // P
FF = 4 * D
FT = FF // P
EW = 32 + H
EPS = 1e-5
BIG = 1e30
NOWHERE = 1 << 20

F32 = mybir.dt.float32
BF16 = mybir.dt.bfloat16
I32 = mybir.dt.int32
ALU = mybir.AluOpType
ACT = mybir.ActivationFunctionType
AX = mybir.AxisListType
ds = bass.ds


class Kept:
    pass


def wait(eng, sem, value):
    if not isinstance(value, int) or value > 0:
        eng.wait_ge(sem, value)


def ticks(eng, total, unroll, lag, body, peel=1):
    groups = total // unroll
    for it in range(peel):
        for u in range(unroll):
            body(it, u)
    with eng.Fori(peel, groups) as it:
        for u in range(unroll):
            body(it, u)
    for u in range(total - groups * unroll + lag):
        body(groups, u)


def live(it, c, unroll, total):
    return not isinstance(it, int) or 0 <= it * unroll + c < total


def fills(it, c, unroll, ring):
    return it * (unroll // ring) + c // ring + 1


class Chain:

    def __init__(self, eng, sem):
        self.eng, self.sem, self.n = eng, sem, 0

    def __call__(self, ins):
        self.n += 1
        ins.then_inc(self.sem, 1)
        self.eng.wait_ge(self.sem, self.n)


def walk_tables(nc, k, src, dst, ew, x, xr):
    with ExitStack() as c:
        sb = lambda name, shape, dt=F32: c.enter_context(nc.sbuf_tensor(name, shape, dt))
        sem = lambda name: c.enter_context(nc.semaphore(name))
        pad_row = sb("pad_row", [2, 4 * P], I32)
        same_i = sb("same_i", [P, NS], I32)
        pad_key = sb("pad_key", [1, P])
        last_dst = sb("last_dst", [1, ET], I32)
        last_shr = sb("last_shr", [1, ET], I32)
        last_f = sb("last_f", [1, 2, ET])
        tile_i = sb("tile_i", [1, ET], I32)
        step_i = sb("step_i", [P, SB], I32)
        step_col = sb("step_col", [P, SB])
        node_i = sb("node_i", [P, NT], I32)
        node_col = sb("node_col", [P, NT])
        less = sb("less", [P, ET])
        node_half = sb("node_half", [P, NT])
        sign = sb("sign", [P, 2, ET])
        i_col = sb("i_col", [P, SB])
        j_col = sb("j_col", [P, SB])
        base_col = sb("base_col", [P, SB])
        jbase = sb("jbase", [P, SB])
        i_idx = sb("i_idx", [P, SB], I32)
        ij_row = sb("ij_row", [SB, 2, P], I32)
        before = sb("before", [P, NT])
        before_idx = sb("before_idx", [P, NT], I32)
        lo = sb("lo", [P, NT])
        lo_row = sb("lo_row", [NT, P])
        lo_next = sb("lo_next", [NT, P])
        deg_row = sb("deg_row", [NT, P])
        end_row = sb("end_row", [1, P])
        rows = sb("rows", [P, 2, 4 * P], I32)
        nrows = sb("nrows", [P, 4, 4 * P], I32)
        ncmp = sb("ncmp", [P, P])
        rowf = sb("rowf", [P, 2, 5, P])
        d1 = sb("d1", [P, P])
        ge0 = sb("ge0", [P, P])
        valid = sb("valid", [P, P])
        pv = c.enter_context(nc.psum_tensor("pv", [P, 2, 2, 512], F32))
        pt = [c.enter_context(nc.psum_tensor(f"ptab{n}", [P, 4, P], F32)) for n in range(2)]

        s_pad, s_tail, s_last, s_tab, s_io = sem("pad"), sem("tail"), sem("last"), sem("tab"), sem("io")
        s_key0 = sem("padkey")
        s_xpad, s_x = sem("xpad"), sem("x_")
        s_ij, s_ijrow, s_ijback = sem("ij"), sem("ijrow"), sem("ijback")
        s_v, s_bcast, s_vec = sem("v"), sem("bcast"), sem("vec")
        s_idx = sem("idx")
        s_rowf, s_rowt, s_rowc, s_key = sem("rowf"), sem("rowt"), sem("rowc"), [sem(f"key{n}") for n in range(2)]
        s_nh, s_sign, s_summed = sem("nh"), sem("sign_"), sem("summed")
        s_bidx, s_ncnt = sem("bidx"), sem("ncnt")
        s_lo, s_lot, s_lor, s_lod, s_lon, s_degr, s_degt, s_deg = (
            sem("lo_"), sem("lot"), sem("lor"), sem("lod"), sem("lon"), sem("degr"), sem("degt"), sem("deg"))
        s_act = sem("actc")
        full = (ET - 1) * P
        HALF = ET // 2
        NC = 7

        with nc.Block() as block:
            @block.sync
            def _(sp):
                tab = k.tab.ap()
                parts = [dst, src, ew.bitcast(I32), dst]
                for n, a in enumerate(parts):
                    sp.dma_start(tab[0:ET - 1, n * P:(n + 1) * P],
                                 a[0:full].rearrange("(i p) -> i p", p=P)).then_inc(s_tab, 16)
                    sp.dma_start(tab[ET - 1:ET, (n + 1) * P - TAIL:(n + 1) * P],
                                 a[full:E].rearrange("(i p) -> i p", i=1)).then_inc(s_tab, 16)
                sp.dma_start(last_dst[0:1, 0:ET - 1],
                             dst[0:full].rearrange("(i p) -> p i", p=P)[P - 1:P, :]).then_inc(s_last, 16)
                sp.dma_start(last_dst[0:1, ET - 1:ET],
                             dst[E - 1:E].rearrange("(a b) -> a b", a=1)).then_inc(s_last, 16)
                sp.wait_ge(s_pad, 4)
                for n in range(3):
                    sp.dma_start(tab[ET - 1:ET, n * P:(n + 1) * P - TAIL],
                                 pad_row[0:1, n * P:(n + 1) * P - TAIL]).then_inc(s_tab, 16)
                sp.dma_start(tab[ET - 1:ET, 3 * P:4 * P - TAIL].rearrange("a b -> b a"),
                             dst[full - 1:full].rearrange("(a b) -> a b", a=1).to_broadcast([P - TAIL, 1])
                             ).then_inc(s_tab, 16)
                sp.dma_start(tab[ET:ET + 1, :], pad_row[0:1, :]).then_inc(s_tab, 16)
                sp.dma_start(k.keys.ap()[0:P].rearrange("(a b) -> a b", a=1),
                             pad_key[:, :]).then_inc(s_key0, 16)
                sp.wait_ge(s_ijrow, 1)
                sp.dma_start(k.ij.ap().rearrange("a (b p) -> b a p", p=P), ij_row[:, :, :]).then_inc(s_ij, 16)
                sp.wait_ge(s_ij, 16)
                sp.dma_start(k.step_base[0:1, :], k.ij.ap()[0:1, 0:NS]).then_inc(s_ijback, 16)
                sp.dma_start(k.step_j[0:1, :], k.ij.ap()[1:2, 0:NS]).then_inc(s_ijback, 16)
                sp.dma_start(same_i[:, :], k.ij.ap()[1:2, 0:NS].to_broadcast([P, NS])).then_inc(s_ijback, 16)
                for b in range(SB):
                    sp.wait_ge(s_rowf, b + 1)
                    sp.dma_start(k.keys.ap()[P + b * P * P:P + (b + 1) * P * P].rearrange("(s e) -> s e", e=P),
                                 rowf[:, b % 2, 4, :]).then_inc(s_key[b % 2], 16)
                whole = (NT - 1) * P
                sp.wait_ge(s_xpad, 1)
                sp.dma_start(xr[:, 0:(NT - 1) * D].rearrange("p (t d) -> p t d", d=D),
                             x[0:whole, :].rearrange("(t p) d -> p t d", p=P)).then_inc(s_x, 16)
                sp.dma_start(xr[0:LAST_ROWS, (NT - 1) * D:NT * D], x[whole:N, :]).then_inc(s_x, 16)
                sp.wait_ge(s_lor, 2)
                sp.dma_start(k.lod.ap()[0:NPAD].rearrange("(t p) -> t p", p=P), lo_row[:, :]).then_inc(s_lod, 16)
                sp.dma_start(k.lod.ap()[NPAD:NPAD + P].rearrange("(t p) -> t p", p=P),
                             end_row[:, :]).then_inc(s_lod, 16)
                sp.wait_ge(s_lod, 32)
                sp.dma_start(lo_next[:, :], k.lod.ap()[1:NPAD + 1].rearrange("(t p) -> t p", p=P)).then_inc(s_lon, 16)
                sp.wait_ge(s_key0, 16)
                sp.wait_ge(s_ijback, 48)
                sp.wait_ge(s_key[0], 16 * ((SB + 1) // 2))
                sp.wait_ge(s_key[1], 16 * (SB // 2))
                sp.wait_ge(s_x, 32)

            @block.gpsimd
            def _(pool):
                nc.gpsimd.memset(pad_row[:, :], 0).then_inc(s_pad, 1)
                nc.gpsimd.memset(xr[:, (NT - 1) * D:NT * D], 0.0).then_inc(s_xpad, 1)
                pool.wait_ge(s_pad, 1)
                nc.gpsimd.memset(pad_row[:, 0:P], NOWHERE)
                nc.gpsimd.memset(pad_row[:, 3 * P:4 * P], NOWHERE).then_inc(s_pad, 1)
                nc.gpsimd.memset(pad_key[:, :], -5.0).then_inc(s_pad, 1)
                nc.gpsimd.memset(end_row[:, :], float(E)).then_inc(s_pad, 1)
                nc.gpsimd.iota(tile_i[:, :], [[1, ET]], base=0, channel_multiplier=0).then_inc(s_io, 1)
                nc.gpsimd.iota(step_i[:, :], [[P, SB]], base=0, channel_multiplier=1).then_inc(s_io, 1)
                nc.gpsimd.iota(node_i[:, :], [[P, NT]], base=0, channel_multiplier=1).then_inc(s_io, 1)
                nc.gpsimd.iota(k.iota_i[:, :], [[1, P]], base=0, channel_multiplier=0).then_inc(s_io, 1)
                nc.gpsimd.memset(k.ident[:, :], 0.0).then_inc(s_io, 1)
                nc.gpsimd.memset(k.ones[:, :], 1.0).then_inc(s_io, 1)
                pool.wait_ge(s_io, 6)
                nc.gpsimd.affine_select(out=k.ident[:, :], in_=k.ident[:, :], compare_op=ALU.not_equal, fill=1.0,
                                        base=0, pattern=[[-1, P]], channel_multiplier=1).then_inc(s_io, 1)
                pool.wait_ge(s_tab, 16 * 13)
                pool.wait_ge(s_idx, 1)
                for b in range(SB):
                    if b >= 2:
                        pool.wait_ge(s_rowf, b - 1)
                    pool.indirect_dma_start(rows[:, b % 2, :], None, k.tab.ap(),
                                            bass.IndirectOffsetOnAxis(i_idx[:, b:b + 1], 0)).then_inc(k.got[b % 2], 16)
                for t in range(NT):
                    if t % NC == 0:
                        pool.wait_ge(s_bidx, t // NC + 1)
                    if t >= 4:
                        pool.wait_ge(s_ncnt, t - 3)
                    pool.indirect_dma_start(nrows[:, t % 4, :], None, k.tab.ap(),
                                            bass.IndirectOffsetOnAxis(before_idx[:, t:t + 1], 0)).then_inc(k.got[4 + t % 4], 16)

            @block.tensor
            def _(pe):
                pe.wait_ge(s_io, 7)
                pe.wait_ge(s_v, 1)
                for n in range(2):
                    for h in range(2):
                        last = nc.tensor.matmul(pv[:, n, h, 0:HALF], k.ones[0:1, :],
                                                last_f[0:1, n, h * HALF:(h + 1) * HALF], start=True, stop=True)
                last.then_inc(s_bcast, 1)
                pe.wait_ge(s_idx, 1)
                nc.tensor.transpose(pt[0][0:SB, 0, :], base_col[:, :], k.ident[:, :])
                nc.tensor.transpose(pt[0][0:SB, 1, :], j_col[:, :], k.ident[:, :]).then_inc(s_bcast, 1)
                pe.wait_ge(s_ijrow, 1)
                for b in range(SB):
                    pe.wait_ge(s_rowf, b + 1)
                    if b >= 2:
                        pe.wait_ge(s_rowc, b - 1)
                    for n in range(4):
                        last = nc.tensor.transpose(pt[b % 2][:, n, :], rowf[:, b % 2, n, :], k.ident[:, :])
                    last.then_inc(s_rowt, 1)
                pe.wait_ge(s_lo, 1)
                pe.wait_ge(s_rowc, SB)
                nc.tensor.transpose(pt[0][0:NT, 0, :], lo[:, :], k.ident[:, :]).then_inc(s_lot, 1)
                pe.wait_ge(s_degr, 1)
                nc.tensor.transpose(pt[1][:, 0, 0:NT], deg_row[:, :], k.ident[0:NT, 0:NT]).then_inc(s_degt, 1)

            @block.scalar
            def _(act):
                act.wait_ge(s_bcast, 2)
                nc.scalar.activation(ij_row[:, :, :], pt[0][0:SB, 0:2, :], ACT.Copy).then_inc(s_ijrow, 1)
                for b in range(SB):
                    act.wait_ge(s_rowt, b + 1)
                    w = min(P, NS - b * P)
                    for n, to in enumerate((k.drel, k.neg, k.weight, k.src)):
                        last = nc.scalar.activation(to[:, b * P:b * P + w], pt[b % 2][:, n, 0:w], ACT.Copy)
                    last.then_inc(s_rowc, 1)
                act.wait_ge(s_nh, 1)
                for t in range(NT):
                    wait(act, s_summed, t - 1)
                    nc.scalar.activation(sign[:, t % 2, :].rearrange("p (h n) -> p h n", h=2), pv[:, 1, :, 0:HALF],
                                         ACT.Sign, bias=node_half[:, t:t + 1], scale=-1.0).then_inc(s_sign, 1)
                act.wait_ge(s_lot, 1)
                nc.scalar.activation(lo_row[:, :], pt[0][0:NT, 0, :], ACT.Copy).then_inc(s_lor, 1)
                act.wait_ge(s_pad, 4)
                act.sem_inc(s_lor, 1)
                act.wait_ge(s_degt, 1)
                nc.scalar.activation(k.deg[:, :], pt[1][:, 0, 0:NT], ACT.Copy).then_inc(s_deg, 1)

            @block.vector
            def _(dve):
                v = Chain(dve, s_vec)
                dve.wait_ge(s_io, 4)
                v(nc.vector.tensor_copy(k.iota[:, :], k.iota_i[:, :]))
                v(nc.vector.tensor_copy(step_col[:, :], step_i[:, :]))
                v(nc.vector.tensor_copy(node_col[:, :], node_i[:, :]))
                nc.vector.tensor_scalar(node_half[:, :], node_col[:, :], 0.5, None, ALU.subtract).then_inc(s_nh, 1)
                dve.wait_ge(s_last, 32)
                v(nc.vector.tensor_single_scalar(last_shr[:, :], last_dst[:, :], 7, op=ALU.logical_shift_right))
                v(nc.vector.tensor_copy(last_f[:, 0, :], last_shr[:, :]))
                v(nc.vector.tensor_copy(last_f[:, 1, :], tile_i[:, :]))
                v(nc.vector.tensor_tensor(last_f[:, 0, :], last_f[:, 0, :], last_f[:, 1, :], ALU.add))
                v(nc.vector.tensor_copy(last_f[:, 1, :], last_dst[:, :]))
                dve.sem_inc(s_v, 1)
                dve.wait_ge(s_bcast, 1)
                less2 = less[:, :].rearrange("p (h n) -> p h n", h=2)
                for b in range(SB):
                    v(nc.vector.tensor_scalar(less2, pv[:, 0, :, 0:HALF], step_col[:, b:b + 1], None, ALU.is_lt))
                    v(nc.vector.tensor_reduce(i_col[:, b:b + 1], less[:, :], AX.X, ALU.add))
                v(nc.vector.tensor_tensor(j_col[:, :], step_col[:, :], i_col[:, :], ALU.subtract))
                v(nc.vector.tensor_scalar_min(j_col[:, :], j_col[:, :], float(NT - 1)))
                v(nc.vector.tensor_scalar(base_col[:, :], i_col[:, :], float(P), float(E - P), ALU.mult, ALU.min))
                v(nc.vector.tensor_scalar(jbase[:, :], j_col[:, :], float(P), None, ALU.mult))
                v(nc.vector.tensor_copy(i_idx[:, :], i_col[:, :]))
                dve.sem_inc(s_idx, 1)
                for b in range(SB):
                    dve.wait_ge(k.got[b % 2], 16 * (b // 2 + 1))
                    if b >= 2:
                        dve.wait_ge(s_key[b % 2], 16 * (b // 2))
                        dve.wait_ge(s_rowt, b - 1)
                    r, f = rows[:, b % 2, :], rowf[:, b % 2, :, :]
                    v(nc.vector.tensor_scalar(f[:, 0, :], r[:, 0:P], jbase[:, b:b + 1], None, ALU.subtract))
                    v(nc.vector.tensor_scalar(ge0[:, :], f[:, 0, :], 0.0, None, ALU.is_ge))
                    v(nc.vector.scalar_tensor_tensor(out=valid[:, :], in0=f[:, 0, :], scalar=float(P), in1=ge0[:, :],
                                                     op0=ALU.is_lt, op1=ALU.mult))
                    v(nc.vector.tensor_scalar(f[:, 1, :], valid[:, :], BIG, -BIG, ALU.mult, ALU.add))
                    v(nc.vector.tensor_scalar(d1[:, :], r[:, 3 * P:4 * P], jbase[:, b:b + 1], None, ALU.subtract))
                    v(nc.vector.tensor_scalar(ge0[:, :], d1[:, :], 0.0, None, ALU.is_ge))
                    v(nc.vector.scalar_tensor_tensor(out=valid[:, :], in0=d1[:, :], scalar=float(P), in1=ge0[:, :],
                                                     op0=ALU.is_lt, op1=ALU.mult))
                    v(nc.vector.tensor_scalar(d1[:, :], r[:, 3 * P:4 * P], 1.0, None, ALU.add))
                    v(nc.vector.tensor_tensor(f[:, 4, :], d1[:, :], valid[:, :], ALU.mult))
                    v(nc.vector.tensor_scalar(f[:, 2, :], r[:, 2 * P:3 * P].bitcast(F32), float(C) ** -0.5, None, ALU.mult))
                    v(nc.vector.tensor_copy(f[:, 3, :], r[:, P:2 * P]))
                    dve.sem_inc(s_rowf, 1)
                dve.wait_ge(s_ijback, 48)
                v(nc.vector.tensor_tensor(k.same[:, 1:NS], same_i[:, 1:NS], same_i[:, 0:NS - 1], ALU.is_equal))
                v(nc.vector.memset(k.same[:, 0:1], 0.0))
                for c0 in range(0, NT + NC, NC):
                    if c0 < NT:
                        cs = slice(c0, c0 + NC)
                        for t in range(c0, c0 + NC):
                            dve.wait_ge(s_sign, t + 1)
                            nc.vector.tensor_reduce(before[:, t:t + 1], sign[:, t % 2, :], AX.X, ALU.add
                                                    ).then_inc(s_summed, 1)
                        dve.wait_ge(s_summed, c0 + NC)
                        v(nc.vector.tensor_scalar(before[:, cs], before[:, cs], float(ET), 0.5, ALU.add, ALU.mult))
                        v(nc.vector.tensor_copy(before_idx[:, cs], before[:, cs]))
                        dve.sem_inc(s_bidx, 1)
                    if c0:
                        for t in range(c0 - NC, c0):
                            dve.wait_ge(k.got[4 + t % 4], 16 * (t // 4 + 1))
                            v(nc.vector.tensor_scalar(ncmp[:, :], nrows[:, t % 4, 0:P], node_col[:, t:t + 1], None,
                                                      ALU.is_lt))
                            v(nc.vector.tensor_reduce(lo[:, t:t + 1], ncmp[:, :], AX.X, ALU.add))
                            dve.sem_inc(s_ncnt, 1)
                v(nc.vector.scalar_tensor_tensor(out=lo[:, :], in0=before[:, :], scalar=float(P), in1=lo[:, :],
                                                 op0=ALU.mult, op1=ALU.add))
                v(nc.vector.tensor_scalar_min(lo[:, :], lo[:, :], float(E)))
                dve.sem_inc(s_lo, 1)
                dve.wait_ge(s_lon, 16)
                v(nc.vector.tensor_tensor(deg_row[:, :], lo_next[:, :], lo_row[:, :], ALU.subtract))
                dve.sem_inc(s_degr, 1)
                dve.wait_ge(s_deg, 1)
                v(nc.vector.tensor_scalar_max(k.deg1[:, :], k.deg[:, :], 1.0))

    for n in range(2):
        k.seen[n] += 16 * len(range(n, SB, 2))
    for n in range(4):
        k.seen[4 + n] += 16 * len(range(n, NT, 4))
    with ExitStack() as c:
        s_sq, s_di = c.enter_context(nc.semaphore("sq")), c.enter_context(nc.semaphore("di"))
        with nc.Block() as block:
            @block.scalar
            def _(act):
                nc.scalar.activation(k.dis[:, :], k.deg1[:, :], ACT.Sqrt).then_inc(s_sq, 1)

            @block.vector
            def _(dve):
                v = Chain(dve, s_di)
                dve.wait_ge(s_sq, 1)
                v(nc.vector.reciprocal(k.dis[:, :], k.dis[:, :]))
                v(nc.vector.tensor_scalar_min(k.deg1[:, :], k.deg[:, :], 1.0))
                v(nc.vector.tensor_tensor(k.dis[:, :], k.dis[:, :], k.deg1[:, :], ALU.mult))


def globals_of(nc, c):
    sb = lambda name, shape, dt=F32: c.enter_context(nc.sbuf_tensor(name, shape, dt))
    c.enter_context(nc.allow_non_contiguous_dma(reason="a few small strided loads of indices and columns"))
    k = Kept()
    k.got = [c.enter_context(nc.semaphore(f"got{n}")) for n in range(8)]
    k.seen = [0] * 8
    k.tab = nc.dram_tensor("edge_rows", [ET + 1, 4 * P], I32)
    k.keys = nc.dram_tensor("keys", [P + SB * P * P], F32)
    k.runs = nc.dram_tensor("runs", [NS * H, RW], F32)
    k.ij = nc.dram_tensor("steps_ij", [2, SB * P], I32)
    k.lod = nc.dram_tensor("first_edge", [NPAD + P], F32)
    k.ident = sb("ident", [P, P])
    k.iota = sb("iota", [P, P])
    k.iota_i = sb("iota_i", [P, P], I32)
    k.ones = sb("ones", [1, P])
    k.drel = sb("drel", [P, NS])
    k.neg = sb("neg", [P, NS])
    k.weight = sb("weight", [P, NS])
    k.src = sb("srct", [P, NS], I32)
    k.same = sb("same", [P, NS])
    k.step_j = sb("step_j", [1, NS], I32)
    k.step_base = sb("step_base", [1, NS], I32)
    k.smask = sb("smask", [P, G])
    k.hmask = sb("hmask", [P, H])
    k.hmask_t = sb("hmask_t", [H, P])
    k.deg = sb("deg_", [P, NT])
    k.deg1 = sb("deg1", [P, NT])
    k.dis = sb("dis", [P, NT])
    k.eps = sb("eps", [P, 1])
    k.rs = sb("rs", [P, NT])
    k.nb = sb("nb", [P, NT])
    k.rs_x = sb("rs_x", [P, NT])
    k.nb_x = sb("nb_x", [P, NT])
    k.st = sb("bn_st", [P, NT * 6])
    k.acc = sb("acc", [P, 2 * SEQ])
    return k


def row_stats(nc, tag, k, x, kept=False):
    TG = 7
    rs, nb = (k.rs_x, k.nb_x) if kept else (k.rs, k.nb)
    with ExitStack() as c:
        sb = lambda name, shape, dt=F32: c.enter_context(nc.sbuf_tensor(f"{tag}_{name}", shape, dt))
        sem = lambda name: c.enter_context(nc.semaphore(f"{tag}_{name}"))
        mv = sb("bn_mv", [P, NT, 2])
        s_vec, s_var, s_std = sem("rs_vec"), sem("rs_var"), sem("rs_std")
        with nc.Block() as block:
            @block.vector
            def _(dve):
                v = Chain(dve, s_vec)
                if x is not None:
                    with dve.Fori(0, NT // TG) as it:
                        for u in range(TG):
                            nc.vector.bn_stats(k.st[:, ds(it * (6 * TG) + 6 * u, 6)], x[:, ds(it * (TG * D) + u * D, D)])
                    dve.drain()
                v(nc.vector.memset(k.eps[:, :], EPS))
                for t in range(NT):
                    last = nc.vector.bn_aggr(mv[:, t, :], k.st[:, 6 * t:6 * t + 6])
                last.then_inc(s_var, 1)
                dve.wait_ge(s_std, 1)
                v(nc.vector.reciprocal(rs[:, :], rs[:, :]))
                v(nc.vector.scalar_tensor_tensor(out=nb[:, :], in0=mv[:, :, 0], scalar=-1.0, in1=rs[:, :],
                                                 op0=ALU.mult, op1=ALU.mult))

            @block.scalar
            def _(act):
                act.wait_ge(s_var, 1)
                nc.scalar.activation(rs[:, :], mv[:, :, 1], ACT.Sqrt, bias=k.eps[:, 0:1]).then_inc(s_std, 1)


def normalized(nc, tag, k, x, y, func, rs, nb, stats):
    with nc.semaphore(f"{tag}_norm") as s_norm, nc.Block() as block:
        @block.scalar
        def _(act):
            def body(it, u):
                t = it * 7 + u
                nc.scalar.activation(y[:, ds(t * D, D)], x[:, ds(t * D, D)], func, bias=nb[:, ds(t, 1)],
                                     scale=rs[:, ds(t, 1)]).then_inc(s_norm, 1)
            ticks(act, NT, 7, 0, body)
            act.wait_ge(s_norm, NT)

        if stats:
            @block.vector
            def _(dve):
                def body(it, u):
                    t = it * 7 + u
                    dve.wait_ge(s_norm, t + 1)
                    nc.vector.bn_stats(k.st[:, ds(t * 6, 6)], y[:, ds(t * D, D)])
                ticks(dve, NT, 7, 0, body)


def project(nc, tag, k, x, func, outs):
    U = 4
    nout = len(outs)
    PB = 2
    OB = 4
    with ExitStack() as c:
        sb = lambda name, shape, dt=F32: c.enter_context(nc.sbuf_tensor(f"{tag}_{name}", shape, dt))
        sem = lambda name: c.enter_context(nc.semaphore(f"{tag}_{name}"))
        z = sb("pj_z", [P, 2, D])
        zt = sb("pj_zt", [P, 2, D])
        pt = [c.enter_context(nc.psum_tensor(f"{tag}_pj_t{n}", [P, 512], F32)) for n in range(2)]
        po = [[c.enter_context(nc.psum_tensor(f"{tag}_pj_o{m}_{n}", [P, 512], F32)) for n in range(PB)] for m in range(nout)]
        ob = [sb(f"pj_b{m}", [P, OB, o[2]]) if o[5] is None else None for m, o in enumerate(outs)]
        s_z, s_t, s_zt, s_o, s_ev = sem("pj_sz"), sem("pj_st"), sem("pj_szt"), sem("pj_so"), sem("pj_ev")
        stored = [sem(f"pj_store{n}") for n in range(OB)]
        nst = sum(len(o[4]) for o in outs)
        biased = outs[0][1] is not None

        def results(eng, it, u):
            r = u - 2
            if live(it, r, U, NT):
                s = it * U + r
                eng.wait_ge(s_o, s + 1)
                if nst:
                    wait(eng, stored[r % OB], (it + r // OB) * (16 * nst))
                for m, (w, b, width, col, st, target) in enumerate(outs):
                    scale = 1.0 if col is None else col[:, ds(s, 1)]
                    o = ob[m][:, r % OB, :] if target is None else target[:, ds(s * width, width)]
                    if biased:
                        last = nc.vector.tensor_tensor(o, po[m][r % PB][:, 0:width], b, ALU.add)
                    else:
                        last = nc.scalar.activation(o, po[m][r % PB][:, 0:width], ACT.Copy, scale=scale)
                last.then_inc(s_ev, 1)

        with nc.Block() as block:
            @block.scalar
            def _(act):
                def body(it, u):
                    t = it * U + u
                    if live(it, u, U, NT):
                        wait(act, s_t, t - 1)
                        nc.scalar.activation(z[:, u % 2, :], x[:, ds(t * D, D)], func, bias=k.nb[:, ds(t, 1)],
                                             scale=k.rs[:, ds(t, 1)]).then_inc(s_z, 1)
                    if not biased:
                        results(act, it, u)
                ticks(act, NT, U, 2, body, 2)
                act.wait_ge(s_ev, NT)

            @block.vector
            def _(dve):
                def body(it, u):
                    t = it * U + u
                    if live(it, u, U, NT):
                        dve.wait_ge(s_t, t + 1)
                        wait(dve, s_o, t - 1)
                        nc.vector.tensor_copy(zt[:, u % 2, :], pt[u % 2][:, 0:D]).then_inc(s_zt, 1)
                    if biased:
                        results(dve, it, u)
                ticks(dve, NT, U, 2, body, 2)

            @block.tensor
            def _(pe):
                def body(it, u):
                    t = it * U + u
                    if live(it, u, U, NT):
                        pe.wait_ge(s_z, t + 1)
                        wait(pe, s_zt, t - 1)
                        for n in range(KT):
                            last = nc.tensor.transpose(pt[u % 2][:, n * P:(n + 1) * P], z[:, u % 2, n * P:(n + 1) * P],
                                                       k.ident[:, :])
                        last.then_inc(s_t, 1)
                    r = u - 1
                    if live(it, r, U, NT):
                        s = it * U + r
                        pe.wait_ge(s_zt, s + 1)
                        wait(pe, s_ev, s - PB + 1)
                        for m, (w, b, width, col, st, target) in enumerate(outs):
                            o = po[m][r % PB][:, 0:width]
                            for n in range(KT):
                                last = nc.tensor.matmul(o, zt[:, r % 2, n * P:(n + 1) * P], w[:, n, :],
                                                        start=(n == 0), stop=(n == KT - 1))
                        last.then_inc(s_o, 1)
                ticks(pe, NT, U, 1, body)

            @block.sync
            def _(sp):
                def body(it, u):
                    t = it * U + u
                    if nst and live(it, u, U, NT):
                        sp.wait_ge(s_ev, t + 1)
                        for m, (w, b, width, col, st, target) in enumerate(outs):
                            for first, cols, table in st:
                                sp.dma_start(table[ds(t * P, P), :],
                                             ob[m][:, u % OB, first:first + cols]).then_inc(stored[u % OB], 16)
                if nst:
                    ticks(sp, NT, U, 0, body)
                    for n in range(OB):
                        sp.wait_ge(stored[n], 16 * nst * len(range(n, NT, OB)))


def aggregate(nc, tag, k, table, weights):
    R, W, LAG = 8, 4, 2
    width = AW if weights else D
    with ExitStack() as c:
        sb = lambda name, shape, dt=F32: c.enter_context(nc.sbuf_tensor(f"{tag}_{name}", shape, dt))
        sem = lambda name: c.enter_context(nc.semaphore(f"{tag}_{name}"))
        idx = sb("ag_idx", [P, 2, UNROLL // 2], I32)
        got = sb("ag_got", [P, R, width])
        sel = sb("ag_sel", [P, W, P])
        wgt = sb("ag_wgt", [P, W, AW]) if weights else None
        cur = sb("ag_cur", [P, W, AW])
        pa = [c.enter_context(nc.psum_tensor(f"{tag}_ag_p{n}", [P, 512], F32)) for n in range(W)]
        s_idx, s_turn, s_got = sem("ag_si"), sem("ag_turn"), k.got
        s_rhs, s_mm, s_cur, s_acc, s_init = (sem("ag_rhs"), sem("ag_mm"), sem("ag_scur"), sem("ag_acc"),
                                             sem("ag_init"))
        s_used = s_rhs if weights else s_mm
        with nc.Block() as block:
            @block.gpsimd
            def _(pool):
                half = UNROLL // 2

                def body(it, u):
                    t = it * UNROLL + u
                    if u % half == 0:
                        h = u // half
                        nc.gpsimd.tensor_copy(idx[:, h, :], k.src[:, ds(t, half)]).then_inc(s_idx, 1)
                        pool.wait_ge(s_idx, it * 2 + h + 1)
                    wait(pool, s_used, t - R + 1)
                    pool.sem_inc(s_turn, 1)
                    pool.indirect_dma_start(got[:, u % R, :], None, table,
                                            bass.IndirectOffsetOnAxis(idx[:, u // half, u % half:u % half + 1], 0)
                                            ).then_inc(s_got[u % R], 16)
                ticks(pool, NS, UNROLL, 0, body)

            @block.vector
            def _(dve):
                for n in range(W):
                    last = nc.vector.memset(cur[:, n, :], 0.0)
                last.then_inc(s_init, 1)
                dve.wait_ge(s_init, 1)

                def body(it, u):
                    t = it * UNROLL + u
                    if live(it, u, UNROLL, NS):
                        wait(dve, s_mm, t - W + 1)
                        last = nc.vector.tensor_scalar(sel[:, u % W, :], k.iota[:, :], k.drel[:, ds(t, 1)], None,
                                                       ALU.is_equal)
                        if weights:
                            dve.wait_ge(s_got[u % R], 16 * fills(it, u, UNROLL, R) + k.seen[u % R])
                            last = nc.vector.tensor_tensor(
                                wgt[:, u % W, :].rearrange("p (h c) -> p h c", h=H),
                                got[:, u % R, :].rearrange("p (h c) -> p h c", h=H),
                                k.edge[:, ds(t * H, H)].unsqueeze(2).to_broadcast([P, H, C1]), ALU.mult)
                        last.then_inc(s_rhs, 1)
                    r = u - LAG
                    if live(it, r, UNROLL, NS):
                        s = it * UNROLL + r
                        dve.wait_ge(s_mm, s + 1)
                        wait(dve, s_cur, s)
                        wait(dve, s_acc, s - W + 1)
                        nc.vector.scalar_tensor_tensor(
                            out=cur[:, r % W, 0:width], in0=cur[:, (r - 1) % W, 0:width], scalar=k.same[:, ds(s, 1)],
                            in1=pa[r % W][:, 0:width], op0=ALU.mult, op1=ALU.add).then_inc(s_cur, 1)
                ticks(dve, NS, UNROLL, LAG, body)

            @block.tensor
            def _(pe):
                def body(it, u):
                    t = it * UNROLL + u
                    pe.wait_ge(s_rhs, t + 1)
                    wait(pe, s_cur, t - W + 1)
                    if weights:
                        nc.tensor.matmul(pa[u % W][:, 0:AW], sel[:, u % W, :], wgt[:, u % W, :],
                                         start=True, stop=True).then_inc(s_mm, 1)
                    else:
                        pe.wait_ge(s_got[u % R], 16 * fills(it, u, UNROLL, R) + k.seen[u % R])
                        nc.tensor.matmul(pa[u % W][:, 0:D], sel[:, u % W, :], got[:, u % R, :],
                                         start=True, stop=True).then_inc(s_mm, 1)
                ticks(pe, NS, UNROLL, 0, body)

            @block.scalar
            def _(act):
                def body(it, u):
                    s = it * UNROLL + u
                    if u % 4 == 0:
                        _, act_j[0] = nc.values_load_multi_w_load_instructions(
                            k.step_j[0:1, ds(s, 4)], engines=(mybir.EngineType.Activation,), min_val=0, max_val=NT - 1,
                            skip_runtime_bounds_check_because="j(s) is clamped to the last node tile")
                    act.wait_ge(s_cur, s + 1)
                    wait(act, s_acc, s)
                    nc.scalar.activation(k.acc[:, ds(act_j[0][u % 4] * AW, width)], cur[:, u % W, 0:width],
                                         ACT.Copy).then_inc(s_acc, 1)
                act_j = [None]
                ticks(act, NS, UNROLL, 0, body)
                act.wait_ge(s_acc, NS)
    for n in range(R):
        k.seen[n] += 16 * (NS // R)


def layer0_edges(nc, k, xr, src, dst, t0, al0):
    TG = 7
    W0 = D + H0
    with ExitStack() as c:
        sb = lambda name, shape, dt=F32: c.enter_context(nc.sbuf_tensor(name, shape, dt))
        sem = lambda name: c.enter_context(nc.semaphore(name))
        er = sb("l0_er", [NT, 2, P], I32)
        erf = sb("l0_erf", [NT, 2, P])
        ei = sb("l0_ei", [P, 2, NT], I32)
        al = sb("l0_al", [P, NT, H0])
        lg = sb("l0_lg", [P, NT, H0])
        mx = sb("l0_mx", [P, NT])
        tmp = sb("l0_tmp", [P, TG, C0])
        got = k.acc[:, 0:NT * W0].rearrange("p (t w) -> p t w", w=W0)
        pt = c.enter_context(nc.psum_tensor("l0_pt", [P, 2, P], F32))
        s_ld, s_f, s_t, s_i = sem("l0_ld"), sem("l0_sf"), sem("l0_st"), sem("l0_si")
        s_got, s_ex, s_v, s_lg = k.got[0:NT // TG], sem("l0_ex"), sem("l0_v"), sem("l0_slg")
        with nc.Block() as block:
            @block.sync
            def _(sp):
                for n, a in enumerate((src, dst)):
                    sp.dma_start(er[:, n, :], a[0:NPAD].rearrange("(t p) -> t p", p=P)).then_inc(s_ld, 16)

            @block.tensor
            def _(pe):
                pe.wait_ge(s_f, 1)
                nc.tensor.transpose(pt[:, 0, 0:NT], erf[:, 0, :], k.ident[0:NT, 0:NT])
                nc.tensor.transpose(pt[:, 1, 0:NT], erf[:, 1, :], k.ident[0:NT, 0:NT]).then_inc(s_t, 1)

            @block.gpsimd
            def _(pool):
                pool.wait_ge(s_i, 1)
                for t in range(NT):
                    pool.indirect_dma_start(al[:, t, :], None, al0, bass.IndirectOffsetOnAxis(ei[:, 0, t:t + 1], 0)
                                            ).then_inc(s_got[t // TG], 16)
                    pool.indirect_dma_start(got[:, t, :], None, t0, bass.IndirectOffsetOnAxis(ei[:, 1, t:t + 1], 0)
                                            ).then_inc(s_got[t // TG], 16)

            @block.scalar
            def _(act):
                for g in range(NT // TG):
                    act.wait_ge(s_lg, g + 1)
                    ts = slice(g * TG, (g + 1) * TG)
                    nc.scalar.activation(lg[:, ts, :], lg[:, ts, :], ACT.Exp).then_inc(s_ex, 1)

            @block.vector
            def _(dve):
                v = Chain(dve, s_v)
                dve.wait_ge(s_ld, 32)
                v(nc.vector.tensor_copy(erf[:, :, :], er[:, :, :]))
                dve.sem_inc(s_f, 1)
                dve.wait_ge(s_t, 1)
                v(nc.vector.tensor_copy(ei[:, :, :], pt[:, :, 0:NT]))
                dve.sem_inc(s_i, 1)
                bc = lambda a: a.unsqueeze(2).to_broadcast([P, TG, H0])
                for g in range(NT // TG):
                    ts = slice(g * TG, (g + 1) * TG)
                    lgg, mxg = lg[:, ts, :], mx[:, ts]
                    dve.wait_ge(s_got[g], k.seen[g] + 32 * TG)
                    v(nc.vector.tensor_tensor(lgg, al[:, ts, :], got[:, ts, D:W0], ALU.add))
                    v(nc.vector.scalar_tensor_tensor(out=lgg, in0=lgg, scalar=0.01, in1=lgg, op0=ALU.mult, op1=ALU.max))
                    v(nc.vector.tensor_reduce(mxg, lgg, AX.X, ALU.max))
                    v(nc.vector.tensor_tensor(lgg, lgg, bc(mxg), ALU.subtract))
                    dve.sem_inc(s_lg, 1)
                    dve.wait_ge(s_ex, g + 1)
                    v(nc.vector.tensor_reduce(mxg, lgg, AX.X, ALU.add))
                    v(nc.vector.reciprocal(mxg, mxg))
                    v(nc.vector.tensor_tensor(lgg, lgg, bc(mxg), ALU.mult))
                    rows = got[:, ts, 0:D].rearrange("p t (h d) -> p t h d", h=H0)
                    v(nc.vector.tensor_tensor(rows, rows, lgg.unsqueeze(3).to_broadcast([P, TG, H0, C0]), ALU.mult))
                    v(nc.vector.tensor_reduce(tmp[:, :, :], got[:, ts, 0:D].rearrange("p t (h d) -> p t d h", h=H0),
                                              AX.X, ALU.add))
                    xv = xr[:, g * TG * D:(g + 1) * TG * D].rearrange("p (t h d) -> p t h d", t=TG, h=H0)
                    v(nc.vector.tensor_tensor(xv, xv, tmp[:, :, :].unsqueeze(2).to_broadcast([P, TG, H0, C0]), ALU.add))
                    for t in range(g * TG, (g + 1) * TG):
                        nc.vector.bn_stats(k.st[:, 6 * t:6 * t + 6], xr[:, t * D:(t + 1) * D])
    for g in range(NT // TG):
        k.seen[g] += 32 * TG


def add_scaled(nc, k, xr):
    with nc.semaphore("as_v") as s_v, nc.Block() as block:
        @block.vector
        def _(dve):
            def body(it, u):
                t = it * 7 + u
                if live(it, u, 7, NT):
                    nc.vector.scalar_tensor_tensor(out=xr[:, ds(t * D, D)], in0=k.acc[:, ds(t * AW, D)],
                                                   scalar=k.dis[:, ds(t, 1)], in1=xr[:, ds(t * D, D)],
                                                   op0=ALU.mult, op1=ALU.add).then_inc(s_v, 1)
                r = u - 1
                if live(it, r, 7, NT):
                    s = it * 7 + r
                    dve.wait_ge(s_v, s + 1)
                    nc.vector.bn_stats(k.st[:, ds(s * 6, 6)], xr[:, ds(s * D, D)])
            ticks(dve, NT, 7, 1, body)


def layer2_scores(nc, k, keys, queries, we, ef):
    R, W, EB = 8, 4, 4
    with ExitStack() as c:
        sb = lambda name, shape, dt=F32: c.enter_context(nc.sbuf_tensor(name, shape, dt))
        sem = lambda name: c.enter_context(nc.semaphore(name))
        half = UNROLL // 2
        idx = sb("sc_idx", [P, 2, half], I32)
        got = sb("sc_got", [P, R, D])
        sel = sb("sc_sel", [P, W, P])
        dist = sb("sc_dist", [P, 2, P])
        efr = sb("sc_ef", [P, EB, P])
        tr = sb("sc_tr", [P, 2, 2 * P])
        prod = sb("sc_prod", [P, W, D])
        epr = sb("sc_ep", [P, W, C])
        pt = [c.enter_context(nc.psum_tensor(f"sc_t{n}", [P, 512], F32)) for n in range(2)]
        pq = [c.enter_context(nc.psum_tensor(f"sc_q{n}", [P, 512], F32)) for n in range(W)]
        pw = [c.enter_context(nc.psum_tensor(f"sc_w{n}", [P, 512], F32)) for n in range(2)]
        s_idx, s_turn, s_got, s_ef = sem("sc_idx_"), sem("sc_turn"), k.got, [sem(f"sc_efs{n}") for n in range(EB)]
        s_dist = sem("sc_sdist")
        s_init, s_sel, s_tr, s_cp, s_q, s_key, s_prod, s_sc, s_ae = (
            sem("sc_init"), sem("sc_ssel"), sem("sc_str"), sem("sc_cp"), sem("sc_sq"), sem("sc_key"),
            sem("sc_sprod"), sem("sc_sc"), sem("sc_ae"))
        with nc.Block() as block:
            @block.gpsimd
            def _(pool):
                nc.gpsimd.memset(efr[:, :, :], 0.0).then_inc(s_init, 1)
                pool.wait_ge(s_init, 1)
                nc.gpsimd.memset(efr[:, :, ED:ED + 1], 1.0).then_inc(s_init, 1)

                def body(it, u):
                    t = it * UNROLL + u
                    if u % half == 0:
                        h = u // half
                        nc.gpsimd.tensor_copy(idx[:, h, :], k.src[:, ds(t, half)]).then_inc(s_idx, 1)
                        pool.wait_ge(s_idx, it * 2 + h + 1)
                    wait(pool, s_key, t - R + 1)
                    pool.sem_inc(s_turn, 1)
                    pool.indirect_dma_start(got[:, u % R, :], None, keys,
                                            bass.IndirectOffsetOnAxis(idx[:, u // half, u % half:u % half + 1], 0)
                                            ).then_inc(s_got[u % R], 16)
                ticks(pool, NS, UNROLL, 0, body)

            @block.sync
            def _(sp):
                base = [None]
                sp.wait_ge(s_init, 2)

                def body(it, u):
                    t = it * UNROLL + u
                    if u % 4 == 0:
                        _, base[0] = nc.values_load_multi_w_load_instructions(
                            k.step_base[0:1, ds(t, 4)], engines=(mybir.EngineType.SP,), min_val=0, max_val=E - P,
                            skip_runtime_bounds_check_because="the first edge of a tile is clamped to E - P")
                    wait(sp, s_tr, t - EB + 1)
                    sp.dma_start(efr[:, u % EB, 0:ED], ef[ds(base[0][u % 4], P), :]).then_inc(s_ef[u % EB], 16)
                ticks(sp, NS, UNROLL, 0, body)

            @block.vector
            def _(dve):
                heads = lambda a: a.rearrange("p (h c) -> p h c", h=H)

                def body(it, u):
                    a = u - 3
                    if live(it, a, UNROLL, NS):
                        s = it * UNROLL + a
                        dve.wait_ge(s_ae, s + 1)
                        dve.wait_ge(s_got[a % R], 16 * fills(it, a, UNROLL, R) + k.seen[a % R])
                        wait(dve, s_sc, s - W + 1)
                        nc.vector.tensor_tensor(
                            heads(prod[:, a % W, :]), heads(got[:, a % R, :]),
                            epr[:, a % W, :].unsqueeze(1).to_broadcast([P, H, C]), ALU.add).then_inc(s_key, 1)
                    b = u - 4
                    if live(it, b, UNROLL, NS):
                        s = it * UNROLL + b
                        dve.wait_ge(s_key, s + 1)
                        dve.wait_ge(s_q, s + 1)
                        nc.vector.tensor_tensor(prod[:, b % W, :], prod[:, b % W, :], pq[b % W][:, 0:D],
                                                ALU.mult).then_inc(s_prod, 1)
                    e = u - 5
                    if live(it, e, UNROLL, NS):
                        s = it * UNROLL + e
                        dve.wait_ge(s_prod, s + 1)
                        nc.vector.tensor_reduce(k.edge[:, ds(s * H, H)], heads(prod[:, e % W, :]), AX.X,
                                                ALU.add).then_inc(s_sc, 1)
                ticks(dve, NS, UNROLL, 5, body)
                dve.wait_ge(s_sc, NS)

            @block.tensor
            def _(pe):
                j = [None]

                def body(it, u):
                    t = it * UNROLL + u
                    if live(it, u, UNROLL, NS):
                        pe.wait_ge(s_sel, t + 1)
                        pe.wait_ge(s_ef[u % EB], 16 * fills(it, u, UNROLL, EB))
                        wait(pe, s_cp, t - 1)
                        nc.tensor.transpose(pt[u % 2][:, 0:P], sel[:, u % W, :], k.ident[:, :])
                        nc.tensor.transpose(pt[u % 2][:, P:2 * P], efr[:, u % EB, :], k.ident[:, :]).then_inc(s_tr, 1)
                    r = u - 1
                    if live(it, r, UNROLL, NS):
                        s = it * UNROLL + r
                        if r % 4 == 0 or j[0] is None or (u == 0):
                            first = s - r % 4
                            _, j[0] = nc.values_load_multi_w_load_instructions(
                                k.step_j[0:1, ds(first, 4)], engines=(mybir.EngineType.PE,), min_val=0, max_val=NT - 1,
                                skip_runtime_bounds_check_because="j(s) is clamped to the last node tile")
                        pe.wait_ge(s_cp, s + 1)
                        wait(pe, s_prod, s - W + 1)
                        wait(pe, s_ae, s - 1)
                        nc.tensor.matmul(pq[r % W][:, 0:D], tr[:, r % 2, 0:P], queries[:, ds(j[0][r % 4] * D, D)],
                                         start=True, stop=True)
                        nc.tensor.matmul(pw[r % 2][:, 0:EW], tr[:, r % 2, P:2 * P], we, start=True,
                                         stop=True).then_inc(s_q, 1)
                ticks(pe, NS, UNROLL, 1, body)

            @block.scalar
            def _(act):
                def body(it, u):
                    t = it * UNROLL + u
                    if live(it, u, UNROLL, NS):
                        wait(act, s_sel, t - 1)
                        nc.scalar.activation(dist[:, u % 2, :], k.iota[:, :], ACT.Abs, bias=k.drel[:, ds(t, 1)],
                                             scale=-1.0).then_inc(s_dist, 1)
                    e = u - 1
                    if live(it, e, UNROLL, NS):
                        s = it * UNROLL + e
                        act.wait_ge(s_tr, s + 1)
                        wait(act, s_q, s - 1)
                        nc.scalar.activation(tr[:, e % 2, :], pt[e % 2][:, 0:2 * P], ACT.Copy).then_inc(s_cp, 1)
                    if live(it, u, UNROLL, NS):
                        act.wait_ge(s_dist, t + 1)
                        wait(act, s_tr, t - W + 1)
                        nc.scalar.activation(sel[:, u % W, :], dist[:, u % 2, :], ACT.Relu, bias=1.0,
                                             scale=-1.0).then_inc(s_sel, 1)
                    r = u - 3
                    if live(it, r, UNROLL, NS):
                        s = it * UNROLL + r
                        act.wait_ge(s_q, s + 1)
                        wait(act, s_key, s - W + 1)
                        nc.scalar.activation(k.ae[:, ds(s * H, H)], pw[r % 2][:, C:EW], ACT.Copy)
                        nc.scalar.activation(epr[:, r % W, :], pw[r % 2][:, 0:C], ACT.Copy).then_inc(s_ae, 1)
                ticks(act, NS, UNROLL, 3, body)
                act.wait_ge(s_ae, NS)
    for n in range(R):
        k.seen[n] += 16 * (NS // R)


def run_flags(nc, k):
    R, S = NS // CF, CF
    with ExitStack() as c:
        sb = lambda name, shape, dt=F32: c.enter_context(nc.sbuf_tensor(name, shape, dt))
        keys = [sb(f"rf_k{n}", [R, S, P]) for n in range(3)]
        flags = sb("rf_f", [R, S, RW])
        s_ld, s_v, s_st = (c.enter_context(nc.semaphore(n)) for n in ("rf_ld", "rf_v", "rf_st"))
        with nc.Block() as block:
            @block.vector
            def _(dve):
                v = Chain(dve, s_v)
                v(nc.vector.tensor_reduce(k.smask[:, :], k.ident[:, :].rearrange("p (s h) -> p s h", h=H), AX.X, ALU.add))
                v(nc.vector.tensor_reduce(k.hmask[:, :], k.ident[:, :].rearrange("p (s h) -> p h s", h=H), AX.X, ALU.add))
                v(nc.vector.tensor_copy(k.hmask_t[:, :].rearrange("p (s h) -> p s h", h=H),
                                        k.ident[0:H, 0:H].unsqueeze(1).to_broadcast([H, G, H])))
                dve.wait_ge(s_ld, 48)
                own, later = flags[:, :, 0:P], keys[2][:, :, :]
                v(nc.vector.tensor_tensor(own, keys[1][:, :, :], keys[0][:, :, :], ALU.not_equal))
                v(nc.vector.tensor_tensor(later, keys[2][:, :, :], keys[1][:, :, :], ALU.not_equal))
                v(nc.vector.tensor_scalar(own, own, -BIG, None, ALU.mult))
                v(nc.vector.tensor_scalar(later, later, -BIG, None, ALU.mult))
                v(nc.vector.tensor_copy(flags[:, :, P:P + 1], keys[2][:, :, P - 1:P]))
                v(nc.vector.tensor_reduce(flags[:, :, P + 1], own, AX.X, ALU.min))
                v(nc.vector.tensor_reduce(flags[:, :, P + 2], later, AX.X, ALU.min))

            @block.sync
            def _(sp):
                for n in range(3):
                    sp.dma_start(keys[n][:, :, :], k.keys.ap()[P - 1 + n:P - 1 + n + NS * P]
                                 .rearrange("(r s e) -> r s e", r=R, s=S)).then_inc(s_ld, 16)
                sp.wait_ge(s_v, 10)
                for h in range(H):
                    sp.dma_start(k.runs.ap().rearrange("(r s h) n -> r s h n", s=S, h=H)[:, :, h, :],
                                 flags[:, :, :]).then_inc(s_st, 16)
                sp.wait_ge(s_st, 16 * H)


def layer3_edges(nc, k, table, a_dst):
    U, LAG = 2 * G, 3
    FW = G * H
    half = 8
    with ExitStack() as c:
        sb = lambda name, shape, dt=F32: c.enter_context(nc.sbuf_tensor(name, shape, dt))
        sem = lambda name: c.enter_context(nc.semaphore(name))
        idx = sb("le_idx", [P, U // half, half], I32)
        got = sb("le_got", [P, U, AW])
        sel = sb("le_sel", [P, U, P])
        tr = sb("le_tr", [P, 2, 4 * P], BF16)
        ae = sb("le_ae", [P, 2, FW])
        flags = sb("le_flags", [P, 2, RW])
        lg = sb("le_lg", [P, FW])
        ex = sb("le_ex", [P, 2, FW])
        part = sb("le_part", [P, 2 * P])
        run = sb("le_run", [P, P])
        mx = sb("le_mx", [P, P])
        cols = sb("le_cols", [P, 4, G])
        heads = sb("le_heads", [H, 4, G])
        chain = sb("le_chain", [H, 2, 2, G + 1])
        ini = sb("le_ini", [P, 2, G])
        init = sb("le_init", [P, 2])
        rise = sb("le_rise", [H, 1])
        drop = sb("le_drop", [H, P])
        drop_row = sb("le_droprow", [1, H])
        fac_row = sb("le_facrow", [1, H])
        fac = sb("le_fac", [P, H])
        wgt = sb("le_wgt", [P, 4, AW])
        cur = sb("le_cur", [P, 4, AW])
        scaled = sb("le_scaled", [P, AW])
        ps = lambda name: c.enter_context(nc.psum_tensor(name, [P, 512], F32))
        pa = [ps(f"le_pa{n}") for n in range(4)]
        pt, pq, pb, px = ps("le_pt"), ps("le_pq"), ps("le_pb"), ps("le_px")
        s_idx, s_turn, s_got = sem("le_sidx"), sem("le_turn"), k.got[0:2]
        s_sel, s_tr, s_cp, s_q = sem("le_ssel"), sem("le_str"), sem("le_scp"), sem("le_sq")
        s_stat, s_pe, s_ex, s_f = sem("le_stat"), sem("le_spe"), sem("le_sex"), sem("le_sf")
        s_rhs, s_mm, s_cur, s_acc, s_init = sem("le_rhs"), sem("le_mm"), sem("le_scur"), sem("le_acc"), sem("le_sinit")
        s_scaled = sem("le_sscaled")
        s_ld = [sem(f"le_ld{n}") for n in range(2)]
        STATS = ["add_src", "add_edge", "cols_f", "ones", "leaky", "mask", "scan", "scan_b", "cols", "heads", "carry",
                 "chain", "chain_b", "ini", "init", "run", "whole", "rise", "drop", "subtract", "fac_row", "fac"]
        MOVES = ["logits", "tails", "starts", "maxima", "drop", "factor"]
        stat = lambda b, name: b * len(STATS) + STATS.index(name) + 1
        move = lambda b, name: b * len(MOVES) + MOVES.index(name) + 1
        per_step = lambda a: a.rearrange("p (s h) -> p s h", h=H)
        rev = lambda a: a[:, ::-1]

        def group(it, u, tick, back):
            b, n = it * 2 + u // G - back, u // G - back
            if u % G != tick or not (not isinstance(it, int) or 0 <= b < NG):
                return None
            return b, n % 2, it + n // 2

        with nc.Block() as block:
            @block.sync
            def _(sp):
                def body(it, u):
                    if g := group(it, u, 0, 0):
                        b, par, pair = g
                        wait(sp, s_stat, stat(b - 2, "whole"))
                        sp.dma_start(ae[:, par, :], k.ae_dram.ap()[:, ds(b * FW, FW)]).then_inc(s_ld[par], 16)
                        sp.dma_start(flags[:, par, 0:RW], k.runs.ap()[ds(b * FW, FW), :]).then_inc(s_ld[par], 16)
                ticks(sp, NS, U, 0, body, 2)
                for n in range(2):
                    sp.wait_ge(s_ld[n], 32 * (NG // 2))

            @block.gpsimd
            def _(pool):
                def body(it, u):
                    t = it * U + u
                    if u % half == 0:
                        h = u // half
                        if u % G == 0:
                            wait(pool, s_stat, stat(it * 2 + u // G - 2, "add_src"))
                        nc.gpsimd.tensor_copy(idx[:, h, :], k.src[:, ds(t, half)]).then_inc(s_idx, 1)
                        pool.wait_ge(s_idx, it * (U // half) + h + 1)
                    wait(pool, s_rhs, t - U + 1)
                    pool.sem_inc(s_turn, 1)
                    pool.indirect_dma_start(got[:, u, :], None, table,
                                            bass.IndirectOffsetOnAxis(idx[:, u // half, u % half:u % half + 1], 0)
                                            ).then_inc(s_got[u // G], 16)
                ticks(pool, NS, U, 0, body, 2)

            @block.vector
            def _(dve):
                for n in range(4):
                    nc.vector.memset(cur[:, n, :], 0.0)
                nc.vector.memset(chain[:, :, :, :], -BIG).then_inc(s_init, 1)
                dve.wait_ge(s_init, 1)

                def maxima(it, u, slot):
                    now = lambda tick, at, back=1: slot == at and group(it, u, tick, back)
                    own = lambda b, name: dve.wait_ge(s_stat, stat(b, name))
                    if g := now(6, 0):
                        b, par, pair = g
                        dve.wait_ge(s_got[par], pair * (16 * G) + (16 * G + k.seen[par]))
                        dve.wait_ge(s_q, b * 4 + 4)
                        wait(dve, s_ex, b)
                        last_cols = got[:, par * G:(par + 1) * G, :].rearrange("p s (h c) -> p s h c", h=H)[:, :, :, C]
                        nc.vector.tensor_tensor(per_step(lg[:, :]), last_cols, per_step(pq[:, 0:FW]),
                                                ALU.add).then_inc(s_stat, 1)
                    if g := now(6, 1):
                        b, par, pair = g
                        dve.wait_ge(s_ld[par], pair * 32 + 32)
                        own(b, "add_src")
                        nc.vector.tensor_tensor(lg[:, :], lg[:, :], ae[:, par, :], ALU.add).then_inc(s_stat, 1)
                        nc.vector.tensor_tensor(
                            cols[:, 0:2, :], flags[:, par, P + 1:RW].unsqueeze(2).to_broadcast([P, 2, G]),
                            k.smask[:, :].unsqueeze(1).to_broadcast([P, 2, G]), ALU.mult).then_inc(s_stat, 1)
                    if g := now(6, 2):
                        b, par, pair = g
                        last_cols = got[:, par * G:(par + 1) * G, :].rearrange("p s (h c) -> p s h c", h=H)[:, :, :, C]
                        nc.vector.memset(last_cols, 1.0).then_inc(s_stat, 1)
                        own(b, "add_edge")
                        nc.vector.scalar_tensor_tensor(out=lg[:, :], in0=lg[:, :], scalar=0.2, in1=lg[:, :],
                                                       op0=ALU.mult, op1=ALU.max).then_inc(s_stat, 1)
                    if g := now(7, 0):
                        b, par, pair = g
                        own(b, "leaky")
                        nc.vector.tensor_tensor(per_step(lg[:, :]), per_step(lg[:, :]),
                                                k.neg[:, ds(b * G, G)].unsqueeze(2).to_broadcast([P, G, H]),
                                                ALU.add).then_inc(s_stat, 1)
                    if g := now(8, 2):
                        b, par, pair = g
                        dve.wait_ge(s_pe, move(b, "logits"))
                        nc.vector.tensor_tensor_scan(part[:, 0:P], flags[:, par, 0:P], pb[:, 0:P], -BIG, ALU.add,
                                                     ALU.max).then_inc(s_stat, 1)
                    if g := now(9, 0):
                        b, par, pair = g
                        nc.vector.tensor_tensor_scan(rev(part[:, P:2 * P]), rev(flags[:, par, 1:P + 1]), rev(pb[:, 0:P]),
                                                     -BIG, ALU.add, ALU.max).then_inc(s_stat, 1)
                    if g := now(9, 1):
                        b, par, pair = g
                        own(b, "scan_b")
                        nc.vector.tensor_tensor(
                            cols[:, 2:4, :], part[:, P - 1:P + 1].unsqueeze(2).to_broadcast([P, 2, G]),
                            k.smask[:, :].unsqueeze(1).to_broadcast([P, 2, G]), ALU.mult).then_inc(s_stat, 1)
                    if g := now(10, 2):
                        b, par, pair = g
                        dve.wait_ge(s_pe, move(b, "tails"))
                        nc.vector.tensor_copy(heads[:, :, :], px[0:H, 0:4 * G].rearrange("p (a s) -> p a s", a=4)
                                              ).then_inc(s_stat, 1)
                        nc.vector.tensor_copy(chain[:, par, 0, 0:1], chain[:, 1 - par, 0, G:G + 1]).then_inc(s_stat, 1)
                    if g := now(11, 0):
                        b, par, pair = g
                        own(b, "carry")
                        nc.vector.tensor_tensor_scan(chain[:, par, 0, 1:G + 1], heads[:, 0, :], heads[:, 2, :],
                                                     chain[:, par, 0, 0:1], ALU.add, ALU.max).then_inc(s_stat, 1)
                        nc.vector.tensor_tensor_scan(rev(chain[:, par, 1, 0:G - 1]), rev(heads[:, 1, 1:G]),
                                                     rev(heads[:, 3, 1:G]), -BIG, ALU.add, ALU.max).then_inc(s_stat, 1)
                    if g := now(12, 1):
                        b, par, pair = g
                        dve.wait_ge(s_pe, move(b, "starts"))
                        nc.vector.tensor_tensor(
                            ini[:, :, :], px[:, 64:64 + 2 * G + 2].rearrange("p (a s) -> p a s", a=2)[:, :, 0:G],
                            k.smask[:, :].unsqueeze(1).to_broadcast([P, 2, G]), ALU.mult).then_inc(s_stat, 1)
                    if g := now(12, 2):
                        b, par, pair = g
                        own(b, "ini")
                        nc.vector.tensor_reduce(init[:, :], ini[:, :, :], AX.X, ALU.add).then_inc(s_stat, 1)
                    if g := now(13, 0):
                        b, par, pair = g
                        own(b, "init")
                        nc.vector.tensor_tensor_scan(run[:, :], flags[:, par, 0:P], pb[:, 0:P], init[:, 0:1], ALU.add,
                                                     ALU.max).then_inc(s_stat, 1)
                    if g := now(13, 1):
                        b, par, pair = g
                        own(b, "run")
                        nc.vector.tensor_tensor_scan(rev(mx[:, :]), rev(flags[:, par, 1:P + 1]), rev(run[:, :]),
                                                     init[:, 1:2], ALU.add, ALU.max).then_inc(s_stat, 1)
                    if g := now(13, 2):
                        b, par, pair = g
                        own(b, "whole")
                        nc.vector.tensor_tensor(rise[:, :], chain[:, par, 0, 0:1], mx[0:H, 0:1],
                                                ALU.subtract).then_inc(s_stat, 1)
                    if g := now(14, 0):
                        b, par, pair = g
                        own(b, "rise")
                        nc.vector.tensor_scalar_min(drop[:, :], rise[:, 0:1].to_broadcast([H, P]), 0.0
                                                    ).then_inc(s_stat, 1)
                    if g := now(15, 0):
                        b, par, pair = g
                        dve.wait_ge(s_pe, move(b, "maxima"))
                        nc.vector.tensor_tensor(lg[:, :], lg[:, :], pb[:, 0:FW], ALU.subtract).then_inc(s_stat, 1)
                    if g := now(0, 1, 2):
                        b, par, pair = g
                        dve.wait_ge(s_f, b + 1)
                        nc.vector.tensor_scalar(fac_row[:, :], drop_row[:, :], 1.0, None, ALU.subtract).then_inc(s_stat, 1)
                    if g := now(2, 1, 2):
                        b, par, pair = g
                        dve.wait_ge(s_pe, move(b, "factor"))
                        nc.vector.tensor_scalar(fac[:, :], px[:, 192:192 + H], 1.0, None, ALU.add).then_inc(s_stat, 1)

                def body(it, u):
                    r = u - U - LAG
                    if r % G == 0 and live(it, r, U, NS):
                        wait(dve, s_cur, it * U + r)
                        dve.wait_ge(s_stat, stat(it * 2 + r // G, "fac"))
                        nc.vector.tensor_tensor(
                            scaled[:, :].rearrange("p (h c) -> p h c", h=H),
                            cur[:, (r - 1) % 4, :].rearrange("p (h c) -> p h c", h=H),
                            fac[:, :].unsqueeze(2).to_broadcast([P, H, C1]), ALU.mult).then_inc(s_scaled, 1)
                    a = u - U
                    if live(it, a, U, NS):
                        t = it * U + a
                        if u % G == 0:
                            dve.wait_ge(s_ex, it * 2 + u // G - 1)
                        wait(dve, s_mm, t - 3)
                        nc.vector.tensor_tensor(
                            wgt[:, u % 4, :].rearrange("p (h c) -> p h c", h=H),
                            got[:, u, :].rearrange("p (h c) -> p h c", h=H),
                            ex[:, u // G, (u % G) * H:(u % G + 1) * H].unsqueeze(2).to_broadcast([P, H, C1]),
                            ALU.mult).then_inc(s_rhs, 1)
                    maxima(it, u, 0)
                    r = a - LAG
                    if live(it, r, U, NS):
                        s = it * U + r
                        before = cur[:, (r - 1) % 4, :]
                        wait(dve, s_cur, s)
                        if r % G == 0:
                            dve.wait_ge(s_scaled, it * 2 + r // G + 1)
                            before = scaled[:, :]
                        dve.wait_ge(s_mm, s + 1)
                        wait(dve, s_acc, s - 3)
                        nc.vector.scalar_tensor_tensor(out=cur[:, r % 4, :], in0=before, scalar=k.same[:, ds(s, 1)],
                                                       in1=pa[r % 4][:, 0:AW], op0=ALU.mult,
                                                       op1=ALU.add).then_inc(s_cur, 1)
                    maxima(it, u, 1)
                    n = u - 2
                    if live(it, n, U, NS):
                        s = it * U + n
                        wait(dve, s_mm, s - U + 1)
                        nc.vector.tensor_scalar(sel[:, n % U, :], k.iota[:, :], k.drel[:, ds(s, 1)], None,
                                                ALU.is_equal).then_inc(s_sel, 1)
                    maxima(it, u, 2)
                ticks(dve, NS, U, U + LAG, body, 2)

            @block.tensor
            def _(pe):
                pe_j = [None]

                def body(it, u):
                    a = u - U
                    if live(it, a, U, NS):
                        t = it * U + a
                        pe.wait_ge(s_rhs, t + 1)
                        wait(pe, s_cur, t - 3)
                        nc.tensor.matmul(pa[u % 4][:, 0:AW], sel[:, u, :], wgt[:, u % 4, :], start=True,
                                         stop=True).then_inc(s_mm, 1)
                    if g := group(it, u, 7, 1):
                        pe.wait_ge(s_stat, stat(g[0], "mask"))
                        nc.tensor.transpose(pb[:, 0:P], lg[:, :], k.ident[:, :]).then_inc(s_pe, 1)
                    if g := group(it, u, 11, 1):
                        pe.wait_ge(s_stat, stat(g[0], "chain_b"))
                        nc.tensor.matmul(px[:, 64:64 + 2 * G + 2], k.hmask_t[:, :],
                                         chain[:, g[1], :, :].rearrange("p a s -> p (a s)"), start=True,
                                         stop=True).then_inc(s_pe, 1)
                    if g := group(it, u, 14, 1):
                        pe.wait_ge(s_stat, stat(g[0], "drop"))
                        nc.tensor.matmul(px[:, 160:160 + H], drop[:, :], k.ident[0:H, 0:H], start=True,
                                         stop=True).then_inc(s_pe, 1)
                    n = u - 2
                    if live(it, n, U, NS):
                        pe.wait_ge(s_sel, it * U + n + 1)
                        if n % 4 == 0:
                            wait(pe, s_cp, it * 8 + n // 4)
                        nc.tensor.transpose(pt[:, (n % 4) * P:(n % 4 + 1) * P], sel[:, n % U, :],
                                            k.ident[:, :]).then_inc(s_tr, 1)
                    q = u - 6
                    if q % 4 < 2 and live(it, q - q % 4, U, NS):
                        first = q - q % 4
                        f = it * 8 + first // 4
                        if q % 4 == 0 or u == 0:
                            _, pe_j[0] = nc.values_load_multi_w_load_instructions(
                                k.step_j[0:1, ds(it * U + first, 4)], engines=(mybir.EngineType.PE,), min_val=0,
                                max_val=NT - 1,
                                skip_runtime_bounds_check_because="j(s) is clamped to the last node tile")
                        if q % 4 == 0:
                            pe.wait_ge(s_cp, f + 1)
                        if q % G == 0:
                            wait(pe, s_stat, stat(it * 2 + q // G - 1, "add_src"))
                        for m in (q % 4 * 2, q % 4 * 2 + 1):
                            o = (first + m) % G * H
                            for n in range(3):
                                last = nc.tensor.matmul(pq[:, o:o + H], tr[:, (first // 4) % 2, m * P:(m + 1) * P],
                                                        a_dst[:, ds(pe_j[0][m] * H + n * (NT * H), H)],
                                                        start=(n == 0), stop=(n == 2))
                        if q % 4 == 1:
                            last.then_inc(s_q, 1)
                    if g := group(it, u, 9, 1):
                        pe.wait_ge(s_stat, stat(g[0], "cols"))
                        nc.tensor.matmul(px[0:H, 0:4 * G], k.hmask[:, :], cols[:, :, :].rearrange("p a s -> p (a s)"),
                                         start=True, stop=True).then_inc(s_pe, 1)
                    if g := group(it, u, 13, 1):
                        pe.wait_ge(s_stat, stat(g[0], "whole"))
                        nc.tensor.transpose(pb[:, 0:P], mx[:, :], k.ident[:, :]).then_inc(s_pe, 1)
                    if g := group(it, u, 0, 2):
                        pe.wait_ge(s_stat, stat(g[0], "fac_row"))
                        nc.tensor.matmul(px[:, 192:192 + H], sel[0:1, g[1] * G, :], fac_row[:, :], start=True,
                                         stop=True).then_inc(s_pe, 1)
                ticks(pe, NS, U, U, body, 2)

            @block.scalar
            def _(act):
                act_j = [None]

                def body(it, u):
                    if g := group(it, u, 15, 1):
                        b, par, pair = g
                        act.wait_ge(s_pe, move(b, "drop"))
                        wait(act, s_stat, stat(b - 1, "fac_row"))
                        nc.scalar.activation(drop_row[:, :], px[0:1, 160:160 + H], ACT.Exp).then_inc(s_f, 1)
                    if g := group(it, u, 15, 1):
                        b, par, pair = g
                        act.wait_ge(s_stat, stat(b, "subtract"))
                        wait(act, s_mm, b * G - G)
                        nc.scalar.activation(ex[:, par, :], lg[:, :], ACT.Exp).then_inc(s_ex, 1)
                    e = u - 5
                    if e % 4 == 0 and live(it, e, U, NS):
                        f = it * 8 + e // 4
                        act.wait_ge(s_tr, f * 4 + 4)
                        wait(act, s_q, f - 1)
                        nc.scalar.activation(tr[:, (e // 4) % 2, :], pt[:, :], ACT.Copy).then_inc(s_cp, 1)
                    r = u - U - LAG
                    if live(it, r, U, NS):
                        s = it * U + r
                        if r % 4 == 0 or u == 0:
                            _, act_j[0] = nc.values_load_multi_w_load_instructions(
                                k.step_j[0:1, ds(s - r % 4, 4)], engines=(mybir.EngineType.Activation,), min_val=0,
                                max_val=NT - 1,
                                skip_runtime_bounds_check_because="j(s) is clamped to the last node tile")
                        act.wait_ge(s_cur, s + 1)
                        wait(act, s_acc, s)
                        nc.scalar.activation(k.acc[:, ds(act_j[0][r % 4] * AW, AW)], cur[:, r % 4, :],
                                             ACT.Copy).then_inc(s_acc, 1)
                ticks(act, NS, U, U + LAG, body, 2)
                act.wait_ge(s_acc, NS)
    for n in range(2):
        k.seen[n] += 16 * G * (NG // 2)


def segment_softmax(nc, tag, k):
    NB4 = CB // 4
    with ExitStack() as c:
        sb = lambda name, shape, dt=F32: c.enter_context(nc.sbuf_tensor(f"{tag}_{name}", shape, dt))
        sem = lambda name: c.enter_context(nc.semaphore(f"{tag}_{name}"))
        seq, run = k.acc[:, 0:SEQ], k.acc[:, SEQ:2 * SEQ]
        kraw = k.acc[:, 0:SEQ + 2]
        new = sb("sm_new", [P, SEQ + 1])
        per = sb("sm_per", [P, CB * P])
        tail = sb("sm_tail", [P, 2])
        ct = sb("sm_ct", [H, CH, 2])
        chain = sb("sm_chain", [H, CH + 1])
        init = sb("sm_init", [P, 1])
        dt_ = [nc.dram_tensor(f"{tag}_sm_tail{n}", [P, 2], F32) for n in range(2)]
        dc_ = [nc.dram_tensor(f"{tag}_sm_chain{n}", [P, 1], F32) for n in range(2)]
        pt = [c.enter_context(nc.psum_tensor(f"{tag}_sm_p{n}", [P, 512], F32)) for n in range(4)]
        s_key, s_v, s_per, s_t, s_seq, s_max, s_b, s_sub, s_ex = (
            sem("sm_key"), sem("sm_v"), sem("sm_sper"), sem("sm_st"), sem("sm_sseq"), sem("sm_max"), sem("sm_b"),
            sem("sm_sub"), sem("sm_ex"))
        s_tail, s_ct, s_chain, s_in, s_td = sem("sm_stail"), sem("sm_sct"), sem("sm_schain"), sem("sm_sin"), sem("sm_std")
        bch = lambda a: a.rearrange("p (c b h) -> p c b h", c=CH, h=H)
        perm = per[:, :].rearrange("p (b c h) -> p c b h", c=CH, h=H)
        perh = lambda a: a.rearrange("p (c b) -> p c b", c=CH).unsqueeze(3).to_broadcast([P, CH, CB, H])
        edge4 = bch(k.edge[:, :])
        with nc.Block() as block:
            @block.sync
            def _(sp):
                for ch in range(CH):
                    sp.dma_start(kraw[ch * H:(ch + 1) * H, :],
                                 k.keys.ap()[P - 1 + ch * SEQ:P + 1 + (ch + 1) * SEQ]
                                 .rearrange("(a n) -> a n", a=1).to_broadcast([H, SEQ + 2])).then_inc(s_key, 16)
                for n in range(2):
                    sp.wait_ge(s_tail, n + 1)
                    sp.dma_start(dt_[n].ap(), tail[:, :]).then_inc(s_td, 16)
                    sp.wait_ge(s_td, 16 * (4 * n + 1))
                    sp.dma_start(ct[:, :, :], dt_[n].ap().rearrange("(c h) w -> h c w", h=H)).then_inc(s_td, 16)
                    sp.wait_ge(s_td, 16 * (4 * n + 2))
                    sp.sem_inc(s_ct, 1)
                    sp.wait_ge(s_chain, n + 1)
                    sp.dma_start(dc_[n].ap().rearrange("(c h) w -> h (c w)", h=H),
                                 chain[:, n:n + CH]).then_inc(s_td, 16)
                    sp.wait_ge(s_td, 16 * (4 * n + 3))
                    sp.dma_start(init[:, :], dc_[n].ap()).then_inc(s_td, 16)
                    sp.wait_ge(s_td, 16 * (4 * n + 4))
                    sp.sem_inc(s_in, 1)

            @block.vector
            def _(dve):
                v = Chain(dve, s_v)
                v(nc.vector.tensor_tensor(perm, edge4, perh(k.weight[:, :]), ALU.mult))
                v(nc.vector.tensor_tensor(perm, perm, perh(k.neg[:, :]), ALU.add))
                dve.sem_inc(s_per, 1)
                dve.wait_ge(s_key, 16 * CH)
                v(nc.vector.tensor_tensor(new[:, :], kraw[:, 1:SEQ + 2], kraw[:, 0:SEQ + 1], ALU.not_equal))
                v(nc.vector.tensor_scalar(new[:, :], new[:, :], -BIG, None, ALU.mult))
                dve.sem_inc(s_per, 1)
                dve.wait_ge(s_seq, NB4)
                rev = lambda a: a[:, ::-1]
                v(nc.vector.tensor_tensor_scan(run, new[:, 0:SEQ], seq, -BIG, ALU.add, ALU.max))
                v(nc.vector.tensor_copy(tail[:, 1:2], run[:, SEQ - 1:SEQ]))
                v(nc.vector.tensor_reduce(tail[:, 0:1], new[:, 0:SEQ], AX.X, ALU.min))
                dve.sem_inc(s_tail, 1)
                v(nc.vector.memset(chain[:, :], -BIG))
                dve.wait_ge(s_ct, 1)
                v(nc.vector.tensor_tensor_scan(chain[:, 1:CH + 1], ct[:, :, 0], ct[:, :, 1], -BIG, ALU.add, ALU.max))
                dve.sem_inc(s_chain, 1)
                dve.wait_ge(s_in, 1)
                v(nc.vector.tensor_tensor_scan(run, new[:, 0:SEQ], seq, init[:, 0:1], ALU.add, ALU.max))
                v(nc.vector.tensor_tensor_scan(rev(seq), rev(new[:, 1:SEQ + 1]), rev(run), -BIG, ALU.add, ALU.max))
                v(nc.vector.tensor_copy(tail[:, 1:2], seq[:, 0:1]))
                v(nc.vector.tensor_reduce(tail[:, 0:1], new[:, 1:SEQ + 1], AX.X, ALU.min))
                dve.sem_inc(s_tail, 1)
                v(nc.vector.memset(chain[:, :], -BIG))
                dve.wait_ge(s_ct, 2)
                v(nc.vector.tensor_tensor_scan(chain[:, 0:CH][:, ::-1], ct[:, ::-1, 0], ct[:, ::-1, 1], -BIG,
                                               ALU.add, ALU.max))
                dve.sem_inc(s_chain, 1)
                dve.wait_ge(s_in, 2)
                v(nc.vector.tensor_tensor_scan(rev(seq), rev(new[:, 1:SEQ + 1]), rev(run), init[:, 0:1], ALU.add, ALU.max))
                dve.sem_inc(s_max, 1)
                for g in range(NB4):
                    dve.wait_ge(s_b, g + 1)
                    nc.vector.tensor_tensor(per[:, g * 512:(g + 1) * 512], per[:, g * 512:(g + 1) * 512], pt[g % 4][:, :],
                                            ALU.subtract).then_inc(s_sub, 1)

            @block.tensor
            def _(pe):
                pe.wait_ge(s_per, 1)
                for g in range(NB4):
                    wait(pe, s_seq, g - 3)
                    for n in range(4):
                        b = g * 4 + n
                        last = nc.tensor.transpose(pt[g % 4][:, n * P:(n + 1) * P], per[:, b * P:(b + 1) * P], k.ident[:, :])
                    last.then_inc(s_t, 1)
                pe.wait_ge(s_max, 1)
                for g in range(NB4):
                    wait(pe, s_sub, g - 3)
                    for n in range(4):
                        b = g * 4 + n
                        last = nc.tensor.transpose(pt[g % 4][:, n * P:(n + 1) * P], k.acc[:, b * P:(b + 1) * P], k.ident[:, :])
                    last.then_inc(s_b, 1)

            @block.scalar
            def _(act):
                act.wait_ge(s_per, 2)
                for g in range(NB4):
                    act.wait_ge(s_t, g + 1)
                    nc.scalar.activation(k.acc[:, g * 512:(g + 1) * 512], pt[g % 4][:, :], ACT.Copy).then_inc(s_seq, 1)
                for g in range(NB4):
                    act.wait_ge(s_sub, g + 1)
                    nc.scalar.activation(edge4[:, :, g * 4:(g + 1) * 4, :],
                                         per[:, g * 512:(g + 1) * 512].rearrange("p (b c h) -> p c b h", c=CH, h=H),
                                         ACT.Exp).then_inc(s_ex, 1)
                act.wait_ge(s_ex, NB4)


def recycle(nc):
    used = sorted(nc.released_uncleared_semaphores)
    with nc.Block() as block:
        @block.gpsimd
        def _(pool):
            pool.sem_clear(range(used[0], used[-1] + 1))


def load(nc, name, pairs):
    with nc.semaphore(name) as s, nc.Block() as block:
        @block.sync
        def _(sp):
            for tile, source in pairs:
                sp.dma_start(tile, source).then_inc(s, 16)
            sp.wait_ge(s, 16 * len(pairs))


def store(nc, name, target, tile):
    with nc.semaphore(name) as s, nc.Block() as block:
        @block.sync
        def _(sp):
            sp.dma_start(target, tile).then_inc(s, 16)
            sp.wait_ge(s, 16)


def rows_of(w, kt=KT):
    return w.rearrange("(k p) n -> p k n", k=kt)


def by_head(a):
    return a.rearrange("p (h c) -> p h c", h=H)


def spread(a, rows=P):
    return a.rearrange("(a n) -> a n", a=1).to_broadcast([rows, a.shape[0]])


def column(a):
    return a.rearrange("(k p) -> p k", p=P)


def fold_gain(nc, k, name, w, width, gain, shift, bias, cols, in_rows=None):
    with ExitStack() as c:
        sem = lambda n: c.enter_context(nc.semaphore(name + n))
        pb = [c.enter_context(nc.psum_tensor(f"{name}p{n}", [P, 512], F32)) for n in range(2)]
        s_mm, s_v, s_b = sem("mm"), sem("v"), sem("b")
        with nc.Block() as block:
            @block.tensor
            def _(pe):
                if cols:
                    for f in range(width // P):
                        for n in range(KT):
                            last = nc.tensor.matmul(pb[0][:, f:f + 1], w[:, n, f * P:(f + 1) * P], shift[:, n:n + 1],
                                                    start=(n == 0), stop=(n == KT - 1))
                else:
                    for n in range(KT):
                        last = nc.tensor.matmul(pb[0][0:1, 0:width], shift[:, n:n + 1], w[:, n, :], start=(n == 0),
                                                stop=(n == KT - 1))
                last.then_inc(s_mm, 1)
                if not cols:
                    pe.wait_ge(s_b, 1)
                    nc.tensor.matmul(pb[1][:, 0:width], k.ones[0:1, :], bias, start=True, stop=True).then_inc(s_mm, 1)

            @block.vector
            def _(dve):
                v = Chain(dve, s_v)
                dve.wait_ge(s_mm, 1)
                if cols:
                    v(nc.vector.tensor_tensor(bias, bias, pb[0][:, 0:width // P], ALU.add))
                else:
                    v(nc.vector.tensor_tensor(bias, bias, pb[0][0:1, 0:width], ALU.add))
                    dve.sem_inc(s_b, 1)
                    dve.wait_ge(s_mm, 2)
                    v(nc.vector.tensor_copy(in_rows, pb[1][:, 0:width]))
                for n in range(KT):
                    v(nc.vector.tensor_scalar(w[:, n, :], w[:, n, :], gain[:, n:n + 1], None, ALU.mult))


def attention_output(nc, k, y, wo, bo, alpha, rd):
    U = 4
    with ExitStack() as c:
        sb = lambda name, shape, dt=F32: c.enter_context(nc.sbuf_tensor(name, shape, dt))
        sem = lambda name: c.enter_context(nc.semaphore(name))
        a = sb("ao_a", [P, 2, D])
        at = sb("ao_at", [P, 2, D])
        pt = [c.enter_context(nc.psum_tensor(f"ao_t{n}", [P, 512], F32)) for n in range(2)]
        po = [c.enter_context(nc.psum_tensor(f"ao_o{n}", [P, 512], F32)) for n in range(2)]
        s_row, s_bias = sem("ao_srow"), sem("ao_sbias")
        s_a, s_t, s_at, s_o, s_y = sem("ao_sa"), sem("ao_st"), sem("ao_sat"), sem("ao_so"), sem("ao_sy")
        with nc.Block() as block:
            @block.gpsimd
            def _(pool):
                pool.wait_ge(s_row, 1)

                def body(it, u):
                    t = it * U + u
                    nc.gpsimd.tensor_tensor(y[:, ds(t * D, D)], y[:, ds(t * D, D)], bo, ALU.add).then_inc(s_bias, 1)
                ticks(pool, NT, U, 0, body)

            @block.vector
            def _(dve):
                nc.vector.tensor_scalar(bo, bo, alpha, None, ALU.mult).then_inc(s_row, 1)

                def body(it, u):
                    t = it * U + u
                    if live(it, u, U, NT):
                        wait(dve, s_t, t - 1)
                        nc.vector.tensor_tensor(
                            a[:, u % 2, :].rearrange("p (h c) -> p h c", h=H),
                            k.acc[:, ds(t * AW, AW)].rearrange("p (h c) -> p h c", h=H)[:, :, 0:C],
                            rd[:, ds(t * H, H)].unsqueeze(2).to_broadcast([P, H, C]), ALU.mult).then_inc(s_a, 1)
                    r = u - 2
                    if live(it, r, U, NT):
                        s = it * U + r
                        dve.wait_ge(s_o, s + 1)
                        dve.wait_ge(s_bias, s + 1)
                        nc.vector.scalar_tensor_tensor(out=y[:, ds(s * D, D)], in0=po[r % 2][:, 0:D], scalar=alpha,
                                                       in1=y[:, ds(s * D, D)], op0=ALU.mult, op1=ALU.add).then_inc(s_y, 1)
                    e = u - 3
                    if live(it, e, U, NT):
                        s = it * U + e
                        dve.wait_ge(s_y, s + 1)
                        nc.vector.bn_stats(k.st[:, ds(s * 6, 6)], y[:, ds(s * D, D)])
                ticks(dve, NT, U, 3, body)

            @block.scalar
            def _(act):
                def body(it, u):
                    t = it * U + u
                    act.wait_ge(s_t, t + 1)
                    wait(act, s_o, t - 1)
                    nc.scalar.activation(at[:, u % 2, :], pt[u % 2][:, 0:D], ACT.Copy).then_inc(s_at, 1)
                ticks(act, NT, U, 0, body)

            @block.tensor
            def _(pe):
                def body(it, u):
                    t = it * U + u
                    if live(it, u, U, NT):
                        pe.wait_ge(s_a, t + 1)
                        wait(pe, s_at, t - 1)
                        for n in range(KT):
                            last = nc.tensor.transpose(pt[u % 2][:, n * P:(n + 1) * P], a[:, u % 2, n * P:(n + 1) * P],
                                                       k.ident[:, :])
                        last.then_inc(s_t, 1)
                    r = u - 1
                    if live(it, r, U, NT):
                        s = it * U + r
                        pe.wait_ge(s_at, s + 1)
                        wait(pe, s_y, s - 1)
                        for n in range(KT):
                            last = nc.tensor.matmul(po[r % 2][:, 0:D], at[:, r % 2, n * P:(n + 1) * P], wo[:, n, :],
                                                    start=(n == 0), stop=(n == KT - 1))
                        last.then_inc(s_o, 1)
                ticks(pe, NT, U, 1, body)


def feed_forward(nc, k, y, xr, wf1, bf1, wf2, bf2, beta):
    U = 4
    with ExitStack() as c:
        sb = lambda name, shape, dt=F32: c.enter_context(nc.sbuf_tensor(name, shape, dt))
        sem = lambda name: c.enter_context(nc.semaphore(name))
        z = sb("ff_z", [P, 2, D])
        zt = sb("ff_zt", [P, 2, D])
        g = k.acc[:, 0:2 * FF].rearrange("p (s f) -> p s f", s=2)
        pt = [c.enter_context(nc.psum_tensor(f"ff_t{n}", [P, 512], F32)) for n in range(2)]
        ph = [[c.enter_context(nc.psum_tensor(f"ff_h{n}{m}", [P, 512], F32)) for m in range(2)] for n in range(2)]
        po = [c.enter_context(nc.psum_tensor(f"ff_o{n}", [P, 512], F32)) for n in range(2)]
        s_row, s_bias = sem("ff_srow"), sem("ff_sbias")
        s_z, s_t, s_zt, s_h, s_g, s_o, s_y, s_x = (sem("ff_sz"), sem("ff_st"), sem("ff_szt"), sem("ff_sh"), sem("ff_sg"),
                                                   sem("ff_so"), sem("ff_sy"), sem("ff_sx"))
        with nc.Block() as block:
            @block.scalar
            def _(act):
                def body(it, u):
                    t = it * U + u
                    if live(it, u, U, NT):
                        wait(act, s_t, t - 1)
                        nc.scalar.activation(z[:, u % 2, :], y[:, ds(t * D, D)], ACT.Identity, bias=k.nb[:, ds(t, 1)],
                                             scale=k.rs[:, ds(t, 1)]).then_inc(s_z, 1)
                    r = u - 2
                    if live(it, r, U, NT):
                        s = it * U + r
                        act.wait_ge(s_h, s + 1)
                        wait(act, s_o, s - 1)
                        for f in range(FT):
                            last = nc.scalar.activation(g[:, r % 2, f * P:(f + 1) * P],
                                                        ph[r % 2][f // 4][:, (f % 4) * P:(f % 4 + 1) * P], ACT.Gelu,
                                                        bias=bf1[:, f:f + 1])
                        last.then_inc(s_g, 1)
                ticks(act, NT, U, 2, body)

            @block.gpsimd
            def _(pool):
                pool.wait_ge(s_row, 1)

                def body(it, u):
                    t = it * U + u
                    nc.gpsimd.tensor_tensor(xr[:, ds(t * D, D)], xr[:, ds(t * D, D)], bf2, ALU.add).then_inc(s_bias, 1)
                ticks(pool, NT, U, 0, body)

            @block.vector
            def _(dve):
                nc.vector.tensor_scalar(bf2, bf2, beta, None, ALU.mult).then_inc(s_row, 1)

                def body(it, u):
                    t = it * U + u
                    if live(it, u, U, NT):
                        dve.wait_ge(s_t, t + 1)
                        wait(dve, s_h, t - 1)
                        nc.vector.tensor_copy(zt[:, u % 2, :], pt[u % 2][:, 0:D]).then_inc(s_zt, 1)
                    r = u - 4
                    if live(it, r, U, NT):
                        s = it * U + r
                        dve.wait_ge(s_o, s + 1)
                        nc.vector.scalar_tensor_tensor(out=y[:, ds(s * D, D)], in0=po[r % 2][:, 0:D], scalar=beta,
                                                       in1=y[:, ds(s * D, D)], op0=ALU.mult, op1=ALU.add).then_inc(s_y, 1)
                        dve.wait_ge(s_y, s + 1)
                        dve.wait_ge(s_bias, s + 1)
                        nc.vector.tensor_tensor(xr[:, ds(s * D, D)], xr[:, ds(s * D, D)], y[:, ds(s * D, D)],
                                                ALU.add).then_inc(s_x, 1)
                        dve.wait_ge(s_x, s + 1)
                        nc.vector.bn_stats(k.st[:, ds(s * 6, 6)], xr[:, ds(s * D, D)])
                ticks(dve, NT, U, 4, body)

            @block.tensor
            def _(pe):
                def body(it, u):
                    t = it * U + u
                    if live(it, u, U, NT):
                        pe.wait_ge(s_z, t + 1)
                        wait(pe, s_zt, t - 1)
                        for n in range(KT):
                            last = nc.tensor.transpose(pt[u % 2][:, n * P:(n + 1) * P], z[:, u % 2, n * P:(n + 1) * P],
                                                       k.ident[:, :])
                        last.then_inc(s_t, 1)
                    q = u - 3
                    if live(it, q, U, NT):
                        s = it * U + q
                        pe.wait_ge(s_g, s + 1)
                        wait(pe, s_y, s - 1)
                        for f in range(FT):
                            last = nc.tensor.matmul(po[q % 2][:, 0:D], g[:, q % 2, f * P:(f + 1) * P], wf2[:, f, :],
                                                    start=(f == 0), stop=(f == FT - 1))
                        last.then_inc(s_o, 1)
                    r = u - 1
                    if live(it, r, U, NT):
                        s = it * U + r
                        pe.wait_ge(s_zt, s + 1)
                        wait(pe, s_g, s - 1)
                        for f in range(FT):
                            for n in range(KT):
                                last = nc.tensor.matmul(ph[r % 2][f // 4][:, (f % 4) * P:(f % 4 + 1) * P],
                                                        wf1[:, n, f * P:(f + 1) * P], zt[:, r % 2, n * P:(n + 1) * P],
                                                        start=(n == 0), stop=(n == KT - 1))
                        last.then_inc(s_h, 1)
                ticks(pe, NT, U, 3, body, 2)


def layer3_rows(nc, k, xr, y, rd, bias):
    U = 7
    with ExitStack() as c:
        a = c.enter_context(nc.sbuf_tensor("l3_a", [P, U, D], F32))
        s_n, s_b, s_a, s_y = (c.enter_context(nc.semaphore(n)) for n in ("l3_sn", "l3_sb", "l3_sa", "l3_sy"))
        with nc.Block() as block:
            @block.scalar
            def _(act):
                def body(it, u):
                    t = it * U + u
                    nc.scalar.activation(y[:, ds(t * D, D)], xr[:, ds(t * D, D)], ACT.Relu, bias=k.nb[:, ds(t, 1)],
                                         scale=k.rs[:, ds(t, 1)]).then_inc(s_n, 1)
                ticks(act, NT, U, 0, body)

            @block.gpsimd
            def _(pool):
                def body(it, u):
                    t = it * U + u
                    pool.wait_ge(s_n, t + 1)
                    nc.gpsimd.tensor_tensor(y[:, ds(t * D, D)], y[:, ds(t * D, D)], bias, ALU.add).then_inc(s_b, 1)
                ticks(pool, NT, U, 0, body)

            @block.vector
            def _(dve):
                def body(it, u):
                    t = it * U + u
                    if live(it, u, U, NT):
                        nc.vector.tensor_tensor(
                            a[:, u, :].rearrange("p (h c) -> p h c", h=H),
                            k.acc[:, ds(t * AW, AW)].rearrange("p (h c) -> p h c", h=H)[:, :, 0:C],
                            rd[:, ds(t * H, H)].unsqueeze(2).to_broadcast([P, H, C]), ALU.mult).then_inc(s_a, 1)
                    r = u - 2
                    if live(it, r, U, NT):
                        s = it * U + r
                        dve.wait_ge(s_a, s + 1)
                        dve.wait_ge(s_b, s + 1)
                        nc.vector.tensor_tensor(y[:, ds(s * D, D)], y[:, ds(s * D, D)], a[:, r % U, :],
                                                ALU.add).then_inc(s_y, 1)
                    e = u - 3
                    if live(it, e, U, NT):
                        s = it * U + e
                        dve.wait_ge(s_y, s + 1)
                        nc.vector.bn_stats(k.st[:, ds(s * 6, 6)], y[:, ds(s * D, D)])
                ticks(dve, NT, U, 3, body)


def final_output(nc, k, xr, y, gamma, beta, out):
    U = 8
    with ExitStack() as c:
        z = c.enter_context(nc.sbuf_tensor("fo_z", [P, U, D], F32))
        sem = lambda n: c.enter_context(nc.semaphore(n))
        s_z, s_b, s_1, s_2, s_out = sem("fo_z_"), sem("fo_b"), sem("fo_1"), sem("fo_2"), [sem(f"fo_out{n}") for n in range(U)]
        with nc.Block() as block:
            @block.scalar
            def _(act):
                def body(it, u):
                    t = it * U + u
                    wait(act, s_out[u], it * 16)
                    nc.scalar.activation(z[:, u, :], y[:, ds(t * D, D)], ACT.Identity, bias=k.nb[:, ds(t, 1)],
                                         scale=k.rs[:, ds(t, 1)]).then_inc(s_z, 1)
                ticks(act, NT, U, 0, body)

            @block.gpsimd
            def _(pool):
                def body(it, u):
                    t = it * U + u
                    nc.gpsimd.tensor_tensor(xr[:, ds(t * D, D)], xr[:, ds(t * D, D)], beta, ALU.add).then_inc(s_b, 1)
                ticks(pool, NT, U, 0, body)

            @block.vector
            def _(dve):
                def body(it, u):
                    if live(it, u, U, NT):
                        dve.wait_ge(s_z, it * U + u + 1)
                        nc.vector.tensor_tensor(z[:, u, :], z[:, u, :], gamma, ALU.mult).then_inc(s_1, 1)
                    r = u - 1
                    if live(it, r, U, NT):
                        s = it * U + r
                        dve.wait_ge(s_1, s + 1)
                        dve.wait_ge(s_b, s + 1)
                        nc.vector.tensor_tensor(z[:, r % U, :], z[:, r % U, :], xr[:, ds(s * D, D)],
                                                ALU.add).then_inc(s_2, 1)
                ticks(dve, NT, U, 1, body)

            @block.sync
            def _(sp):
                def body(it, u):
                    t = it * U + u
                    sp.wait_ge(s_2, t + 1)
                    if isinstance(t, int) and t == NT - 1:
                        sp.dma_start(out[t * P:N, :], z[0:LAST_ROWS, u, :]).then_inc(s_out[u], 16)
                    else:
                        sp.dma_start(out[ds(t * P, P), :], z[:, u, :]).then_inc(s_out[u], 16)
                ticks(sp, NT, U, 0, body)
                for n in range(U):
                    sp.wait_ge(s_out[n], 16 * len(range(n, NT, U)))


def split3(nc, a, parts, n):
    with nc.semaphore("split3") as s_v, nc.Block() as block:
        @block.vector
        def _(dve):
            v = Chain(dve, s_v)
            for m in range(3):
                part = parts[:, m * n:(m + 1) * n]
                v(nc.vector.tensor_copy(part, a))
                v(nc.vector.tensor_tensor(a, a, part, ALU.subtract))


def denominators(nc, tag, k, rd):
    with nc.semaphore(f"{tag}_dn") as s_v, nc.Block() as block:
        @block.vector
        def _(dve):
            v = Chain(dve, s_v)
            r3 = rd.rearrange("p (t h) -> p t h", h=H)
            v(nc.vector.tensor_scalar(r3, k.acc[:, 0:NT * AW].rearrange("p (t h c) -> p t h c", h=H, c=C1)[:, :, :, C], 1e-16,
                                      None, ALU.add))
            v(nc.vector.reciprocal(rd, rd))


def fold_attention(nc, name, tmp, jobs):
    with nc.semaphore(name) as s_v, nc.Block() as block:
        @block.vector
        def _(dve):
            v = Chain(dve, s_v)
            for w, att, out, heads in jobs:
                v(nc.vector.tensor_tensor(tmp, w, att, ALU.mult))
                v(nc.vector.tensor_reduce(out, tmp.rearrange("p (h c) -> p h c", h=heads), AX.X, ALU.add))


def gnn_kernel(nc, x, src, dst, edge_attr, edge_weight, w0, att_l, att_r, w1, wq, bq, wk, bk, wv, bv, we, be, wo, bo,
               ln1_g, ln1_b, ln2_g, ln2_b, wf1, bf1, wf2, bf2, alpha, beta, w3, we3, att_src, att_dst, att_edge,
               bias3, gamma3, beta3, out):
    flat = lambda a: a.rearrange("h c -> (h c)")
    table = lambda name, w: nc.dram_tensor(name, [NPAD, w], F32).ap()
    with ExitStack() as c:
        k = globals_of(nc, c)
        k.ae_dram = nc.dram_tensor("layer3_edge_part", [P, SEQ], F32)
        xr = c.enter_context(nc.sbuf_tensor("xr", [P, NT * D], F32))
        xrv = xr[:, :]
        walk_tables(nc, k, src, dst, edge_weight, x, xr)
        run_flags(nc, k)

        t0, al0 = table("t0", D + H0), table("al0", H0)
        s01 = c.enter_context(ExitStack())
        w1t = s01.enter_context(nc.sbuf_tensor("w1t", [P, KT, D], F32))
        with ExitStack() as s:
            sb = lambda name, shape, dt=F32: s.enter_context(nc.sbuf_tensor(name, shape, dt))
            w0t = sb("w0t", [P, KT, D + 2 * H0])
            att = sb("att0", [P, 2, D])
            tmp = sb("tmp0", [P, D])
            load(nc, "ld0", [
                             (w0t[:, :, 0:D], rows_of(w0)), (w1t[:, :, :], rows_of(w1)), (att[:, 0, :], spread(flat(att_r))),
                             (att[:, 1, :], spread(flat(att_l)))])
            fold_attention(nc, "fold0", tmp[:, :],
                           [(w0t[:, kt, 0:D], att[:, n, :], w0t[:, kt, D + n * H0:D + (n + 1) * H0], H0)
                            for kt in range(KT) for n in range(2)])
            row_stats(nc, "p1", k, xrv)
            project(nc, "p2", k, xrv, ACT.Relu, [(w0t, None, D + 2 * H0, None, [(0, D + H0, t0), (D + H0, H0, al0)], None)])
        layer0_edges(nc, k, xrv, src, dst, t0, al0)

        t1 = table("t1", D)
        row_stats(nc, "p3", k, None)
        project(nc, "p4", k, xrv, ACT.Relu, [(w1t, None, D, k.dis, [(0, D, t1)], None)])
        s01.close()
        aggregate(nc, "p5", k, t1, False)
        add_scaled(nc, k, xrv)
        recycle(nc)

        t_k, t_v = table("t_k", D), table("t_v", AW)
        with ExitStack() as s:
            sb = lambda name, shape, dt=F32: s.enter_context(nc.sbuf_tensor(name, shape, dt))
            h2 = sb("h2", [P, NT * D])
            width = [D, D, AW]
            w = [sb(f"w2_{n}", [P, KT, m]) for n, m in enumerate(width)]
            b = [sb(f"b2_{n}", [1, m]) for n, m in enumerate(width)]
            b_rows = [sb(f"b2r_{n}", [P, m]) for n, m in enumerate(width)]
            gain, shift = sb("gain1", [P, KT]), sb("shift1", [P, KT])
            with nc.semaphore("ones2") as s_p, nc.Block() as block:
                @block.gpsimd
                def _(pool):
                    nc.gpsimd.memset(w[2][:, :, :], 0.0).then_inc(s_p, 1)
                    nc.gpsimd.memset(b[2][:, :], 1.0).then_inc(s_p, 1)
                    pool.wait_ge(s_p, 2)
            load(nc, "ld2", [(w[n][:, :, :], rows_of(a)) for n, a in enumerate((wq, wk))] +
                 [(by_head(w[2][:, n, :])[:, :, 0:C], by_head(wv[n * P:(n + 1) * P, :])) for n in range(KT)] +
                 [(b[n][:, :], spread(a, 1)) for n, a in enumerate((bq, bk))] +
                 [(by_head(b[2][:, :])[:, :, 0:C], by_head(spread(bv, 1)))] +
                 [(gain[:, :], column(ln1_g)), (shift[:, :], column(ln1_b))])
            for n in range(3):
                fold_gain(nc, k, f"fg{n}", w[n], width[n], gain, shift, b[n][:, :], False, b_rows[n][:, :])
            row_stats(nc, "p6", k, None, True)
            normalized(nc, "p7", k, xrv, h2[:, :], ACT.Relu, k.rs_x, k.nb_x, True)
            row_stats(nc, "p8", k, None)
            project(nc, "p9", k, h2[:, :], ACT.Identity,
                    [(w[0], b_rows[0][:, :], D, None, [], k.acc[:, :]), (w[1], b_rows[1][:, :], D, None, [(0, D, t_k)], None),
                     (w[2], b_rows[2][:, :], AW, None, [(0, AW, t_v)], None)])
        with ExitStack() as s:
            sb = lambda name, shape, dt=F32: s.enter_context(nc.sbuf_tensor(name, shape, dt))
            k.edge = sb("edge2", [P, SEQ])
            with ExitStack() as s2:
                sb2 = lambda name, shape, dt=F32: s2.enter_context(nc.sbuf_tensor(name, shape, dt))
                k.ae = sb2("ae", [P, SEQ])
                wet = sb2("wet", [P, EW])
                we3t, atte, tmp = sb2("we3t", [ED, D]), sb2("atte", [ED, D]), sb2("tmp2", [ED, D])
                with nc.semaphore("wepad") as s_p, nc.Block() as block:
                    @block.gpsimd
                    def _(pool):
                        nc.gpsimd.memset(wet[:, :], 0.0).then_inc(s_p, 1)
                        pool.wait_ge(s_p, 1)
                load(nc, "ld2e", [(wet[0:ED, 0:C], we), (wet[ED:ED + 1, 0:C], spread(be, 1)), (we3t[:, :], we3),
                                  (atte[:, :], spread(flat(att_edge), ED))])
                fold_attention(nc, "fold2", tmp[:, :], [(we3t[:, :], atte[:, :], wet[0:ED, C:EW], H)])
                layer2_scores(nc, k, t_k, k.acc, wet[:, :], edge_attr)
                store(nc, "st_ae", k.ae_dram.ap(), k.ae[:, :])
            segment_softmax(nc, "p10", k)
            aggregate(nc, "p11", k, t_v, True)
        with ExitStack() as s:
            sb = lambda name, shape, dt=F32: s.enter_context(nc.sbuf_tensor(name, shape, dt))
            recycle(nc)
            y = sb("y2", [P, NT * D])
            wot, bot = sb("wot", [P, KT, D]), sb("bot", [P, D])
            wf1t, bf1t = sb("wf1t", [P, KT, FF]), sb("bf1t", [P, FT])
            wf2t, bf2t = sb("wf2t", [P, FT, D]), sb("bf2t", [P, D])
            gain, shift = sb("gain2", [P, KT]), sb("shift2", [P, KT])
            al_, be_ = sb("alpha_", [P, 1]), sb("beta_", [P, 1])
            rd = sb("rd2", [P, NT * H])
            load(nc, "ld3", [(wot[:, :, :], rows_of(wo)), (bot[:, :], spread(bo)), (wf1t[:, :, :], rows_of(wf1)),
                             (bf1t[:, :], column(bf1)), (wf2t[:, :, :], rows_of(wf2, FT)), (bf2t[:, :], spread(bf2)),
                             (gain[:, :], column(ln2_g)), (shift[:, :], column(ln2_b)), (al_[:, :], spread(alpha)),
                             (be_[:, :], spread(beta))])
            fold_gain(nc, k, "fgf", wf1t, FF, gain, shift, bf1t[:, :], True)
            denominators(nc, "p12", k, rd[:, :])
            normalized(nc, "p14", k, xrv, y[:, :], ACT.Relu, k.rs_x, k.nb_x, False)
            attention_output(nc, k, y[:, :], wot, bot[:, :], al_[:, 0:1], rd[:, :])
            row_stats(nc, "p15", k, None)
            feed_forward(nc, k, y[:, :], xrv, wf1t, bf1t, wf2t, bf2t[:, :], be_[:, 0:1])

        recycle(nc)
        t_xp = table("t_xp", AW)
        with ExitStack() as s:
            sb = lambda name, shape, dt=F32: s.enter_context(nc.sbuf_tensor(name, shape, dt))
            a_parts = sb("a_parts", [P, 3 * NT * H], BF16)
            with ExitStack() as s2:
                sb2 = lambda name, shape, dt=F32: s2.enter_context(nc.sbuf_tensor(name, shape, dt))
                a_dst = sb2("a_dst", [P, NT * H])
                w3t, w3d = sb2("w3t", [P, KT, AW]), sb2("w3d", [P, KT, H])
                att, tmp = sb2("att3", [P, 2, D]), sb2("tmp3", [P, D])
                w3p = sb2("w3p", [P, KT, D])
                load(nc, "ld4", [(w3p[:, :, :], rows_of(w3)), (att[:, 0, :], spread(flat(att_src))),
                                 (att[:, 1, :], spread(flat(att_dst)))])
                fold_attention(nc, "fold3", tmp[:, :],
                               [(w3p[:, kt, :], att[:, n, :], to, H) for kt in range(KT)
                                for n, to in enumerate((by_head(w3t[:, kt, :])[:, :, C], w3d[:, kt, :]))])
                with nc.semaphore("w3heads") as s_w, nc.Block() as block:
                    @block.vector
                    def _(dve):
                        for kt in range(KT):
                            nc.vector.tensor_copy(by_head(w3t[:, kt, :])[:, :, 0:C], by_head(w3p[:, kt, :])
                                                  ).then_inc(s_w, 1)
                        dve.wait_ge(s_w, KT)
                row_stats(nc, "p16", k, None)
                project(nc, "p17", k, xrv, ACT.Relu, [(w3t, None, AW, None, [(0, AW, t_xp)], None),
                                               (w3d, None, H, None, [], a_dst[:, :])])
                split3(nc, a_dst[:, :], a_parts[:, :], NT * H)
            layer3_edges(nc, k, t_xp, a_parts)
        with ExitStack() as s:
            sb = lambda name, shape, dt=F32: s.enter_context(nc.sbuf_tensor(name, shape, dt))
            y = sb("y3", [P, NT * D])
            b3, g3, be3 = sb("bias3t", [P, D]), sb("gamma3t", [P, D]), sb("beta3t", [P, D])
            rd = sb("rd3", [P, NT * H])
            load(nc, "ld5", [(b3[:, :], spread(bias3)), (g3[:, :], spread(gamma3)), (be3[:, :], spread(beta3))])
            denominators(nc, "p20", k, rd[:, :])
            layer3_rows(nc, k, xrv, y[:, :], rd[:, :], b3[:, :])
            row_stats(nc, "p23", k, None)
            final_output(nc, k, xrv, y[:, :], g3[:, :], be3[:, :], out)


_INS = ['x', 'src', 'dst', 'edge_attr_64', 'edge_weight', 'L0_gnn_weight', 'L0_gnn_attn_l', 'L0_gnn_attn_r',
        'L1_gnn_W', 'L2_gnn_Wq', 'L2_gnn_bq', 'L2_gnn_Wk', 'L2_gnn_bk', 'L2_gnn_Wv', 'L2_gnn_bv', 'L2_gnn_We',
        'L2_gnn_be', 'L2_gnn_Wo', 'L2_gnn_bo', 'L2_gnn_ln1_g', 'L2_gnn_ln1_b', 'L2_gnn_ln2_g', 'L2_gnn_ln2_b',
        'L2_gnn_W1', 'L2_gnn_b1', 'L2_gnn_W2', 'L2_gnn_b2', 'L2_gnn_alpha', 'L2_gnn_beta', 'L3_gnn_W', 'L3_gnn_W_e',
        'L3_gnn_att_src', 'L3_gnn_att_dst', 'L3_gnn_att_edge', 'L3_gnn_bias', 'L3_gnn_gamma', 'L3_gnn_beta']


def kernel(**inputs):
    import numpy as _np
    import concourse.bacc as _bacc
    from concourse import mybir as _mybir
    from concourse.bass_utils import run_bass_kernel_spmd as _run

    nc = _bacc.Bacc("TRN2", target_bir_lowering=False, num_devices=1)
    arrays, args = {}, []
    for name in _INS:
        a = _np.ascontiguousarray(inputs[name])
        arrays[f"in_{name}_dram"] = a
        args.append(nc.dram_tensor(f"in_{name}_dram", a.shape, _mybir.dt.from_np(a.dtype), kind="ExternalInput").ap())
    args.append(nc.dram_tensor("out_dram", (N, D), F32, kind="ExternalOutput").ap())
    gnn_kernel(nc, *args)
    r = _run(nc, [arrays], core_ids=[0])
    return r.results[0]["out_dram"]
```
